# Optimizing a Trainium2 kernel written in Bass

```python
import numpy as np
import jax
import jax.numpy as jnp

def _softmax(x, axis=-1):
    return jax.nn.softmax(x, axis=axis)

def _gelu(x):
    return jax.nn.gelu(x, approximate=True)

def _silu(x):
    return jax.nn.silu(x)

def _sigmoid(x):
    return jax.nn.sigmoid(x)

def _layernorm(x, axis=-1, eps=1e-05):
    m = jnp.mean(x, axis=axis, keepdims=True)
    v = jnp.var(x, axis=axis, keepdims=True)
    return (x - m) / jnp.sqrt(v + eps)

def _scatter_add(tgt, idx, src, axis=0):
    return tgt.at[idx].add(src)

def _segment_sum(src, seg, n):
    return jax.ops.segment_sum(src, seg, n)
kernel_name = 'mk_perceiver_d1_seqx_r2_0ea943'

def setup_inputs(seed: int=0):
    np.random.seed(seed)
    _w = jnp.asarray

    def _rec_inputs():
        import jax
        import jax.numpy as jnp
        _rk = jax.random.key(seed)
        x = -0.0003929 + 0.9999 * jax.random.normal(jax.random.fold_in(_rk, 1), (2, 512, 512), jnp.float32)
        _lenS = 512 - jax.random.randint(jax.random.fold_in(_rk, 7), (2,), 0, max(1, 512 // 4) + 1, jnp.int32)
        _lenS2 = 8192 - jax.random.randint(jax.random.fold_in(_rk, 8), (2,), 0, max(1, 8192 // 4) + 1, jnp.int32)
        _ctx_2048P = jax.random.normal(jax.random.fold_in(_rk, 11), (2, 16, 1024), jnp.float32)
        _ctx_2048c = jax.random.dirichlet(jax.random.fold_in(_rk, 511), 0.3 * jnp.ones((16,), jnp.float32), (2, 8192))
        _ctx_2048t = jnp.einsum('bsk,bkd->bsd', _ctx_2048c, _ctx_2048P)
        _ctx_2048t = _ctx_2048t * jax.lax.rsqrt(jnp.mean(jnp.square(_ctx_2048t)) + 1e-12) * 0.953939
        ctx_2048 = 4.13588e-05 + 0.999923 * (_ctx_2048t + 0.3 * jax.random.normal(jax.random.fold_in(_rk, 611), (2, 8192, 1024), jnp.float32))
        _validS = jnp.arange(512)[None, :] < _lenS[:, None]
        _validS2 = jnp.arange(8192)[None, :] < _lenS2[:, None]
        _causal = jnp.tril(jnp.ones((512, 512), dtype=bool))
        mask_BxS2_if0 = jnp.where(jnp.ones((2, 8192), dtype=bool), 4, 0).astype(jnp.int32)
        return (x, ctx_2048, mask_BxS2_if0)
    x, ctx_2048, mask_BxS2_if0 = _rec_inputs()

    def _L0_xattn_setup():
        import jax, jax.numpy as jnp
        import numpy as np
        B, L, P = (4, 2048, 512)
        D_MODEL = 512
        D_GLOBAL = 1024
        HEADDIM = 32
        EPSILON = 0.001
        RMS_EPS = 1e-05

        def rmsnorm(x, g, eps=RMS_EPS):
            var = jnp.mean(jnp.square(x), axis=-1, keepdims=True)
            return x * jax.lax.rsqrt(var + eps) * g

        def _hnet_depool(h, h_patch_full, patch_lens):
            h_patch = h_patch_full[..., :D_MODEL]
            bsz, plen = (h_patch.shape[0], h_patch.shape[1])
            seqlen = h.shape[1]
            logp = jnp.full((bsz, plen), -EPSILON, dtype=jnp.float32)
            bidx = jnp.cumsum(patch_lens, axis=1) - 1
            boundary_mask = jnp.zeros((bsz, seqlen), dtype=jnp.int32)
            boundary_mask = boundary_mask.at[jnp.arange(bsz)[:, None], bidx].set(1)
            dt = (-jnp.log(-jnp.expm1(logp))).astype(h_patch.dtype)
            x = h_patch / dt[..., None]
            n_heads = D_MODEL // HEADDIM
            A = -jnp.ones((n_heads,), dtype=jnp.float32)
            bcoef = jnp.exp(logp).astype(h_patch.dtype)
            x4 = x.reshape(bsz, plen, n_heads, HEADDIM)
            a = jnp.exp(dt[:, :, None] * A[None, None, :])
            u = (dt * bcoef)[:, :, None, None] * x4
            a_b = jnp.broadcast_to(a[..., None], u.shape)

            def comb(lft, rgt):
                aL, uL = lft
                aR, uR = rgt
                return (aL * aR, uL * aR + uR)
            _, s = jax.lax.associative_scan(comb, (a_b, u), axis=1)
            depool = s.reshape(bsz, plen, D_MODEL)
            plug = jnp.clip(jnp.cumsum(boundary_mask, axis=1) - 1, 0, plen - 1)
            depool_out = depool[jnp.arange(bsz)[:, None], plug]
            return depool_out + h
        key = jax.random.key(seed)
        k1, k2, k3, k4 = jax.random.split(key, 4)
        embeds = jax.random.normal(k1, (B, L, D_MODEL), dtype=jnp.float32)
        patch_embeds = jax.random.normal(k2, (B, P, D_GLOBAL), dtype=jnp.float32)
        patch_lens = jnp.full((B, P), L // P, dtype=jnp.int64)
        W_in = jax.random.normal(k3, (D_MODEL, D_MODEL), dtype=jnp.float32) * 0.02
        b_in = jnp.zeros((D_MODEL,), dtype=jnp.float32)
        g_res = jnp.ones((D_MODEL,), dtype=jnp.float32)
        g_init = jnp.ones((D_GLOBAL,), dtype=jnp.float32)
        return {'embeds': embeds, 'patch_embeds': patch_embeds, 'patch_lens': patch_lens, 'W_in': W_in, 'b_in': b_in, 'g_res': g_res, 'g_init': g_init}
    _L0_xattn_all = _L0_xattn_setup()
    _L0_xattn_in = {k: v for k, v in _L0_xattn_all.items() if k in ('W_in', 'b_in', 'g_res', 'g_init')}
    del _L0_xattn_all

    def _L0_attn_setup():
        import jax, jax.numpy as jnp
        import numpy as np
        B, L, C, H, W = (4, 2048, 512, 16, 256)
        D = C // H
        STRIDE = W // 2

        def _local_attention(x, w_qkv, b_qkv, w_out, b_out):
            b, l, c = x.shape
            pad = -l % W
            x = jnp.pad(x, ((0, 0), (0, pad), (0, 0)))
            lp = l + pad
            qkv = (x @ w_qkv + b_qkv).reshape(b, lp, 3, H, D).transpose(2, 0, 3, 1, 4)
            q, k, v = (qkv[0], qkv[1], qkv[2])
            nw = (lp - W) // STRIDE + 1
            idx = jnp.arange(nw)[:, None] * STRIDE + jnp.arange(W)[None, :]
            qw = q[:, :, idx, :]
            kw = k[:, :, idx, :]
            vw = v[:, :, idx, :]
            scores = jnp.einsum('bhnqd,bhnkd->bhnqk', qw, kw) / jnp.sqrt(jnp.float32(D))
            probs = jax.nn.softmax(scores, axis=-1)
            ow = jnp.einsum('bhnqk,bhnkd->bhnqd', probs, vw)
            o = ow.transpose(0, 2, 3, 1, 4).reshape(b, nw * W, c)
            o = o @ w_out + b_out
            return o[:, :l, :]
        key = jax.random.key(seed)
        k0, k1, k2 = jax.random.split(key, 3)
        s = 0.02
        return {'x': jax.random.normal(k0, (B, L, C), jnp.float32), 'w_qkv': jax.random.normal(k1, (C, 3 * C), jnp.float32) * s, 'b_qkv': jnp.zeros((3 * C,), jnp.float32), 'w_out': jax.random.normal(k2, (C, C), jnp.float32) * s, 'b_out': jnp.zeros((C,), jnp.float32)}
    _L0_attn_all = _L0_attn_setup()
    _L0_attn_in = {k: v for k, v in _L0_attn_all.items() if k in ('w_qkv', 'b_qkv', 'w_out', 'b_out')}
    del _L0_attn_all

    def _L0_ffn_setup():
        import jax, jax.numpy as jnp
        import numpy as np
        E = 8
        D = 512
        H = 1024
        TOP_K = 2
        key = jax.random.key(seed)
        k_x, k_g, k_w1, k_w2 = jax.random.split(key, 4)
        B, S = (4, 1024)
        inp = {'input': jax.random.normal(k_x, (B, S, D), dtype=jnp.float32), 'Wg': jax.random.normal(k_g, (D, E), dtype=jnp.float32) * 0.02, 'W1': jax.random.normal(k_w1, (E, D, H), dtype=jnp.float32) * 0.02, 'b1': jnp.zeros((E, H), dtype=jnp.float32), 'W2': jax.random.normal(k_w2, (E, H, D), dtype=jnp.float32) * 0.02, 'b2': jnp.zeros((E, D), dtype=jnp.float32)}
        return inp
    _L0_ffn_all = _L0_ffn_setup()
    _L0_ffn_in = {k: v for k, v in _L0_ffn_all.items() if k in ('Wg', 'W1', 'b1', 'W2', 'b2')}
    del _L0_ffn_all
    return {'x': x, 'ctx_2048': ctx_2048, 'mask_BxS2_if0': mask_BxS2_if0, 'L0_xattn_W_in': _L0_xattn_in['W_in'], 'L0_xattn_b_in': _L0_xattn_in['b_in'], 'L0_xattn_g_res': _L0_xattn_in['g_res'], 'L0_xattn_g_init': _L0_xattn_in['g_init'], 'L0_attn_w_qkv': _L0_attn_in['w_qkv'], 'L0_attn_b_qkv': _L0_attn_in['b_qkv'], 'L0_attn_w_out': _L0_attn_in['w_out'], 'L0_attn_b_out': _L0_attn_in['b_out'], 'L0_ffn_Wg': _L0_ffn_in['Wg'], 'L0_ffn_W1': _L0_ffn_in['W1'], 'L0_ffn_b1': _L0_ffn_in['b1'], 'L0_ffn_W2': _L0_ffn_in['W2'], 'L0_ffn_b2': _L0_ffn_in['b2']}

def reference(x, ctx_2048, mask_BxS2_if0, L0_xattn_W_in, L0_xattn_b_in, L0_xattn_g_res, L0_xattn_g_init, L0_attn_w_qkv, L0_attn_b_qkv, L0_attn_w_out, L0_attn_b_out, L0_ffn_Wg, L0_ffn_W1, L0_ffn_b1, L0_ffn_W2, L0_ffn_b2):
    import jax
    import jax.numpy as jnp

    def _L0_xattn_ref(embeds, patch_embeds, patch_lens, W_in, b_in, g_res, g_init):
        import jax, jax.numpy as jnp
        import numpy as np
        B, L, P = (4, 2048, 512)
        D_MODEL = 512
        D_GLOBAL = 1024
        HEADDIM = 32
        EPSILON = 0.001
        RMS_EPS = 1e-05

        def rmsnorm(x, g, eps=RMS_EPS):
            var = jnp.mean(jnp.square(x), axis=-1, keepdims=True)
            return x * jax.lax.rsqrt(var + eps) * g

        def _hnet_depool(h, h_patch_full, patch_lens):
            h_patch = h_patch_full[..., :D_MODEL]
            bsz, plen = (h_patch.shape[0], h_patch.shape[1])
            seqlen = h.shape[1]
            logp = jnp.full((bsz, plen), -EPSILON, dtype=jnp.float32)
            bidx = jnp.cumsum(patch_lens, axis=1) - 1
            boundary_mask = jnp.zeros((bsz, seqlen), dtype=jnp.int32)
            boundary_mask = boundary_mask.at[jnp.arange(bsz)[:, None], bidx].set(1)
            dt = (-jnp.log(-jnp.expm1(logp))).astype(h_patch.dtype)
            x = h_patch / dt[..., None]
            n_heads = D_MODEL // HEADDIM
            A = -jnp.ones((n_heads,), dtype=jnp.float32)
            bcoef = jnp.exp(logp).astype(h_patch.dtype)
            x4 = x.reshape(bsz, plen, n_heads, HEADDIM)
            a = jnp.exp(dt[:, :, None] * A[None, None, :])
            u = (dt * bcoef)[:, :, None, None] * x4
            a_b = jnp.broadcast_to(a[..., None], u.shape)

            def comb(lft, rgt):
                aL, uL = lft
                aR, uR = rgt
                return (aL * aR, uL * aR + uR)
            _, s = jax.lax.associative_scan(comb, (a_b, u), axis=1)
            depool = s.reshape(bsz, plen, D_MODEL)
            plug = jnp.clip(jnp.cumsum(boundary_mask, axis=1) - 1, 0, plen - 1)
            depool_out = depool[jnp.arange(bsz)[:, None], plug]
            return depool_out + h
        h = rmsnorm(embeds, g_res)
        h = jnp.einsum('bld,ed->ble', h, W_in) + b_in
        h_patch = rmsnorm(patch_embeds, g_init)
        return _hnet_depool(h, h_patch, patch_lens)

    def _L0_attn_ref(x, w_qkv, b_qkv, w_out, b_out):
        import jax, jax.numpy as jnp
        import numpy as np
        B, L, C, H, W = (4, 2048, 512, 16, 256)
        D = C // H
        STRIDE = W // 2

        def _local_attention(x, w_qkv, b_qkv, w_out, b_out):
            b, l, c = x.shape
            pad = -l % W
            x = jnp.pad(x, ((0, 0), (0, pad), (0, 0)))
            lp = l + pad
            qkv = (x @ w_qkv + b_qkv).reshape(b, lp, 3, H, D).transpose(2, 0, 3, 1, 4)
            q, k, v = (qkv[0], qkv[1], qkv[2])
            nw = (lp - W) // STRIDE + 1
            idx = jnp.arange(nw)[:, None] * STRIDE + jnp.arange(W)[None, :]
            qw = q[:, :, idx, :]
            kw = k[:, :, idx, :]
            vw = v[:, :, idx, :]
            scores = jnp.einsum('bhnqd,bhnkd->bhnqk', qw, kw) / jnp.sqrt(jnp.float32(D))
            probs = jax.nn.softmax(scores, axis=-1)
            ow = jnp.einsum('bhnqk,bhnkd->bhnqd', probs, vw)
            o = ow.transpose(0, 2, 3, 1, 4).reshape(b, nw * W, c)
            o = o @ w_out + b_out
            return o[:, :l, :]
        return _local_attention(x, w_qkv, b_qkv, w_out, b_out)

    def _L0_ffn_ref(input, Wg, W1, b1, W2, b2):
        import jax, jax.numpy as jnp
        import numpy as np
        E = 8
        D = 512
        H = 1024
        TOP_K = 2
        logits = jnp.einsum('bsd,de->bse', input, Wg)
        probs = jax.nn.softmax(logits, axis=-1)
        top_vals, top_idx = jax.lax.top_k(probs, TOP_K)
        top_vals = top_vals / jnp.sum(top_vals, axis=-1, keepdims=True)
        onehot = jax.nn.one_hot(top_idx, E, dtype=input.dtype)
        mask = jnp.sum(onehot, axis=2)
        scores = jnp.sum(onehot * top_vals[..., None], axis=2)
        xm = input[None] * jnp.moveaxis(mask, -1, 0)[..., None]
        h = jnp.einsum('ebsd,edh->ebsh', xm, W1) + b1[:, None, None, :]
        h = jax.nn.relu(h)
        y = jnp.einsum('ebsh,ehd->ebsd', h, W2) + b2[:, None, None, :]
        out = jnp.sum(y * jnp.moveaxis(scores, -1, 0)[..., None], axis=0)
        return out
    x = x + _L0_xattn_ref(_layernorm(x, axis=-1), ctx_2048, mask_BxS2_if0, L0_xattn_W_in, L0_xattn_b_in, L0_xattn_g_res, L0_xattn_g_init)
    x = x + _L0_attn_ref(_layernorm(x, axis=-1), L0_attn_w_qkv, L0_attn_b_qkv, L0_attn_w_out, L0_attn_b_out)
    x = x + _L0_ffn_ref(_layernorm(x, axis=-1), L0_ffn_Wg, L0_ffn_W1, L0_ffn_b1, L0_ffn_W2, L0_ffn_b2)
    return x

_drawn_inputs = setup_inputs


def setup_inputs(seed=0):
    import zlib

    import numpy as np

    out = dict(_drawn_inputs(seed))
    spreads = {'L0_xattn_b_in': (0.0, 0.1),
     'L0_xattn_g_res': (1.0, 0.2),
     'L0_xattn_g_init': (1.0, 0.2),
     'L0_attn_b_qkv': (0.0, 0.1),
     'L0_attn_b_out': (0.0, 0.1),
     'L0_ffn_b1': (0.0, 0.385),
     'L0_ffn_b2': (0.0, 0.1)}
    factors = {}
    for name, (base, spread) in spreads.items():
        noise = np.random.default_rng([zlib.crc32(name.encode()), seed]).standard_normal(out[name].shape)
        drawn = base * np.exp(spread * noise) if base else spread * noise
        out[name] = jnp.asarray(drawn.astype(out[name].dtype))
    for name, factor in factors.items():
        out[name] = (out[name] * factor).astype(out[name].dtype)
    return out
```

```python
import math
from contextlib import ExitStack

import concourse.bass as bass
from concourse import mybir

F32 = mybir.dt.float32
F32R = mybir.dt.float32r
BF16 = mybir.dt.bfloat16
I32 = mybir.dt.int32
U32 = mybir.dt.uint32
ALU = mybir.AluOpType
ACT = mybir.ActivationFunctionType
AX = mybir.AxisListType

P = 128
B, L, D = 2, 512, 512
T = B * L
NT = T // P
LT = L // P
DC = D // P
DG = 1024
NLEN = 8192
NJ = NLEN // P
HEADS, HD = 16, 32
WIN, STRIDE = 256, 128
NWIN = 2
AROWS = STRIDE * (NWIN - 1) + WIN
AT = AROWS // P
E, H = 8, 1024
HC = H // P
LN_EPS = 1e-5
RMS_EPS = 1e-5
LOGP = -0.001
DT = -math.log(-math.expm1(LOGP))
SLOT_TILES = 2 * T // P + E - 1
TC = SLOT_TILES + 1
WQ = 4
WCOLS = DC * H + HC * D
QCOLS = WCOLS // WQ


def perceiver_layer(nc, x_in, ctx_in, lens_in, w_in, b_in, g_res, g_init, w_qkv, b_qkv, w_out, b_out,
                    w_gate, w1, b1, w2, b2, out):
    x_rows = x_in.rearrange("b (i p) d -> p (b i) d", p=P)
    out_rows = out.rearrange("b (i p) d -> p (b i) d", p=P)

    with ExitStack() as ctx:
        def sem(name):
            return ctx.enter_context(nc.semaphore(name))

        banks = [ctx.enter_context(nc.psum_tensor(f"bank{i}", [P, 512], F32)) for i in range(8)]

        BASE = 16512
        K = 1024

        def place(name, shape, dtype, at):
            return nc.alloc_sbuf_tensor_at(name, shape, dtype, offset=BASE + at)

        x_res = place("x_res", [P, NT, D], F32, 0)
        SMALL, RAW, MID, BIG = 16 * K, 27 * K, 43 * K, 79 * K
        small_at = [SMALL]

        def small(name, shape, dtype):
            words = 1
            for n in shape[1:]:
                words *= n
            size = words * (2 if dtype == BF16 else 4)
            t = place(name, shape, dtype, small_at[0])
            small_at[0] += -(-size // 32) * 32
            assert small_at[0] <= RAW
            return t

        ident = small("ident", [P, P], F32)
        before = small("before", [P, P], F32)
        ones_bf = small("ones_bf", [P, P], BF16)
        s_col = small("s_col", [P, LT], F32)
        lnb = small("lnb", [P, 1], F32)
        iota16 = small("iota16", [P, 16], F32)
        iota32 = small("iota32", [P, 32], F32)
        diag16 = small("diag16", [16, 16], F32)
        g_res_col = small("g_res_col", [P, DC], F32)
        bn = small("bn", [P, NT, 6], F32)
        mv = small("mv", [P, NT, 2], F32)
        var_eps = small("var_eps", [P, NT], F32)
        sd = small("sd", [P, NT], F32)
        rstd = small("rstd", [P, NT], F32)
        row_scale = small("row_scale", [P, NT], F32)
        row_shift = small("row_shift", [P, NT], F32)
        tmp8 = small("tmp8", [P, NT], F32)
        ctx_ss = small("ctx_ss", [P, NT], F32)
        ctx_rs = small("ctx_rs", [P, NT], F32)
        ctx_sd = small("ctx_sd", [P, NT], F32)
        prefix = small("prefix", [P, B], F32)

        ctx_sb = place("ctx_sb", [P, B * LT, DG], F32, BIG)
        patches = place("patches", [P, B * LT, D], F32, BIG + 32 * K)
        decay = place("decay", [P, B * LT, L], F32, BIG + 48 * K)
        w_in_sb = place("w_in_sb", [P, DC, D], F32, BIG + 64 * K)
        w_inT = place("w_inT", [P, DC, D], F32, BIG + 72 * K)
        hT = place("hT", [P, 2, DC, P], F32, BIG + 80 * K)
        hn = place("hn", [P, 2, D], F32, BIG + 84 * K)
        oh_hi = place("oh_hi", [P, B * NJ, 16], BF16, BIG + 88 * K)
        oh_lo = place("oh_lo", [P, B * NJ, 32], BF16, BIG + 92 * K)
        lens_f = place("lens_f", [P, B * NJ], F32, BIG + 100 * K)
        within = place("within", [P, B, NJ], F32, BIG + 100 * K + 512)
        bidx = place("bidx", [P, B * NJ], F32, BIG + 101 * K)
        wrap = place("wrap", [P, B * NJ], F32, BIG + 101 * K + 512)
        cell = place("cell", [P, B * NJ], I32, BIG + 102 * K)
        cell_hi = place("cell_hi", [P, B * NJ], I32, BIG + 102 * K + 512)
        cell_lo = place("cell_lo", [P, B * NJ], I32, BIG + 123 * K)
        plug = place("plug", [P, B, L], F32, BIG + 103 * K)
        ones_f = place("ones_f", [P, L], F32, BIG + 107 * K)
        gap = place("gap", [P, 2, L], F32, BIG + 109 * K)
        blocks = place("blocks", [16, B, 16, 32], BF16, BIG + 113 * K)
        b_in_row = place("b_in_row", [P, D], F32, BIG + 115 * K)
        g_init_row = place("g_init_row", [P, D], F32, BIG + 117 * K)
        squares = place("squares", [P, DG], F32, BIG + 119 * K)
        lens_i = place("lens_i", [P, B, NJ], I32, BIG + 123 * K + 512)
        hits = place("hits", [16, B, 32], F32, BIG + 124 * K)

        b_v_row = small("b_v_row", [P, D], F32)
        b_out_row = small("b_out_row", [P, D], F32)
        b_qk_col = small("b_qk_col", [P, 2 * DC], F32)
        neg_max = small("neg_max", [P, 4, 2], F32)
        max_bias = small("max_bias", [P, 4, 2], F32)
        prob_sum = small("prob_sum", [P, 4, 2], F32)
        prob_inv = small("prob_inv", [P, 4, 2], F32)
        w_qkv_sb = place("w_qkv_sb", [P, DC, 3 * D], F32, BIG)
        xn = place("xn", [P, 2, D], F32, BIG + 24 * K)
        xnT = place("xnT", [P, DC, B * AROWS], F32, BIG + 88 * K)
        qk_hi = place("qk_hi", [P, 2, AROWS], F32, BIG + 100 * K)
        qk_lo = place("qk_lo", [P, 2, AROWS], F32, BIG + 103 * K)
        q_parts = [place(f"q_parts{i}", [96, 4, WIN], F32R, BIG + (32 + 4 * i) * K) for i in range(2)]
        k_parts = [place(f"k_parts{i}", [96, 4, WIN], F32R, BIG + (40 + 4 * i) * K) for i in range(2)]
        v_heads = place("v_heads", [P, 2, 2, P], F32, BIG + 48 * K)
        probs = place("probs", [P, 4, 2, WIN], F32, BIG + 50 * K)
        probs_n = place("probs_n", [P, 2, 2, WIN], F32, BIG + 58 * K)
        probsT = place("probsT", [P, 2, 2, WIN], F32, BIG + 62 * K)
        oT = place("oT", [P, B * NWIN * 4, WIN], F32, MID)
        w_out_sb = place("w_out_sb", [P, DC, D], F32, MID + 16 * K)
        v_sb = place("v_sb", [P, B * AT, D], F32, MID + 24 * K)
        qk_dram = nc.dram_tensor("qk_parts", (2, 2 * DC, P, B * AROWS), F32, kind="Internal").ap()

        w_gate_sb = small("w_gate_sb", [P, DC, E], F32)
        x3 = place("x3", [P, 2, D], F32, MID + 24 * K)
        x3T = place("x3T", [P, 2, DC, P], F32, MID + 28 * K)
        ROUTE = BIG + 110 * K
        route_at = [ROUTE]

        def route(name, shape, dtype=F32):
            words = 1
            for n in shape[1:]:
                words *= n
            t = place(name, shape, dtype, route_at[0])
            route_at[0] += -(-words * (2 if dtype == BF16 else 4) // 32) * 32
            assert route_at[0] <= BIG + 128 * K
            return t

        logit = route("logit", [P, NT, E])
        top = [route(f"top{c}", [P, NT]) for c in range(2)]
        eq = route("eq", [P, NT, E])
        rank_key = route("rank_key", [P, NT])
        pick = route("pick", [P, 2, NT, E])
        score = route("score", [P, 2, NT])
        exp_gap = route("exp_gap", [P, NT])
        denom = route("denom", [P, NT])
        chosen = route("chosen", [P, NT, E], BF16)
        earlier = route("earlier", [P, NT + 1, E], BF16)
        before_bf = route("before_bf", [P, P], BF16)
        rank_sb = route("rank_sb", [P, NT + 1, E])
        count_i = route("count_i", [P, E], I32)
        tiles_of = route("tiles_of", [P, E])
        tiles_end = route("tiles_end", [P, E])
        slot_base = route("slot_base", [P, E])
        slot_all = route("slot_all", [P, NT, E])
        slot_pick = route("slot_pick", [P, 2, NT, E])
        slot_f = route("slot_f", [P, 2, NT])
        slot_hi = route("slot_hi", [P, 2 * NT], I32)
        slot_lo = route("slot_lo", [P, 2 * NT], I32)
        lo_hot = route("lo_hot", [P, 2 * NT, P])
        hi_hot = route("hi_hot", [P, 2 * NT, TC])
        cast = route("cast", [P, 2 * NT, 2, TC])
        token_no = route("token_no", [P, NT])
        iota128 = route("iota128", [P, P])
        iota_tc = route("iota_tc", [P, TC])
        down8 = route("down8", [P, E])
        tile_cmp = route("tile_cmp", [P, TC, E])
        tile_e = route("tile_e", [P, TC])
        tile_new = route("tile_new", [P, TC])
        slot_u = small("slot_u", [P, 2 * NT], I32)
        tile_expert = small("tile_expert", [1, TC], I32)
        tile_loads = small("tile_loads", [1, TC], I32)
        tile_next = small("tile_next", [1, TC], I32)
        slot_token = small("slot_token", [P, TC], I32)
        slot_score = small("slot_score", [P, TC], F32)
        gather_at = [small(f"gather_at{i}", [P, 1], I32) for i in range(2)]
        score_col = small("score_col", [P, 2], F32)
        ones8 = small("ones8", [P, E], F32)

        x_gath = place("x_gath", [P, 2, D], F32, MID + 32 * K)
        xT_hi = place("xT_hi", [P, DC, P], F32R, MID)
        xT_lo = place("xT_lo", [P, DC, P], F32R, MID + 2 * K)
        h_sb = place("h_sb", [P, H], F32, MID + 4 * K)
        hT_hi = place("hT_hi", [P, HC, P], F32R, MID + 8 * K)
        hT_lo = place("hT_lo", [P, HC, P], F32R, MID + 12 * K)
        b1_row = place("b1_row", [P, 2, H], F32, MID + 16 * K)
        b2_row = place("b2_row", [P, 2, D], F32, MID + 24 * K)
        y_sb = place("y_sb", [P, 2, D], F32, MID + 28 * K)
        w_raw = place("w_raw", [P, 2, QCOLS], F32, RAW)
        w_hi = place("w_hi", [P, 2 * WCOLS], F32R, BIG)
        w_lo = place("w_lo", [P, 2 * WCOLS], F32R, BIG + 64 * K)
        y_back = place("y_back", [P, 2 * NT, D], F32, BIG)
        x3_dram = nc.dram_tensor("x3_rows", (T, D), F32, kind="Internal").ap()
        y_dram = nc.dram_tensor("y_slots", (SLOT_TILES * P, D), F32, kind="Internal").ap()

        x_loaded, lens_loaded, ctx_loaded = sem("x_loaded"), sem("lens_loaded"), [sem("ctx_loaded0"), sem("ctx_loaded1")]
        w_in_loaded, rows_loaded = sem("w_in_loaded"), sem("rows_loaded")
        consts, consts2 = sem("consts"), sem("consts2")
        vector_step, scalar_step = sem("vector_step"), sem("scalar_step")
        lens_scanned, prefix_done, onehots, hits_done, blocks_ready, rows_counted = (
            sem(n) for n in ("lens_scanned", "prefix_done", "onehots", "hits_done", "blocks_ready", "rows_counted"))
        ctx_summed, ctx_eps, ctx_rooted, patches_ready = (
            sem(n) for n in ("ctx_summed", "ctx_eps", "ctx_rooted", "patches_ready"))
        var_ready, rooted, scales_ready, normed, xb_ready = (
            sem(n) for n in ("var_ready", "rooted", "scales_ready", "normed", "xb_ready"))
        gap_ready, decayed, decay_ready = sem("gap_ready"), sem("decayed"), sem("decay_ready")
        w_in_turned, w_in_ready = sem("w_in_turned"), sem("w_in_ready")
        h_turned, h_copied, embedded, x1_ready = (sem(n) for n in ("h_turned", "h_copied", "embedded", "x1_ready"))
        w_qkv_loaded, w_out_loaded, x2_ready = sem("w_qkv_loaded"), sem("w_out_loaded"), sem("x2_ready")
        att_var, att_root, att_scale, xn_ready, xn_turned, xnT_ready = (
            sem(n) for n in ("att_var", "att_root", "att_scale", "xn_ready", "xn_turned", "xnT_ready"))
        qk_summed, qk_hi_ready, qk_lo_ready, qk_stored, v_summed, v_ready, xo_ready = (
            sem(n) for n in ("qk_summed", "qk_hi_ready", "qk_lo_ready", "qk_stored", "v_summed", "v_ready", "xo_ready"))
        qk_stored = [qk_stored, sem("qk_stored1")]
        parts_loaded = [sem("parts_loaded0"), sem("parts_loaded1")]
        v_staged, scores_ready, max_ready, exp_done, inv_ready, normalised, turned, probsT_ready, pv_done, oT_ready = (
            sem(n) for n in ("v_staged", "scores_ready", "max_ready", "exp_done", "inv_ready", "normalised",
                             "turned", "probsT_ready", "pv_done", "oT_ready"))
        projected, cols_loaded = sem("projected"), sem("cols_loaded")
        max_taken = sem("max_taken")
        out_stored = [sem("out_stored0"), sem("out_stored1")]
        x3_var, x3_root, x3_scale, x3_ready, x3_turned, x3T_ready, gated = (
            sem(n) for n in ("x3_var", "x3_root", "x3_scale", "x3_ready", "x3_turned", "x3T_ready", "gated"))
        x3_stored = [sem("x3_stored0"), sem("x3_stored1")]
        route_consts, gap2_ready, gap2_exp, ranks_asked, ranked, casts_ready, cast_done, tables_ready, routed = (
            sem(n) for n in ("route_consts", "gap2_ready", "gap2_exp", "ranks_asked", "ranked", "casts_ready",
                             "cast_done", "tables_ready", "routed"))
        raw_loaded, hi_split, lo_split = sem("raw_loaded"), sem("hi_split"), sem("lo_split")
        raw_loaded = [raw_loaded, sem("raw_loaded1")]
        b1_loaded = [sem("b1_loaded0"), sem("b1_loaded1")]
        b2_loaded = [sem("b2_loaded0"), sem("b2_loaded1")]
        picked, gathered = sem("picked"), [sem("gathered0"), sem("gathered1")]
        xg_turned, xT_hi_ready, xT_lo_ready, up_done, h_ready, h_turned2, hT_hi_ready, hT_lo_ready, down_done = (
            sem(n) for n in ("xg_turned", "xT_hi_ready", "xT_lo_ready", "up_done", "h_ready", "h_turned2",
                             "hT_hi_ready", "hT_lo_ready", "down_done"))
        y_added, y_scaled = sem("y_added"), sem("y_scaled")
        y_stored = [sem("y_stored0"), sem("y_stored1")]
        y_fetched = [sem(f"y_fetched{i}") for i in range(NT)]
        gate_loaded, score_picked = sem("gate_loaded"), sem("score_picked")
        y_first, x_out = sem("y_first"), sem("x_out")

        block = ctx.enter_context(nc.Block())

        class Steps:

            def __init__(self, eng, done):
                self.eng, self.done, self.count = eng, done, 0

            def step(self, ins):
                ins.then_inc(self.done, 1)
                self.count += 1

            def join(self):
                self.eng.wait_ge(self.done, self.count)

            def then(self, ins):
                self.step(ins)
                self.join()

        @block.sync
        def _(sp):
            lens_v = lens_in.rearrange("b (p j) -> p b j", p=P)
            sp.dma_start(lens_i[:], lens_v).then_inc(lens_loaded, 16)
            sp.dma_start(x_res[:], x_rows).then_inc(x_loaded, 16)
            sp.dma_start(w_in_sb[:], w_in.rearrange("(j p) d -> p j d", p=P)).then_inc(w_in_loaded, 16)
            for b in range(B):
                sp.dma_start(ctx_sb[:, b * LT:(b + 1) * LT, :],
                             ctx_in[b, 0:L, :].rearrange("(k p) d -> p k d", p=P)).then_inc(ctx_loaded[b], 16)
            sp.dma_start(w_out_sb[:], w_out.rearrange("(k p) n -> p k n", p=P)).then_inc(w_out_loaded, 16)
            sp.wait_ge(patches_ready, B * LT)
            sp.dma_start(w_qkv_sb[:], w_qkv.rearrange("(k p) n -> p k n", p=P)).then_inc(w_qkv_loaded, 16)
            for u in range(B * 2 * DC):
                b, c = divmod(u, 2 * DC)
                cols = slice(b * AROWS, (b + 1) * AROWS)
                sp.wait_ge(qk_hi_ready, u + 1)
                sp.dma_start(qk_dram[0, c, :, cols], qk_hi[:, u % 2, :]).then_inc(qk_stored[u % 2], 16)
                sp.wait_ge(qk_lo_ready, u + 1)
                sp.dma_start(qk_dram[1, c, :, cols], qk_lo[:, u % 2, :]).then_inc(qk_stored[u % 2], 16)

            def load_parts(j, r, first):
                row0 = (j // 4) * AROWS + ((j // 2) % 2) * STRIDE
                g = 2 * (j % 2) + r
                if not first:
                    sp.wait_ge(scores_ready, 8 * j + 4 * r - 4)
                for tile, c, parts in ((q_parts[r], g, (0, 1, 0)), (k_parts[r], g + DC, (0, 0, 1))):
                    for n, part in enumerate(parts):
                        src = qk_dram[part, bass.ds(c, 1), :, bass.ds(row0, WIN)]
                        sp.dma_start(tile[n * HD:(n + 1) * HD].bitcast(F32),
                                     src.rearrange("a (h p) t -> p (a h) t", p=HD)).then_inc(parts_loaded[r], 16)

            for parity in range(2):
                sp.wait_ge(qk_stored[parity], 32 * B * DC)
            for r in range(2):
                load_parts(0, r, True)
            with sp.Fori(1, 8) as j:
                for r in range(2):
                    load_parts(j, r, False)
            for i in range(NT):
                sp.wait_ge(x3_ready, i + 1)
                sp.dma_start(x3_dram[i * P:(i + 1) * P, :], x3[:, i % 2, :]).then_inc(x3_stored[i % 2], 16)

            def w_quarter(e, q):
                if q < 2:
                    return w1[bass.ds(e, 1), q * 2 * P:(q + 1) * 2 * P, :].rearrange("a (k p) n -> p (a k) n", p=P)
                return w2[bass.ds(e, 1), (q - 2) * 4 * P:(q - 1) * 4 * P, :].rearrange("a (k p) n -> p (a k) n", p=P)

            def load_quarter(e, q):
                n = H if q < 2 else D
                sp.dma_start(w_raw[:, q % 2, :].rearrange("p (k n) -> p k n", n=n),
                             w_quarter(e, q)).then_inc(raw_loaded[q % 2], 16)

            for n in range(2 * WQ):
                if n >= 2:
                    sp.wait_ge(hi_split, n - 1)
                    sp.wait_ge(lo_split, n - 1)
                load_quarter(n // WQ, n % WQ)

            def load_biases(t, r, first=False):
                e = sp.value_load(tile_expert[0:1, bass.ds(t, 1)], min_val=0, max_val=E - 1)
                if not first:
                    sp.wait_ge(h_ready, t - 1)
                sp.dma_start(b1_row[:, r, :], b1[bass.ds(e, 1), :].rearrange("a n -> (a n)").partition_broadcast(P)
                             ).then_inc(b1_loaded[r], 16)
                if not first:
                    sp.wait_ge(y_added, t - 1)
                sp.dma_start(b2_row[:, r, :], b2[bass.ds(e, 1), :].rearrange("a n -> (a n)").partition_broadcast(P)
                             ).then_inc(b2_loaded[r], 16)

            def load_next_expert(t):
                load = sp.value_load(tile_loads[0:1, bass.ds(t, 1)], min_val=0, max_val=1)
                e = sp.value_load(tile_next[0:1, bass.ds(t, 1)], min_val=0, max_val=E - 1)
                sp.wait_ge(hi_split, WQ * t + WQ)
                sp.wait_ge(lo_split, WQ * t + WQ)
                sp.nop(nofuse=True)
                with sp.If(load == 1):
                    for q in range(WQ):
                        if q >= 2:
                            sp.wait_ge(hi_split, WQ * t + WQ + q - 1)
                            sp.wait_ge(lo_split, WQ * t + WQ + q - 1)
                        load_quarter(e, q)
                with sp.Else():
                    for q in range(2):
                        sp.sem_inc(raw_loaded[q], 32)
                sp.nop(nofuse=True)

            sp.wait_ge(tables_ready, 1)
            for r in range(2):
                sp.wait_ge(x3_stored[r], 16 * NT // 2)
            load_biases(0, 0, True)
            load_biases(1, 1, True)
            load_next_expert(1)
            with sp.Fori(1, (SLOT_TILES - 1) // 2) as j:
                for r in range(2):
                    load_biases(2 * j + r, r)
                    load_next_expert(2 * j + r)
            load_biases(SLOT_TILES - 1, 0)
            load_next_expert(SLOT_TILES - 1)
            for i in range(NT):
                sp.wait_ge(x_out, i + 1)
                sp.dma_start(out_rows[:, i, :], x_res[:, i, :]).then_inc(out_stored[i % 2], 16)
            for r in range(2):
                sp.wait_ge(out_stored[r], 16 * NT // 2)

        @block.gpsimd
        def _(pool):
            pool.memset(ident[:], 0.0).then_inc(consts, 1)
            pool.memset(before[:], 1.0).then_inc(consts, 1)
            pool.memset(ones_bf[:], 1.0).then_inc(consts, 1)
            pool.memset(lnb[:], LOGP).then_inc(consts, 1)
            pool.memset(ones_f[:], 1.0).then_inc(consts, 1)
            pool.memset(diag16[:], 0.0).then_inc(consts, 1)
            pool.wait_ge(consts, 6)
            pool.affine_select(out=ident[:], in_=ident[:], compare_op=ALU.not_equal, fill=1.0, base=0,
                               pattern=[[-1, P]], channel_multiplier=1).then_inc(consts2, 1)
            pool.affine_select(out=before[:], in_=before[:], compare_op=ALU.is_gt, fill=0.0, base=0,
                               pattern=[[1, P]], channel_multiplier=-1).then_inc(consts2, 1)
            pool.affine_select(out=diag16[:], in_=diag16[:], compare_op=ALU.not_equal, fill=1.0, base=0,
                               pattern=[[-1, 16]], channel_multiplier=1).then_inc(consts2, 1)
            exact = dict(allow_small_or_imprecise_dtypes=True)
            pool.iota(s_col[:], [[P, LT]], base=0, channel_multiplier=1, **exact).then_inc(consts2, 1)
            pool.iota(iota16[:], [[1, 16]], base=0, channel_multiplier=0, **exact).then_inc(consts2, 1)
            pool.iota(iota32[:], [[1, 32]], base=0, channel_multiplier=0, **exact).then_inc(consts2, 1)
            pool.wait_ge(rows_loaded, 48)
            for i in range(NT):
                pool.wait_ge(normed, i + 1)
                pool.tensor_tensor(out=x_res[:, i, :], in0=x_res[:, i, :], in1=b_in_row[:], op=ALU.add).then_inc(xb_ready, 1)
            pool.wait_ge(cols_loaded, 48)
            for i in range(NT):
                pool.wait_ge(x1_ready, i + 1)
                if i % LT < AT:
                    pool.wait_ge(xn_ready, (i // LT) * AT + i % LT + 1)
                pool.tensor_tensor(out=x_res[:, i, :], in0=x_res[:, i, :], in1=b_out_row[:],
                                   op=ALU.add).then_inc(xo_ready, 1)

            def stage_v(j, r, first):
                if not first:
                    pool.wait_ge(pv_done, 8 * j + 4 * r - 4)
                tile = (j // 4) * AT + (j // 2) % 2
                pool.tensor_copy(v_heads[:, r], v_sb[:, bass.ds(tile, 2), bass.ds((2 * (j % 2) + r) * P, P)]
                                 ).then_inc(v_staged, 1)

            def normalise(n, s, first=False):
                pool.wait_ge(inv_ready, n + 1)
                if not first:
                    pool.wait_ge(turned, n - 1)
                pool.tensor_tensor(out=probs_n[:, s % 2], in0=probs[:, s % 4],
                                   in1=prob_inv[:, s % 4].unsqueeze(2).to_broadcast([P, 2, WIN]),
                                   op=ALU.mult).then_inc(normalised, 1)

            def heads(j, first=False, last=False):
                for r in range(8):
                    if r == 2 or r == 6:
                        stage_v(j, r // 4, first)
                    if not (last and r + 2 >= 8):
                        normalise(8 * j + r + 2, r + 2)

            pool.wait_ge(v_ready, B * AT)
            normalise(0, 0, True)
            normalise(1, 1, True)
            heads(0, first=True)
            with pool.Fori(1, 7) as j:
                heads(j)
            heads(7, last=True)
            pool.memset(down8[:], 0.0).then_inc(route_consts, 1)
            pool.iota(token_no[:], [[P, NT]], base=0, channel_multiplier=1, **exact).then_inc(route_consts, 1)
            pool.iota(iota128[:], [[1, P]], base=0, channel_multiplier=0, **exact).then_inc(route_consts, 1)
            pool.iota(iota_tc[:], [[1, TC]], base=0, channel_multiplier=0, **exact).then_inc(route_consts, 1)
            pool.wait_ge(route_consts, 1)
            pool.iota(down8[:], [[-1, E]], base=E, channel_multiplier=0, **exact).then_inc(route_consts, 1)

            def gather(t, r, first=False):
                if not first:
                    pool.wait_ge(xg_turned, t - 1)
                pool.tensor_copy(gather_at[r][:], slot_token[:, bass.ds(t, 1)]).then_inc(picked, 1)
                pool.wait_ge(picked, t + 1)
                pool.nop(nofuse=True)
                pool.indirect_dma_start(out=x_gath[:, r, :], out_offset=None, in_=x3_dram,
                                        in_offset=bass.IndirectOffsetOnAxis(ap=gather_at[r][:].bitcast(U32), axis=0)
                                        ).then_inc(gathered[r], 16)

            def pick_score(t, r, first=False):
                if not first:
                    pool.wait_ge(y_scaled, t - 1)
                pool.tensor_copy(score_col[:, r:r + 1], slot_score[:, bass.ds(t, 1)]).then_inc(score_picked, 1)

            pool.wait_ge(routed, 2)
            for r in range(2):
                pool.wait_ge(x3_stored[r], 16 * NT // 2)
            gather(0, 0, True)
            pick_score(0, 0, True)
            gather(1, 1, True)
            pick_score(1, 1, True)
            gather(2, 0)
            gather(3, 1)
            pick_score(2, 0)
            with pool.Fori(2, (SLOT_TILES - 1) // 2) as j:
                for r in range(2):
                    gather(2 * j + r, r)
                    pick_score(2 * j + r - 1, 1 - r)
            gather(SLOT_TILES - 1, 0)
            for t in range(SLOT_TILES - 2, SLOT_TILES):
                pick_score(t, t % 2)
            pool.wait_ge(y_stored[0], 16 * (SLOT_TILES + 1) // 2)
            pool.wait_ge(y_stored[1], 16 * (SLOT_TILES // 2))
            pool.nop(nofuse=True)
            for i in range(NT):
                for c in range(2):
                    n = c * NT + i
                    pool.indirect_dma_start(out=y_back[:, n, :], out_offset=None, in_=y_dram,
                                            in_offset=bass.IndirectOffsetOnAxis(ap=slot_u[:, n:n + 1].bitcast(U32), axis=0)
                                            ).then_inc(y_fetched[i], 16)

        @block.scalar
        def _(act):
            act.dma_start(b_in_row[:], b_in.partition_broadcast(P)).then_inc(rows_loaded, 16)
            act.dma_start(g_init_row[:], g_init[0:D].partition_broadcast(P)).then_inc(rows_loaded, 16)
            act.dma_start(g_res_col[:], g_res.rearrange("(k p) -> p k", p=P), allow_slow_non_contiguous=True).then_inc(rows_loaded, 16)
            act.dma_start(b_qk_col[:], b_qkv[0:2 * D].rearrange("(k p) -> p k", p=P),
                          allow_slow_non_contiguous=True).then_inc(cols_loaded, 16)
            act.dma_start(w_gate_sb[:], w_gate.rearrange("(k p) e -> p k e", p=P)).then_inc(gate_loaded, 16)
            act.dma_start(b_v_row[:], b_qkv[2 * D:3 * D].partition_broadcast(P)).then_inc(cols_loaded, 16)
            act.dma_start(b_out_row[:], b_out.partition_broadcast(P)).then_inc(cols_loaded, 16)
            act.wait_ge(var_ready, 1)
            act.activation(sd[:], var_eps[:], ACT.Sqrt).then_inc(rooted, 1)
            act.wait_ge(var_ready, 2)
            act.activation(sd[:], var_eps[:], ACT.Sqrt).then_inc(rooted, 1)
            act.wait_ge(scales_ready, 1)
            for i in range(NT):
                if i >= 2:
                    act.wait_ge(h_turned, i - 1)
                act.activation(hn[:, i % 2, :], x_res[:, i, :], ACT.Identity, bias=row_shift[:, i:i + 1],
                               scale=row_scale[:, i:i + 1]).then_inc(normed, 1)
                if i < B:
                    act.wait_ge(ctx_loaded[i], 16)
                    for k in range(LT):
                        n = i * LT + k
                        if n > 0:
                            act.wait_ge(ctx_summed, n)
                        act.activation(squares[:], ctx_sb[:, n, :], ACT.Square,
                                       accum_out=ctx_ss[:, n:n + 1]).then_inc(ctx_summed, 1)
                if i == 1:
                    act.wait_ge(ctx_eps, 1)
                    act.activation(ctx_sd[:], ctx_rs[:], ACT.Sqrt).then_inc(ctx_rooted, 1)
                    for n in range(B * LT):
                        act.wait_ge(gap_ready, n + 1)
                        lo = (n % LT) * P
                        act.activation(gap[:, n % 2, lo:], gap[:, n % 2, lo:], ACT.Exp, bias=lnb[:], scale=-DT).then_inc(decayed, 1)

            act.wait_ge(att_var, 1)
            act.activation(sd[:], var_eps[:], ACT.Sqrt).then_inc(att_root, 1)
            act.wait_ge(att_scale, 1)
            for m in range(B * AT):
                i = (m // AT) * LT + m % AT
                if m >= 2:
                    act.wait_ge(xn_turned, m - 1)
                act.activation(xn[:, m % 2, :], x_res[:, i, :], ACT.Identity, bias=row_shift[:, i:i + 1],
                               scale=rstd[:, i:i + 1]).then_inc(xn_ready, 1)
            act.wait_ge(cols_loaded, 48)
            for u in range(B * 2 * DC):
                c = u % (2 * DC)
                act.wait_ge(qk_summed, u + 1)
                if u >= 2:
                    act.wait_ge(qk_stored[u % 2], 32 * (u // 2))
                act.activation(qk_hi[:, u % 2, :].bitcast(F32R), banks[u % 3][:, 0:AROWS], ACT.Identity,
                               bias=b_qk_col[:, c:c + 1]).then_inc(qk_hi_ready, 1)

            def exponents(n, s, first=False):
                act.wait_ge(max_ready, n + 1)
                if not first:
                    act.wait_ge(normalised, n - 3)
                for q in range(2):
                    last = act.activation(probs[:, s % 4, q], banks[s % 4][:, q * WIN:(q + 1) * WIN], ACT.Exp,
                                          bias=max_bias[:, s % 4, q:q + 1], scale=HD ** -0.5,
                                          accum_out=prob_sum[:, s % 4, q:q + 1])
                last.then_inc(exp_done, 1)

            def keep_heads(it, r):
                act.wait_ge(pv_done, 4 * it + 4)
                act.activation(oT[:, bass.ds(it, 1), :].rearrange("p a t -> p (a t)"), banks[6 + r % 2][:, 0:WIN],
                               ACT.Copy).then_inc(oT_ready, 1)

            def heads(j, first=False, last=False):
                for r in range(8):
                    if not (last and r + 3 >= 8):
                        exponents(8 * j + r + 3, r + 3, first and r + 3 < 4)
                    if r == 4:
                        keep_heads(2 * j, 0)
                    if r == 0 and not first:
                        keep_heads(2 * j - 1, 1)

            for n in range(3):
                exponents(n, n, True)
            heads(0, first=True)
            with act.Fori(1, 7) as j:
                heads(j)
            heads(7, last=True)
            keep_heads(15, 1)
            for i in range(NT):
                act.wait_ge(x3_var, i + 1)
                act.activation(sd[:, i:i + 1], var_eps[:, i:i + 1], ACT.Sqrt).then_inc(x3_root, 1)
                act.wait_ge(x3_scale, i + 1)
                if i >= 2:
                    act.wait_ge(x3_turned, i - 1)
                    act.wait_ge(x3_stored[i % 2], 16 * (i // 2))
                act.activation(x3[:, i % 2, :], x_res[:, i, :], ACT.Identity, bias=row_shift[:, i:i + 1],
                               scale=rstd[:, i:i + 1]).then_inc(x3_ready, 1)

            def split_hi(base, q, n):
                act.wait_ge(raw_loaded[q % 2], 16 * (2 * n + q // 2) + 16)
                act.activation(w_hi[:, bass.ds(base + q * QCOLS, QCOLS)], w_raw[:, q % 2, :], ACT.Copy).then_inc(hi_split, 1)

            for n in range(2):
                for q in range(WQ):
                    split_hi(n * WCOLS, q, n)
                    if n == 0 and q == 1:
                        act.wait_ge(gap2_ready, 1)
                        act.activation(exp_gap[:], exp_gap[:], ACT.Exp).then_inc(gap2_exp, 1)

            def take_x(t, r):
                act.wait_ge(xg_turned, t + 1)
                act.activation(xT_hi[:].rearrange("p k t -> p (k t)"), banks[5][:], ACT.Copy).then_inc(xT_hi_ready, 1)

            def take_h(t):
                act.wait_ge(h_turned2, t + 1)
                for a in range(2):
                    last = act.activation(hT_hi[:, 4 * a:4 * a + 4, :].rearrange("p k t -> p (k t)"), banks[2 + a][:],
                                          ACT.Relu)
                last.then_inc(hT_hi_ready, 1)

            def give_y(t, r):
                act.wait_ge(y_added, t + 1)
                act.wait_ge(score_picked, t + 1)
                act.activation(y_sb[:, r, :], y_sb[:, r, :], ACT.Copy, scale=score_col[:, r:r + 1]).then_inc(y_scaled, 1)
                act.wait_ge(y_scaled, t + 1)
                act.dma_start(y_dram[bass.ds(t * P, P), :], y_sb[:, r, :]).then_inc(y_stored[r], 16)

            def split_next(t, half):
                load = act.value_load(tile_loads[0:1, bass.ds(t, 1)], min_val=0, max_val=1)
                e = act.value_load(tile_next[0:1, bass.ds(t, 1)], min_val=0, max_val=E - 1)
                act.wait_ge(down_done if half else up_done, t)
                act.wait_ge(hi_split, WQ * t + WQ + 2 * half)
                act.nop(nofuse=True)
                with act.If(load == 1):
                    base = act.snap((e % 2) * WCOLS)
                    for q in (2 * half, 2 * half + 1):
                        split_hi(base, q, t + 1)
                with act.Else():
                    act.sem_inc(hi_split, 2)
                act.nop(nofuse=True)

            act.wait_ge(tables_ready, 1)
            take_x(0, 0)
            take_x(1, 1)
            take_h(0)

            def tile(t, r, last=False):
                if not last:
                    take_x(t + 1, 1 - r)
                split_next(t, 0)
                give_y(t - 1, 1 - r)
                take_h(t)
                split_next(t, 1)

            with act.Fori(0, (SLOT_TILES - 3) // 2) as j:
                for r in (1, 0):
                    tile(2 * j + 2 - r, r)
            tile(SLOT_TILES - 2, 1)
            tile(SLOT_TILES - 1, 0, last=True)
            give_y(SLOT_TILES - 1, 0)
            for r in range(2):
                act.wait_ge(y_stored[r], 16 * ((SLOT_TILES + 1 - r) // 2))

        @block.vector
        def _(dve):
            own = Steps(dve, vector_step)
            dve.wait_ge(consts, 6)
            dve.wait_ge(lens_loaded, 16)
            own.then(dve.tensor_copy(lens_f[:], lens_i[:].rearrange("p b j -> p (b j)")))
            for b in range(B):
                dve.tensor_tensor_scan(within[:, b, :], ones_f[:, 0:NJ], lens_f[:, b * NJ:(b + 1) * NJ], 0.0,
                                       ALU.mult, ALU.add).then_inc(lens_scanned, 1)
            dve.wait_ge(x_loaded, 16)
            for i in range(NT):
                own.step(dve.bn_stats(bn[:, i, :], x_res[:, i, :]))
            own.join()
            for i in range(NT):
                own.step(dve.bn_aggr(mv[:, i, :], bn[:, i, :]))
            own.join()
            dve.tensor_scalar(var_eps[:], mv[:, :, 1], LN_EPS, None, ALU.add).then_inc(var_ready, 1)
            dve.wait_ge(prefix_done, 1)
            own.then(dve.tensor_copy(prefix[:], banks[0][:, 0:B]))
            for b in range(B):
                own.step(dve.tensor_scalar(bidx[:, b * NJ:(b + 1) * NJ], within[:, b, :], prefix[:, b:b + 1], -1.0,
                                           ALU.add, ALU.add))
            own.join()
            own.then(dve.tensor_scalar(wrap[:], bidx[:], 0.0, float(L), ALU.is_lt, ALU.mult))
            own.then(dve.tensor_tensor(cell[:], bidx[:], wrap[:], ALU.add))
            own.step(dve.tensor_scalar(cell_hi[:], cell[:], 5, None, ALU.arith_shift_right))
            own.step(dve.tensor_scalar(cell_lo[:], cell[:], 31, None, ALU.bitwise_and))
            own.join()
            dve.wait_ge(consts2, 6)
            dve.tensor_tensor(oh_hi[:], cell_hi[:].unsqueeze(2).to_broadcast([P, B * NJ, 16]),
                              iota16[:].unsqueeze(1).to_broadcast([P, B * NJ, 16]), ALU.is_equal).then_inc(onehots, 1)
            dve.tensor_tensor(oh_lo[:], cell_lo[:].unsqueeze(2).to_broadcast([P, B * NJ, 32]),
                              iota32[:].unsqueeze(1).to_broadcast([P, B * NJ, 32]), ALU.is_equal).then_inc(onehots, 1)
            dve.wait_ge(rooted, 1)
            own.then(dve.reciprocal(rstd[:], sd[:]))
            own.then(dve.tensor_tensor(tmp8[:], rstd[:], rstd[:], ALU.mult))
            own.then(dve.tensor_tensor(tmp8[:], tmp8[:], mv[:, :, 1], ALU.mult))
            dve.tensor_scalar(var_eps[:], tmp8[:], RMS_EPS, None, ALU.add).then_inc(var_ready, 1)
            dve.wait_ge(rooted, 2)
            own.then(dve.reciprocal(tmp8[:], sd[:]))
            own.then(dve.tensor_tensor(row_scale[:], tmp8[:], rstd[:], ALU.mult))
            dve.scalar_tensor_tensor(row_shift[:], mv[:, :, 0], -1.0, row_scale[:], ALU.mult,
                                     ALU.mult).then_inc(scales_ready, 1)
            dve.wait_ge(rows_loaded, 48)
            for k in range(DC):
                dve.wait_ge(w_in_turned, k + 1)
                dve.tensor_scalar(w_inT[:, k, :], banks[1 + k % 2][:], g_res_col[:, k:k + 1], None,
                                  ALU.mult).then_inc(w_in_ready, 1)

            def copy_hT(i):
                dve.wait_ge(h_turned, i + 1)
                if i >= 2:
                    dve.wait_ge(embedded, i - 1)
                dve.tensor_copy(hT[:, i % 2].rearrange("p k t -> p (k t)"), banks[3 + i % 2][:]).then_inc(h_copied, 1)

            copy_hT(0)
            copy_hT(1)
            dve.wait_ge(hits_done, 1)
            own.then(dve.tensor_scalar(hits[:], banks[0][0:16, 64:64 + B * 32].rearrange("p (b c) -> p b c", b=B),
                                       1.0, None, ALU.min))
            for b in range(B):
                dve.tensor_tensor(blocks[:, b], hits[:, b, :].unsqueeze(1).to_broadcast([16, 16, 32]),
                                  diag16[:].unsqueeze(2).to_broadcast([16, 16, 32]), ALU.mult).then_inc(blocks_ready, 1)
            dve.wait_ge(ctx_summed, B * LT)
            dve.tensor_scalar(ctx_rs[:], ctx_ss[:], 1.0 / DG, RMS_EPS, ALU.mult, ALU.add).then_inc(ctx_eps, 1)
            for b in range(B):
                dve.wait_ge(rows_counted, b + 1)
                own.then(dve.tensor_tensor_scan(plug[:, b, :], ones_f[:], banks[1 + b][:], 0.0, ALU.mult, ALU.add))
                own.then(dve.tensor_scalar(plug[:, b, :], plug[:, b, :], -1.0, 0.0, ALU.add, ALU.max))
            dve.wait_ge(ctx_rooted, 1)
            own.then(dve.reciprocal(ctx_rs[:], ctx_sd[:]))

            def decay_gap(n):
                b, k = divmod(n, LT)
                if n >= 2:
                    dve.wait_ge(decay_ready, n - 1)
                dve.tensor_scalar(gap[:, n % 2, k * P:], plug[:, b, k * P:], s_col[:, k:k + 1], 0.0,
                                  ALU.subtract, ALU.max).then_inc(gap_ready, 1)

            def decay_mask(n):
                b, k = divmod(n, LT)
                dve.wait_ge(decayed, n + 1)
                dve.scalar_tensor_tensor(decay[:, n, k * P:], plug[:, b, k * P:], s_col[:, k:k + 1],
                                         gap[:, n % 2, k * P:], ALU.is_ge, ALU.mult).then_inc(decay_ready, 1)

            decay_gap(0)
            for n in range(B * LT):
                if n + 1 < B * LT:
                    decay_gap(n + 1)
                dve.scalar_tensor_tensor(patches[:, n, :], ctx_sb[:, n, 0:D], ctx_rs[:, n:n + 1], g_init_row[:],
                                         ALU.mult, ALU.mult).then_inc(patches_ready, 1)
                decay_mask(n)
            for i in range(NT):
                dve.wait_ge(embedded, i + 1)
                dve.wait_ge(xb_ready, i + 1)
                dve.tensor_tensor(x_res[:, i, :], x_res[:, i, :], banks[5 + i % 2][:], ALU.add).then_inc(x1_ready, 1)
                if i + 2 < NT:
                    copy_hT(i + 2)

            dve.wait_ge(x1_ready, NT)

            def row_stats():
                for i in range(NT):
                    own.step(dve.bn_stats(bn[:, i, :], x_res[:, i, :]))
                own.join()
                for i in range(NT):
                    own.step(dve.bn_aggr(mv[:, i, :], bn[:, i, :]))
                own.join()

            row_stats()
            dve.tensor_scalar(var_eps[:], mv[:, :, 1], LN_EPS, None, ALU.add).then_inc(att_var, 1)
            dve.wait_ge(att_root, 1)
            own.then(dve.reciprocal(rstd[:], sd[:]))
            dve.scalar_tensor_tensor(row_shift[:], mv[:, :, 0], -1.0, rstd[:], ALU.mult, ALU.mult).then_inc(att_scale, 1)
            for m in range(B * AT):
                dve.wait_ge(xn_turned, m + 1)
                dve.tensor_copy(xnT[:, :, m * P:(m + 1) * P],
                                banks[3 + m % 2][:].rearrange("p (k t) -> p k t", k=DC)).then_inc(xnT_ready, 1)
            dve.wait_ge(cols_loaded, 48)
            for u in range(B * 2 * DC):
                c = u % (2 * DC)
                dve.wait_ge(qk_hi_ready, u + 1)
                if u >= 2:
                    dve.wait_ge(qk_stored[u % 2], 32 * (u // 2))
                dve.scalar_tensor_tensor(qk_lo[:, u % 2, :].bitcast(F32R), banks[u % 3][:, 0:AROWS], b_qk_col[:, c:c + 1],
                                         qk_hi[:, u % 2, :], ALU.add, ALU.subtract).then_inc(qk_lo_ready, 1)
            for m in range(B * AT):
                dve.wait_ge(v_summed, m + 1)
                dve.tensor_tensor(v_sb[:, m, :], banks[5 + m % 2][:], b_v_row[:], ALU.add).then_inc(v_ready, 1)

            def maxima(n, s):
                dve.wait_ge(scores_ready, n + 1)
                dve.tensor_reduce(neg_max[:, s % 4, :], banks[s % 4][:].rearrange("p (q k) -> p q k", q=2),
                                  AX.X, ALU.max, negate=True).then_inc(max_taken, 1)
                dve.wait_ge(max_taken, n + 1)
                dve.tensor_scalar(max_bias[:, s % 4, :], neg_max[:, s % 4, :], HD ** -0.5, None,
                                  ALU.mult).then_inc(max_ready, 1)

            def inverse(n, s, first=False):
                dve.wait_ge(exp_done, n + 1)
                if not first:
                    dve.wait_ge(normalised, n - 3)
                dve.reciprocal(prob_inv[:, s % 4, :], prob_sum[:, s % 4, :]).then_inc(inv_ready, 1)

            def copy_probsT(n, s, first=False):
                dve.wait_ge(turned, n + 1)
                if not first:
                    dve.wait_ge(pv_done, n - 1)
                dve.tensor_copy(probsT[:, s % 2].rearrange("p a q -> p (a q)"), banks[4 + s % 2][:]).then_inc(probsT_ready, 1)

            def heads(j, first=False, last=False):
                for r in range(8):
                    if not (last and r + 3 >= 8):
                        maxima(8 * j + r + 3, r + 3)
                    if not (last and r + 2 >= 8):
                        inverse(8 * j + r + 2, r + 2, first and r + 2 < 4)
                    copy_probsT(8 * j + r, r, first and r < 2)

            for n in range(3):
                maxima(n, n)
            inverse(0, 0, True)
            inverse(1, 1, True)
            heads(0, first=True)
            with dve.Fori(1, 7) as j:
                heads(j)
            heads(7, last=True)
            def copy_x3T(i):
                dve.wait_ge(x3_turned, i + 1)
                if i >= 2:
                    dve.wait_ge(gated, i - 1)
                dve.tensor_copy(x3T[:, i % 2].rearrange("p k t -> p (k t)"), banks[3 + i % 2][:]).then_inc(x3T_ready, 1)

            own.step(dve.memset(ones8[:], 1.0))
            for i in range(NT):
                dve.wait_ge(projected, i + 1)
                dve.wait_ge(xo_ready, i + 1)
                dve.tensor_tensor(x_res[:, i, :], x_res[:, i, :], banks[i % 2][:], ALU.add).then_inc(x2_ready, 1)
                dve.wait_ge(x2_ready, i + 1)
                own.then(dve.bn_stats(bn[:, i, :], x_res[:, i, :]))
                own.then(dve.bn_aggr(mv[:, i, :], bn[:, i, :]))
                dve.tensor_scalar(var_eps[:, i:i + 1], mv[:, i, 1:2], LN_EPS, None, ALU.add).then_inc(x3_var, 1)
                dve.wait_ge(x3_root, i + 1)
                own.then(dve.reciprocal(rstd[:, i:i + 1], sd[:, i:i + 1]))
                dve.scalar_tensor_tensor(row_shift[:, i:i + 1], mv[:, i, 0:1], -1.0, rstd[:, i:i + 1], ALU.mult,
                                         ALU.mult).then_inc(x3_scale, 1)
                if i >= 1:
                    copy_x3T(i - 1)
            copy_x3T(NT - 1)
            dve.wait_ge(gated, NT)
            dve.wait_ge(route_consts, 5)
            own.then(dve.tensor_copy(logit[:].rearrange("p i e -> p (i e)"), banks[5][:, 0:NT * E]))

            def over_e(row):
                return row.unsqueeze(2).to_broadcast([P, NT, E])

            down = down8[:].unsqueeze(1).to_broadcast([P, NT, E])
            for c in range(2):
                own.then(dve.tensor_reduce(top[c][:], logit[:], AX.X, ALU.max))
                own.then(dve.tensor_tensor(eq[:], logit[:], over_e(top[c][:]), ALU.is_equal))
                own.then(dve.tensor_tensor(eq[:], eq[:], down, ALU.mult))
                own.then(dve.tensor_reduce(rank_key[:], eq[:], AX.X, ALU.max))
                own.then(dve.tensor_tensor(pick[:, c], down, over_e(rank_key[:]), ALU.is_equal))
                if c == 0:
                    own.then(dve.scalar_tensor_tensor(logit[:], pick[:, 0], -1e30, logit[:], ALU.mult, ALU.add))
            dve.tensor_tensor(exp_gap[:], top[1][:], top[0][:], ALU.subtract).then_inc(gap2_ready, 1)
            own.step(dve.tensor_copy(before_bf[:], before[:]))
            own.step(dve.memset(earlier[:, 0, :], 0.0))
            own.then(dve.tensor_tensor(chosen[:], pick[:, 0], pick[:, 1], ALU.add))
            for i in range(NT):
                own.then(dve.tensor_tensor(earlier[:, i + 1, :], earlier[:, i, :], chosen[:, i, :], ALU.add))
            dve.sem_inc(ranks_asked, 1)

            def split_lo(base, q, n):
                dve.wait_ge(raw_loaded[q % 2], 16 * (2 * n + q // 2) + 16)
                dve.wait_ge(hi_split, WQ * n + q + 1)
                dve.tensor_tensor(w_lo[:, bass.ds(base + q * QCOLS, QCOLS)], w_raw[:, q % 2, :],
                                  w_hi[:, bass.ds(base + q * QCOLS, QCOLS)].bitcast(F32), ALU.subtract).then_inc(lo_split, 1)

            split_lo(0, 0, 0)
            split_lo(0, 1, 0)
            dve.wait_ge(gap2_exp, 1)
            own.then(dve.tensor_scalar(denom[:], exp_gap[:], 1.0, None, ALU.add))
            own.then(dve.reciprocal(score[:, 0, :], denom[:]))
            own.then(dve.tensor_tensor(score[:, 1, :], score[:, 0, :], exp_gap[:], ALU.mult))
            dve.wait_ge(ranked, 1)
            own.then(dve.tensor_copy(rank_sb[:].rearrange("p i e -> p (i e)"), banks[7][:, 0:(NT + 1) * E]))
            own.then(dve.tensor_scalar(count_i[:], rank_sb[:, NT, :], float(P - 1), None, ALU.add))
            own.then(dve.tensor_scalar(count_i[:], count_i[:], 7, None, ALU.arith_shift_right))
            own.then(dve.tensor_scalar(tiles_of[:], count_i[:], 1.0, None, ALU.max))
            own.then(dve.tensor_tensor_scan(tiles_end[:], ones8[:], tiles_of[:], 0.0, ALU.mult, ALU.add))
            own.then(dve.tensor_tensor(slot_base[:], tiles_end[:], tiles_of[:], ALU.subtract))
            own.step(dve.tensor_tensor(tile_cmp[:], iota_tc[:].unsqueeze(2).to_broadcast([P, TC, E]),
                                       tiles_end[:].unsqueeze(1).to_broadcast([P, TC, E]), ALU.is_ge))
            own.then(dve.scalar_tensor_tensor(slot_all[:], slot_base[:].unsqueeze(1).to_broadcast([P, NT, E]), float(P),
                                              rank_sb[:, 0:NT, :], ALU.mult, ALU.add))
            own.step(dve.tensor_reduce(tile_e[:], tile_cmp[:], AX.X, ALU.add))
            for c in range(2):
                own.step(dve.tensor_tensor(slot_pick[:, c], slot_all[:], pick[:, c], ALU.mult))
            own.join()
            own.step(dve.memset(tile_new[:], 0.0))
            own.then(dve.tensor_scalar(tile_e[:], tile_e[:], float(E - 1), None, ALU.min))
            own.step(dve.tensor_copy(tile_expert[:], tile_e[0:1, :]))
            own.then(dve.tensor_tensor(tile_new[:, 1:], tile_e[:, 1:], tile_e[:, :-1], ALU.is_gt))
            own.then(dve.scalar_tensor_tensor(tile_loads[:], tile_e[0:1, :], float(E - 1), tile_new[0:1, :], ALU.is_lt,
                                              ALU.mult))
            own.then(dve.tensor_scalar(tile_next[:], tile_e[0:1, :], 1.0, float(E - 1), ALU.add, ALU.min))
            dve.sem_inc(tables_ready, 1)
            for c in range(2):
                own.step(dve.tensor_reduce(slot_f[:, c, :], slot_pick[:, c], AX.X, ALU.add))
            own.join()
            own.then(dve.tensor_copy(slot_u[:], slot_f[:].rearrange("p c i -> p (c i)")))
            own.step(dve.tensor_scalar(slot_hi[:], slot_u[:], 7, None, ALU.arith_shift_right))
            own.step(dve.tensor_scalar(slot_lo[:], slot_u[:], P - 1, None, ALU.bitwise_and))
            own.join()
            own.step(dve.tensor_tensor(lo_hot[:], slot_lo[:].unsqueeze(2).to_broadcast([P, 2 * NT, P]),
                                       iota128[:].unsqueeze(1).to_broadcast([P, 2 * NT, P]), ALU.is_equal))
            own.then(dve.tensor_tensor(hi_hot[:], slot_hi[:].unsqueeze(2).to_broadcast([P, 2 * NT, TC]),
                                       iota_tc[:].unsqueeze(1).to_broadcast([P, 2 * NT, TC]), ALU.is_equal))
            for c in range(2):
                own.step(dve.tensor_tensor(cast[:, c * NT:(c + 1) * NT, 0, :], hi_hot[:, c * NT:(c + 1) * NT, :],
                                           token_no[:].unsqueeze(2).to_broadcast([P, NT, TC]), ALU.mult))
                own.step(dve.tensor_tensor(cast[:, c * NT:(c + 1) * NT, 1, :], hi_hot[:, c * NT:(c + 1) * NT, :],
                                           score[:, c, :].unsqueeze(2).to_broadcast([P, NT, TC]), ALU.mult))
            own.join()
            dve.sem_inc(casts_ready, 1)
            dve.wait_ge(cast_done, 1)
            dve.tensor_copy(slot_token[:], banks[6][:, 0:TC]).then_inc(routed, 1)
            dve.tensor_copy(slot_score[:], banks[6][:, TC:2 * TC]).then_inc(routed, 1)
            for n in range(2):
                for q in range(WQ):
                    if n or q >= 2:
                        split_lo(n * WCOLS, q, n)

            def take_x(t):
                dve.wait_ge(xT_hi_ready, t + 1)
                dve.tensor_tensor(xT_lo[:].rearrange("p k t -> p (k t)"), banks[5][:],
                                  xT_hi[:].rearrange("p k t -> p (k t)").bitcast(F32), ALU.subtract).then_inc(xT_lo_ready, 1)

            def take_h(t, r):
                dve.wait_ge(up_done, t + 1)
                dve.wait_ge(b1_loaded[r], 16 * (t // 2) + 16)
                for a in range(2):
                    last = dve.tensor_tensor(h_sb[:, a * 512:(a + 1) * 512], banks[a][:],
                                             b1_row[:, r, a * 512:(a + 1) * 512], ALU.add)
                last.then_inc(h_ready, 1)

            def take_hT(t):
                dve.wait_ge(hT_hi_ready, t + 1)
                for a in range(2):
                    last = dve.scalar_tensor_tensor(hT_lo[:, 4 * a:4 * a + 4, :].rearrange("p k t -> p (k t)"),
                                                    banks[2 + a][:], 0.0,
                                                    hT_hi[:, 4 * a:4 * a + 4, :].rearrange("p k t -> p (k t)").bitcast(F32),
                                                    ALU.max, ALU.subtract)
                last.then_inc(hT_lo_ready, 1)

            def take_y(t, r, first=False):
                dve.wait_ge(down_done, t + 1)
                dve.wait_ge(b2_loaded[r], 16 * (t // 2) + 16)
                if not first:
                    dve.wait_ge(y_stored[r], 16 * (t // 2))
                dve.tensor_tensor(y_sb[:, r, :], banks[4][:], b2_row[:, r, :], ALU.add).then_inc(y_added, 1)

            def split_next(t, half):
                load = dve.value_load(tile_loads[0:1, bass.ds(t, 1)], min_val=0, max_val=1)
                e = dve.value_load(tile_next[0:1, bass.ds(t, 1)], min_val=0, max_val=E - 1)
                dve.wait_ge(down_done if half else up_done, t)
                dve.wait_ge(lo_split, WQ * t + WQ + 2 * half)
                dve.nop(nofuse=True)
                with dve.If(load == 1):
                    base = dve.snap((e % 2) * WCOLS)
                    for q in (2 * half, 2 * half + 1):
                        split_lo(base, q, t + 1)
                with dve.Else():
                    dve.sem_inc(lo_split, 2)
                dve.nop(nofuse=True)

            take_x(0)
            take_h(0, 0)
            take_x(1)
            take_hT(0)

            def tile(t, r, first=False, last=False):
                take_h(t, r)
                if not last:
                    take_x(t + 1)
                split_next(t, 0)
                take_y(t - 1, 1 - r, first)
                take_hT(t)
                split_next(t, 1)

            tile(1, 1, first=True)
            tile(2, 0, first=True)
            with dve.Fori(1, (SLOT_TILES - 3) // 2) as j:
                for r in (1, 0):
                    tile(2 * j + 2 - r, r)
            tile(SLOT_TILES - 2, 1)
            tile(SLOT_TILES - 1, 0, last=True)
            take_y(SLOT_TILES - 1, 0)
            for i in range(NT):
                dve.wait_ge(y_fetched[i], 32)
                dve.tensor_tensor(x_res[:, i, :], x_res[:, i, :], y_back[:, i, :], ALU.add).then_inc(y_first, 1)
                dve.wait_ge(y_first, i + 1)
                dve.tensor_tensor(x_res[:, i, :], x_res[:, i, :], y_back[:, NT + i, :], ALU.add).then_inc(x_out, 1)

        @block.tensor
        def _(pe):
            pe.wait_ge(consts2, 6)
            pe.wait_ge(lens_scanned, 2)
            pe.matmul(banks[0][:, 0:B], before[:], within[:, :, NJ - 1], start=True, stop=True).then_inc(prefix_done, 1)
            pe.wait_ge(w_in_loaded, 16)
            for k in range(DC):
                if k >= 2:
                    pe.wait_ge(w_in_ready, k - 1)
                for j in range(DC):
                    last = pe.transpose(banks[1 + k % 2][:, j * P:(j + 1) * P], w_in_sb[:, j, k * P:(k + 1) * P], ident[:])
                last.then_inc(w_in_turned, 1)

            def turn_h(i):
                pe.wait_ge(normed, i + 1)
                if i >= 2:
                    pe.wait_ge(h_copied, i - 1)
                for k in range(DC):
                    last = pe.transpose(banks[3 + i % 2][:, k * P:(k + 1) * P], hn[:, i % 2, k * P:(k + 1) * P], ident[:])
                last.then_inc(h_turned, 1)

            turn_h(0)
            turn_h(1)
            pe.wait_ge(onehots, 2)
            for b in range(B):
                for j in range(NJ):
                    n = b * NJ + j
                    last = pe.matmul(banks[0][0:16, 64 + b * 32:96 + b * 32], oh_hi[:, n, :], oh_lo[:, n, :],
                                     start=(j == 0), stop=(j == NJ - 1))
            last.then_inc(hits_done, 1)
            pe.wait_ge(w_in_ready, DC)
            for b in range(B):
                pe.wait_ge(blocks_ready, b + 1)
                pe.matmul(banks[1 + b][:], ones_bf[0:16, :], blocks[:, b].rearrange("p a c -> p (a c)"),
                          start=True, stop=True).then_inc(rows_counted, 1)
            for i in range(NT):
                b, li = divmod(i, LT)
                pe.wait_ge(h_copied, i + 1)
                if i >= 2:
                    pe.wait_ge(x1_ready, i - 1)
                for k in range(DC):
                    pe.matmul(banks[5 + i % 2][:], hT[:, i % 2, k, :], w_inT[:, k, :], start=(k == 0), stop=False)
                for k in range(li + 1):
                    n = b * LT + k
                    if li == k:
                        pe.wait_ge(patches_ready, n + 1)
                        pe.wait_ge(decay_ready, n + 1)
                    last = pe.matmul(banks[5 + i % 2][:], decay[:, n, li * P:(li + 1) * P], patches[:, n, :],
                                     start=False, stop=(k == li))
                last.then_inc(embedded, 1)
                if i + 2 < NT:
                    turn_h(i + 2)
            for m in range(B * AT):
                pe.wait_ge(xn_ready, m + 1)
                if m >= 2:
                    pe.wait_ge(xnT_ready, m - 1)
                for k in range(DC):
                    last = pe.transpose(banks[3 + m % 2][:, k * P:(k + 1) * P], xn[:, m % 2, k * P:(k + 1) * P], ident[:])
                last.then_inc(xn_turned, 1)
            pe.wait_ge(w_qkv_loaded, 16)
            pe.wait_ge(xnT_ready, B * AT)
            for u in range(B * 2 * DC):
                b, c = divmod(u, 2 * DC)
                if u >= 3:
                    pe.wait_ge(qk_lo_ready, u - 2)
                for k in range(DC):
                    last = pe.matmul(banks[u % 3][:, 0:AROWS], w_qkv_sb[:, k, c * P:(c + 1) * P],
                                     xnT[:, k, b * AROWS:(b + 1) * AROWS], start=(k == 0), stop=(k == DC - 1))
                last.then_inc(qk_summed, 1)
            pe.wait_ge(x1_ready, NT)
            for m in range(B * AT):
                if m >= 2:
                    pe.wait_ge(v_ready, m - 1)
                for k in range(DC):
                    last = pe.matmul(banks[5 + m % 2][:], xnT[:, k, m * P:(m + 1) * P], w_qkv_sb[:, k, 2 * D:3 * D],
                                     start=(k == 0), stop=(k == DC - 1))
                last.then_inc(v_summed, 1)

            def scores(n, s, j, first=False):
                r = s // 4 % 2
                if s % 4 == 0:
                    pe.wait_ge(parts_loaded[r], 96 * j + 96)
                if not first:
                    pe.wait_ge(exp_done, n - 3)
                for q in range(2):
                    last = pe.matmul(banks[s % 4][:, q * WIN:(q + 1) * WIN], q_parts[r][:, s % 4, q * P:(q + 1) * P],
                                     k_parts[r][:, s % 4, :], start=True, stop=True)
                last.then_inc(scores_ready, 1)

            def turn_probs(n, s, first=False):
                pe.wait_ge(normalised, n + 1)
                if not first:
                    pe.wait_ge(probsT_ready, n - 1)
                for a in range(2):
                    for q in range(2):
                        last = pe.transpose(banks[4 + s % 2][:, (2 * a + q) * P:(2 * a + q + 1) * P],
                                            probs_n[:, s % 2, q, a * P:(a + 1) * P], ident[:])
                last.then_inc(turned, 1)

            def weigh(n, s, it, first=False):
                r, h = s // 4 % 2, s % 4
                pe.wait_ge(probsT_ready, n + 1)
                if h == 0:
                    pe.wait_ge(v_staged, it + 1)
                    if not first:
                        pe.wait_ge(oT_ready, it - 1)
                for a in range(2):
                    last = pe.matmul(banks[6 + r][h * HD:(h + 1) * HD, 0:WIN], v_heads[:, r, a, h * HD:(h + 1) * HD],
                                     probsT[:, s % 2, a, :], start=(a == 0), stop=(a == 1))
                last.then_inc(pv_done, 1)

            def heads(j, first=False, last=False):
                for r in range(8):
                    if not (last and r + 3 >= 8):
                        scores(8 * j + r + 3, r + 3, j + (r + 3) // 8, first and r + 3 < 4)
                    turn_probs(8 * j + r, r, first and r < 2)
                    if not (first and r == 0):
                        weigh(8 * j + r - 1, (r - 1) % 8, 2 * j + (r - 1) // 4, first)

            pe.wait_ge(qk_lo_ready, B * 2 * DC)
            pe.wait_ge(v_ready, B * AT)
            for n in range(3):
                scores(n, n, 0, True)
            heads(0, first=True)
            with pe.Fori(1, 7) as j:
                heads(j)
            heads(7, last=True)
            weigh(63, 7, 15)
            def turn_x3(i):
                pe.wait_ge(x3_ready, i + 1)
                if i >= 2:
                    pe.wait_ge(x3T_ready, i - 1)
                for k in range(DC):
                    last = pe.transpose(banks[3 + i % 2][:, k * P:(k + 1) * P], x3[:, i % 2, k * P:(k + 1) * P], ident[:])
                last.then_inc(x3_turned, 1)

            pe.wait_ge(gate_loaded, 16)

            def gate(i):
                pe.wait_ge(x3T_ready, i + 1)
                for k in range(DC):
                    last = pe.matmul(banks[5][:, i * E:(i + 1) * E], x3T[:, i % 2, k, :], w_gate_sb[:, k, :],
                                     start=(k == 0), stop=(k == DC - 1))
                last.then_inc(gated, 1)

            pe.wait_ge(w_out_loaded, 16)
            for i in range(NT):
                w, q = divmod(i, 2)
                pe.wait_ge(oT_ready, 4 * w + 4)
                if i >= 2:
                    pe.wait_ge(x2_ready, i - 1)
                for g in range(4):
                    last = pe.matmul(banks[i % 2][:], oT[:, 4 * w + g, q * P:(q + 1) * P], w_out_sb[:, g, :],
                                     start=(g == 0), stop=(g == 3))
                last.then_inc(projected, 1)
                if i >= 1:
                    turn_x3(i - 1)
                if i >= 2:
                    gate(i - 2)
            turn_x3(NT - 1)
            gate(NT - 2)
            gate(NT - 1)
            pe.wait_ge(ranks_asked, 1)
            pe.matmul(banks[7][:, 0:(NT + 1) * E], ones_bf[:], earlier[:].rearrange("p i e -> p (i e)"), start=True,
                      stop=False)
            pe.matmul(banks[7][:, 0:NT * E], before_bf[:], chosen[:].rearrange("p i e -> p (i e)"), start=False,
                      stop=True).then_inc(ranked, 1)
            pe.wait_ge(casts_ready, 1)
            for n in range(2 * NT):
                last = pe.matmul(banks[6][:, 0:2 * TC], lo_hot[:, n, :], cast[:, n].rearrange("p a t -> p (a t)"),
                                 start=(n == 0), stop=(n == 2 * NT - 1))
            last.then_inc(cast_done, 1)

            def turn_x(t, r, first=False):
                pe.wait_ge(gathered[r], 16 * (t // 2) + 16)
                if not first:
                    pe.wait_ge(xT_lo_ready, t)
                for k in range(DC):
                    last = pe.transpose(banks[5][:, k * P:(k + 1) * P], x_gath[:, r, k * P:(k + 1) * P], ident[:])
                last.then_inc(xg_turned, 1)

            def up(t, s, first=False):
                pe.wait_ge(xT_lo_ready, t + 1)
                pe.wait_ge(hi_split, WQ * t + 2)
                pe.wait_ge(lo_split, WQ * t + 2)
                if not first:
                    pe.wait_ge(h_ready, t)
                for k in range(DC):
                    for x_part, w_parts in ((xT_hi, (w_hi, w_lo)), (xT_lo, (w_hi,))):
                        for a in range(2):
                            for w in w_parts:
                                last = pe.matmul(banks[a][:], x_part[:, k, :],
                                                 w[:, bass.ds(s + k * H + a * 512, 512)],
                                                 start=(k == 0 and x_part is xT_hi and w is w_hi),
                                                 stop=(k == DC - 1 and x_part is xT_lo))
                last.then_inc(up_done, 1)

            def down(t, s, first=False):
                pe.wait_ge(hT_lo_ready, t + 1)
                pe.wait_ge(hi_split, WQ * t + 4)
                pe.wait_ge(lo_split, WQ * t + 4)
                if not first:
                    pe.wait_ge(y_added, t)
                for k in range(HC):
                    for h_part, w_parts in ((hT_hi, (w_hi, w_lo)), (hT_lo, (w_hi,))):
                        for w in w_parts:
                            last = pe.matmul(banks[4][:], h_part[:, k, :], w[:, bass.ds(s + DC * H + k * D, D)],
                                             start=(k == 0 and h_part is hT_hi and w is w_hi),
                                             stop=(k == HC - 1 and h_part is hT_lo))
                last.then_inc(down_done, 1)

            def turn_hidden(t, first=False):
                pe.wait_ge(h_ready, t + 1)
                if not first:
                    pe.wait_ge(hT_lo_ready, t)
                for k in range(HC):
                    last = pe.transpose(banks[2 + k // 4][:, k % 4 * P:(k % 4 + 1) * P], h_sb[:, k * P:(k + 1) * P], ident[:])
                last.then_inc(h_turned2, 1)

            def half_of(t):
                e = pe.value_load(tile_expert[0:1, bass.ds(t, 1)], min_val=0, max_val=E - 1)
                return pe.snap((e % 2) * WCOLS)

            def tile(t, r, first=False, last=False):
                up(t, half_of(t))
                if not last:
                    turn_x(t + 1, 1 - r)
                down(t - 1, half_of(t - 1), first)
                turn_hidden(t)

            pe.wait_ge(tables_ready, 1)
            turn_x(0, 0, True)
            up(0, 0, True)
            turn_x(1, 1)
            turn_hidden(0, True)
            tile(1, 1, first=True)
            tile(2, 0)
            with pe.Fori(1, (SLOT_TILES - 3) // 2) as j:
                for r in (1, 0):
                    tile(2 * j + 2 - r, r)
            tile(SLOT_TILES - 2, 1)
            tile(SLOT_TILES - 1, 0, last=True)
            down(SLOT_TILES - 1, half_of(SLOT_TILES - 1))

    return nc


_INS = ['x', 'ctx_2048', 'mask_BxS2_if0', 'L0_xattn_W_in', 'L0_xattn_b_in', 'L0_xattn_g_res', 'L0_xattn_g_init',
        'L0_attn_w_qkv', 'L0_attn_b_qkv', 'L0_attn_w_out', 'L0_attn_b_out', 'L0_ffn_Wg', 'L0_ffn_W1', 'L0_ffn_b1',
        'L0_ffn_W2', 'L0_ffn_b2']


def kernel(**inputs):
    import numpy as _np
    import concourse.bacc as _bacc
    from concourse import mybir as _mybir
    from concourse.bass_utils import run_bass_kernel_spmd as _run

    nc = _bacc.Bacc("TRN2", target_bir_lowering=False, num_devices=1)
    arrays, args = {}, []
    for name in _INS:
        a = _np.ascontiguousarray(inputs[name])
        arrays[f"in_{name}_dram"] = a
        args.append(nc.dram_tensor(f"in_{name}_dram", a.shape, _mybir.dt.from_np(a.dtype), kind="ExternalInput").ap())
    args.append(nc.dram_tensor("out_0_dram", (B, L, D), _mybir.dt.float32, kind="ExternalOutput").ap())
    perceiver_layer(nc, *args)
    r = _run(nc, [arrays], core_ids=[0])
    return r.results[0]["out_0_dram"]
```

```python
import math
from contextlib import ExitStack

import concourse.bass as bass
from concourse import mybir

F32 = mybir.dt.float32
F32R = mybir.dt.float32r
BF16 = mybir.dt.bfloat16
I32 = mybir.dt.int32
U32 = mybir.dt.uint32
ALU = mybir.AluOpType
ACT = mybir.ActivationFunctionType
AX = mybir.AxisListType

P = 128
B, L, D = 2, 512, 512
T = B * L
NT = T // P
LT = L // P
DC = D // P
DG = 1024
NLEN = 8192
NJ = NLEN // P
HEADS, HD = 16, 32
WIN, STRIDE = 256, 128
NWIN = 2
AROWS = STRIDE * (NWIN - 1) + WIN
AT = AROWS // P
ORDER = [b * (L // P) + i for b in range(B) for i in range(AROWS // P)] + \
        [b * (L // P) + i for b in range(B) for i in range(AROWS // P, L // P)]
E, H = 8, 1024
HC = H // P
LN_EPS = 1e-5
RMS_EPS = 1e-5
LOGP = -0.001
DT = -math.log(-math.expm1(LOGP))
SLOT_TILES = 2 * T // P + E - 1
FULL_TILES = 2 * T // P
TC = SLOT_TILES + 1
WQ = 4
WCOLS = DC * H + HC * D
QCOLS = WCOLS // WQ


def perceiver_layer(nc, x_in, ctx_in, lens_in, w_in, b_in, g_res, g_init, w_qkv, b_qkv, w_out, b_out,
                    w_gate, w1, b1, w2, b2, out):
    x_rows = x_in.rearrange("b (i p) d -> p (b i) d", p=P)
    out_rows = out.rearrange("b (i p) d -> p (b i) d", p=P)

    with ExitStack() as ctx:
        def sem(name):
            return ctx.enter_context(nc.semaphore(name))

        banks = [ctx.enter_context(nc.psum_tensor(f"bank{i}", [P, 512], F32)) for i in range(8)]

        BASE = 16512
        K = 1024

        def place(name, shape, dtype, at):
            return nc.alloc_sbuf_tensor_at(name, shape, dtype, offset=BASE + at)

        x_res = place("x_res", [P, NT, D], F32, 0)
        SMALL, RAW, MID, BIG = 16 * K, 27 * K, 43 * K, 79 * K
        small_at = [SMALL]

        def small(name, shape, dtype):
            words = 1
            for n in shape[1:]:
                words *= n
            size = words * (2 if dtype == BF16 else 4)
            t = place(name, shape, dtype, small_at[0])
            small_at[0] += -(-size // 32) * 32
            assert small_at[0] <= RAW
            return t

        ident = small("ident", [P, P], F32)
        before = small("before", [P, P], F32)
        ones_bf = small("ones_bf", [P, P], BF16)
        s_col = small("s_col", [P, LT], F32)
        lnb = small("lnb", [P, 1], F32)
        iota16 = small("iota16", [P, 16], F32)
        iota32 = small("iota32", [P, 32], F32)
        diag16 = small("diag16", [16, 16], F32)
        g_res_col = small("g_res_col", [P, DC], F32)
        bn = small("bn", [P, NT, 6], F32)
        mv = small("mv", [P, NT, 2], F32)
        var_eps = small("var_eps", [P, NT], F32)
        sd = small("sd", [P, NT], F32)
        rstd = small("rstd", [P, NT], F32)
        row_scale = small("row_scale", [P, NT], F32)
        row_shift = small("row_shift", [P, NT], F32)
        tmp8 = small("tmp8", [P, NT], F32)
        ctx_ss = small("ctx_ss", [P, NT], F32)
        ctx_rs = small("ctx_rs", [P, NT], F32)
        ctx_sd = small("ctx_sd", [P, NT], F32)
        prefix = small("prefix", [P, B], F32)

        ctx_sb = place("ctx_sb", [P, B * LT, DG], F32, BIG)
        patches = place("patches", [P, B * LT, D], F32, BIG + 32 * K)
        decay = place("decay", [P, B * LT, L], F32, BIG + 48 * K)
        w_in_sb = place("w_in_sb", [P, DC, D], F32, BIG + 64 * K)
        w_inT = place("w_inT", [P, DC, D], F32, BIG + 72 * K)
        hT = place("hT", [P, 2, DC, P], F32, BIG + 80 * K)
        hn = place("hn", [P, 2, D], F32, BIG + 84 * K)
        oh_hi = place("oh_hi", [P, B * NJ, 16], BF16, BIG + 88 * K)
        oh_lo = place("oh_lo", [P, B * NJ, 32], BF16, BIG + 92 * K)
        lens_f = place("lens_f", [P, B * NJ], F32, BIG + 100 * K)
        within = place("within", [P, B, NJ], F32, BIG + 100 * K + 512)
        bidx = place("bidx", [P, B * NJ], F32, BIG + 101 * K)
        wrap = place("wrap", [P, B * NJ], F32, BIG + 101 * K + 512)
        cell = place("cell", [P, B * NJ], I32, BIG + 102 * K)
        cell_hi = place("cell_hi", [P, B * NJ], I32, BIG + 102 * K + 512)
        cell_lo = place("cell_lo", [P, B * NJ], I32, BIG + 123 * K)
        plug = place("plug", [P, B, L], F32, BIG + 103 * K)
        ones_f = place("ones_f", [P, L], F32, BIG + 107 * K)
        gap = place("gap", [P, 2, L], F32, BIG + 109 * K)
        blocks = place("blocks", [16, B, 16, 32], BF16, BIG + 113 * K)
        b_in_row = place("b_in_row", [P, D], F32, BIG + 126 * K)
        g_init_row = place("g_init_row", [P, D], F32, BIG + 117 * K)
        squares = place("squares", [P, DG], F32, BIG + 119 * K)
        lens_i = place("lens_i", [P, B, NJ], I32, BIG + 123 * K + 512)
        hits = place("hits", [16, B, 32], F32, BIG + 124 * K)

        w_raw = place("w_raw", [P, 2, QCOLS], F32, RAW)

        wq_raw = [place(f"wq_raw{k}", [P, 3 * D], F32, at) for k, at in
                  enumerate((RAW, RAW + 6 * K, MID + 24 * K, MID + 30 * K))]

        b_v_row = small("b_v_row", [P, D], F32)
        b_out_row = small("b_out_row", [P, D], F32)
        b_qk_col = small("b_qk_col", [P, 2 * DC], F32)
        neg_max = small("neg_max", [P, 4, 2], F32)
        max_bias = small("max_bias", [P, 4, 2], F32)
        prob_sum = small("prob_sum", [P, 4, 2], F32)
        prob_inv = small("prob_inv", [P, 4, 2], F32)
        wq_hi = place("wq_hi", [P, DC, 3 * D], F32R, BIG)
        wq_lo = place("wq_lo", [P, DC, 3 * D], F32R, BIG + 88 * K)
        xn = place("xn", [P, 2, D], F32, BIG + 24 * K)
        xnT_hi = place("xnT_hi", [P, DC, B * AROWS], F32R, MID)
        xnT_lo = place("xnT_lo", [P, DC, B * AROWS], F32R, BIG + 112 * K)
        qk_hi = place("qk_hi", [P, 2, AROWS], F32, BIG + 28 * K)
        qk_lo = place("qk_lo", [P, 2, AROWS], F32, BIG + 31 * K)
        q_parts = place("q_parts", [3 * HD, 8, WIN], F32R, BIG + 46 * K)
        k_parts = place("k_parts", [3 * HD, 8, WIN], F32R, BIG + 54 * K)
        v_heads = place("v_heads", [P, 2, 2, P], F32, BIG + 62 * K)
        probs = place("probs", [P, 4, 2, WIN], F32, BIG + 34 * K)
        probs_n = place("probs_n", [P, 2, 2, WIN], F32, BIG + 96 * K)
        probsT = place("probsT", [P, 2, 2, WIN], F32, BIG + 100 * K)
        oT_hi = place("oT_hi", [P, B * NWIN * 4, WIN], F32R, MID)
        oT_lo = place("oT_lo", [P, B * NWIN * 4, WIN], F32R, BIG + 104 * K)
        w_out_sb = place("w_out_sb", [P, DC, D], F32, MID + 16 * K)
        w_out_lo = place("w_out_lo", [P, DC, D], F32R, MID + 16 * K)
        w_out_hi = place("w_out_hi", [P, DC, D], F32R, BIG + 120 * K)
        v_sb = place("v_sb", [P, B * AT, D], F32, MID + 24 * K)
        qk_dram = nc.dram_tensor("qk_parts", (2 * DC, 4, 3, HD, B * AROWS), F32, kind="Internal").ap()
        Q_PARTS, K_PARTS = (0, 1, 0), (0, 0, 1)

        w_gate_sb = small("w_gate_sb", [P, DC, E], F32)
        x3 = place("x3", [P, 2, D], F32, MID + 24 * K)
        x3T = place("x3T", [P, 2, DC, P], F32, MID + 28 * K)
        ROUTE = BIG + 110 * K
        route_at = [ROUTE]

        def route(name, shape, dtype=F32):
            words = 1
            for n in shape[1:]:
                words *= n
            t = place(name, shape, dtype, route_at[0])
            route_at[0] += -(-words * (2 if dtype == BF16 else 4) // 32) * 32
            assert route_at[0] <= BIG + 128 * K
            return t

        logit = route("logit", [P, NT, E])
        top = [route(f"top{c}", [P, NT]) for c in range(2)]
        eq = route("eq", [P, NT, E])
        rank_key = route("rank_key", [P, NT])
        pick = route("pick", [P, 2, NT, E])
        score = route("score", [P, 2, NT])
        exp_gap = route("exp_gap", [P, NT])
        denom = route("denom", [P, NT])
        chosen = route("chosen", [P, NT, E], BF16)
        earlier = route("earlier", [P, NT + 1, E], BF16)
        before_bf = route("before_bf", [P, P], BF16)
        rank_sb = route("rank_sb", [P, NT + 1, E])
        count_i = route("count_i", [P, E], I32)
        tiles_of = route("tiles_of", [P, E])
        tiles_end = route("tiles_end", [P, E])
        slot_base = route("slot_base", [P, E])
        slot_all = route("slot_all", [P, NT, E])
        slot_pick = route("slot_pick", [P, 2, NT, E])
        slot_f = route("slot_f", [P, 2, NT])
        slot_hi = route("slot_hi", [P, 2 * NT], I32)
        slot_lo = route("slot_lo", [P, 2 * NT], I32)
        lo_hot = route("lo_hot", [P, 2 * NT, P], BF16)
        hi_hot = route("hi_hot", [P, 2 * NT, TC], BF16)
        cast_token = route("cast_token", [P, 2 * NT, 2, TC], BF16)
        cast_score = route("cast_score", [P, 2 * NT, 3, TC], BF16)
        score_part = [route(f"score_part{i}", [P, 2 * NT], BF16) for i in range(3)]
        score_left = [route(f"score_left{i}", [P, 2 * NT]) for i in range(2)]
        token_tile = route("token_tile", [P, 2, NT])
        token_row = route("token_row", [P, 1])
        slot_parts = route("slot_parts", [P, 3 * TC])
        slot_row = route("slot_row", [P, TC])
        iota128 = route("iota128", [P, P])
        iota_tc = route("iota_tc", [P, TC])
        down8 = route("down8", [P, E])
        tile_cmp = route("tile_cmp", [P, TC, E])
        tile_e = route("tile_e", [P, TC])
        tile_new = route("tile_new", [P, TC])
        slot_u = small("slot_u", [P, 2 * NT], I32)
        tile_expert = small("tile_expert", [1, TC], I32)
        tile_loads = small("tile_loads", [1, TC], I32)
        tile_next = small("tile_next", [1, TC], I32)
        tile_after = small("tile_after", [1, TC], I32)
        tile_used = small("tile_used", [1, TC], I32)
        slot_token = small("slot_token", [P, TC], I32)
        slot_score = small("slot_score", [P, TC], F32)
        gather_at = [small(f"gather_at{i}", [P, 1], I32) for i in range(2)]
        score_col = small("score_col", [P, 2], F32)
        ones8 = small("ones8", [P, E], F32)

        x_gath = place("x_gath", [P, 2, D], F32, MID + 32 * K)
        xT_hi = place("xT_hi", [P, DC, P], F32R, MID)
        xT_lo = place("xT_lo", [P, DC, P], F32R, MID + 2 * K)
        h_sb = place("h_sb", [P, H], F32, MID + 4 * K)
        hT_hi = place("hT_hi", [P, HC, P], F32R, MID + 8 * K)
        hT_lo = place("hT_lo", [P, HC, P], F32R, MID + 12 * K)
        b1_row = place("b1_row", [P, 2, H], F32, MID + 16 * K)
        b2_row = place("b2_row", [P, 2, D], F32, MID + 24 * K)
        y_sb = place("y_sb", [P, 2, D], F32, MID + 28 * K)
        w_hi = place("w_hi", [P, 2 * WCOLS], F32R, BIG)
        w_lo = place("w_lo", [P, 2 * WCOLS], F32R, BIG + 64 * K)
        y_back = place("y_back", [P, 2 * NT, D], F32, BIG)
        x3_dram = nc.dram_tensor("x3_rows", (T, D), F32, kind="Internal").ap()
        y_dram = nc.dram_tensor("y_slots", (SLOT_TILES * P, D), F32, kind="Internal").ap()

        x_loaded, h_used = [sem("x_loaded0"), sem("x_loaded1")], sem("h_used")
        lens_loaded, ctx_loaded = sem("lens_loaded"), [sem("ctx_loaded0"), sem("ctx_loaded1")]
        w_in_loaded, rows_loaded = sem("w_in_loaded"), sem("rows_loaded")
        consts, consts2 = sem("consts"), sem("consts2")
        vector_step, scalar_step = sem("vector_step"), sem("scalar_step")
        lens_scanned, prefix_done, onehots, hits_done, blocks_ready, rows_counted = (
            sem(n) for n in ("lens_scanned", "prefix_done", "onehots", "hits_done", "blocks_ready", "rows_counted"))
        ctx_summed, ctx_eps, ctx_rooted, patches_ready = (
            sem(n) for n in ("ctx_summed", "ctx_eps", "ctx_rooted", "patches_ready"))
        var_ready, rooted, scales_ready, normed, xb_ready = (
            sem(n) for n in ("var_ready", "rooted", "scales_ready", "normed", "xb_ready"))
        gap_ready, decayed, decay_ready = sem("gap_ready"), sem("decayed"), sem("decay_ready")
        w_in_turned, w_in_ready = sem("w_in_turned"), sem("w_in_ready")
        h_turned, h_copied, embedded, x1_ready = (sem(n) for n in ("h_turned", "h_copied", "embedded", "x1_ready"))
        wq_hi_ready, wq_lo_ready = sem("wq_hi_ready"), sem("wq_lo_ready")
        wq_loaded = [sem(f"wq_loaded{k}") for k in range(DC)]
        w_out_loaded, x2_ready = sem("w_out_loaded"), sem("x2_ready")
        att_var, att_root, att_scale, xn_ready, xn_turned, xnT_hi_ready = (
            sem(n) for n in ("att_var", "att_root", "att_scale", "xn_ready", "xn_turned", "xnT_hi_ready"))
        xnT_lo_ready = sem("xnT_lo_ready")
        qk_summed, qk_hi_ready, qk_lo_ready, qk_stored, v_summed, v_ready, xo_ready = (
            sem(n) for n in ("qk_summed", "qk_hi_ready", "qk_lo_ready", "qk_stored", "v_summed", "v_ready", "xo_ready"))
        qk_stored = [qk_stored, sem("qk_stored1")]
        parts_loaded = [sem(f"parts_loaded{i}") for i in range(4)]
        v_staged, scores_ready, max_ready, exp_done, inv_ready, normalised, turned, probsT_ready, pv_done, oT_ready = (
            sem(n) for n in ("v_staged", "scores_ready", "max_ready", "exp_done", "inv_ready", "normalised",
                             "turned", "probsT_ready", "pv_done", "oT_ready"))
        oT_lo_ready, w_out_hi_ready, w_out_lo_ready = sem("oT_lo_ready"), sem("w_out_hi_ready"), sem("w_out_lo_ready")
        projected, cols_loaded = sem("projected"), sem("cols_loaded")
        max_taken = sem("max_taken")
        out_stored = [sem("out_stored0"), sem("out_stored1")]
        x3_var, x3_root, x3_scale, x3_ready, x3_turned, x3T_ready, gated = (
            sem(n) for n in ("x3_var", "x3_root", "x3_scale", "x3_ready", "x3_turned", "x3T_ready", "gated"))
        x3_stored = [sem("x3_stored0"), sem("x3_stored1")]
        route_consts, gap2_ready, gap2_exp, ranks_asked, ranked, casts_ready, cast_done, tables_ready, routed = (
            sem(n) for n in ("route_consts", "gap2_ready", "gap2_exp", "ranks_asked", "ranked", "casts_ready",
                             "cast_done", "tables_ready", "routed"))
        scores_asked, scores_cast, scored = sem("scores_asked"), sem("scores_cast"), sem("scored")
        raw_loaded, hi_split, lo_split = sem("raw_loaded"), sem("hi_split"), sem("lo_split")
        raw_loaded = [raw_loaded, sem("raw_loaded1")]
        b1_loaded = [sem("b1_loaded0"), sem("b1_loaded1")]
        b2_loaded = [sem("b2_loaded0"), sem("b2_loaded1")]
        picked, gathered = sem("picked"), [sem("gathered0"), sem("gathered1")]
        xg_turned, xT_hi_ready, xT_lo_ready, up_done, h_ready, h_turned2, hT_hi_ready, hT_lo_ready, down_done = (
            sem(n) for n in ("xg_turned", "xT_hi_ready", "xT_lo_ready", "up_done", "h_ready", "h_turned2",
                             "hT_hi_ready", "hT_lo_ready", "down_done"))
        y_added, y_scaled = sem("y_added"), sem("y_scaled")
        y_stored = [sem("y_stored0"), sem("y_stored1")]
        y_fetched = [sem(f"y_fetched{i}") for i in range(NT)]
        gate_loaded, score_picked = sem("gate_loaded"), sem("score_picked")
        down_half = sem("down_half")
        y_first, x_out = sem("y_first"), sem("x_out")

        block = ctx.enter_context(nc.Block())

        class Steps:

            def __init__(self, eng, done):
                self.eng, self.done, self.count = eng, done, 0

            def step(self, ins):
                ins.then_inc(self.done, 1)
                self.count += 1

            def join(self):
                self.eng.wait_ge(self.done, self.count)

            def then(self, ins):
                self.step(ins)
                self.join()

        @block.sync
        def _(sp):
            def w_quarter(e, q):
                if q < 2:
                    return w1[bass.ds(e, 1), q * 2 * P:(q + 1) * 2 * P, :].rearrange("a (k p) n -> p (a k) n", p=P)
                return w2[bass.ds(e, 1), (q - 2) * 4 * P:(q - 1) * 4 * P, :].rearrange("a (k p) n -> p (a k) n", p=P)

            def load_quarter(e, q):
                n = H if q < 2 else D
                sp.dma_start(w_raw[:, q % 2, :].rearrange("p (k n) -> p k n", n=n),
                             w_quarter(e, q)).then_inc(raw_loaded[q % 2], 16)

            lens_v = lens_in.rearrange("b (p j) -> p b j", p=P)
            sp.dma_start(lens_i[:], lens_v).then_inc(lens_loaded, 16)
            for b in range(B):
                sp.dma_start(x_res[:, b * LT:(b + 1) * LT, :], x_rows[:, b * LT:(b + 1) * LT, :]).then_inc(x_loaded[b], 16)
            sp.dma_start(w_in_sb[:], w_in.rearrange("(j p) d -> p j d", p=P)).then_inc(w_in_loaded, 16)
            for b in range(B):
                sp.dma_start(ctx_sb[:, b * LT:(b + 1) * LT, :],
                             ctx_in[b, 0:L, :].rearrange("(k p) d -> p k d", p=P)).then_inc(ctx_loaded[b], 16)
            sp.dma_start(w_out_sb[:], w_out.rearrange("(k p) n -> p k n", p=P)).then_inc(w_out_loaded, 16)
            for k in range(DC):
                sp.dma_start(wq_raw[k][:], w_qkv[k * P:(k + 1) * P, :]).then_inc(wq_loaded[k], 16)
            for u in range(B * 2 * DC):
                b, c = divmod(u, 2 * DC)
                cols = slice(b * AROWS, (b + 1) * AROWS)
                held = Q_PARTS if c < DC else K_PARTS
                for part, src, ready in ((0, qk_hi, qk_hi_ready), (1, qk_lo, qk_lo_ready)):
                    sp.wait_ge(ready, u + 1)
                    for n in range(3):
                        if held[n] == part:
                            sp.dma_start(qk_dram[c, :, n, :, cols], src[:, u % 2, :]).then_inc(qk_stored[u % 2], 16)

            def load_parts(j, r, first=False):
                row0 = (j // 4) * AROWS + ((j // 2) % 2) * STRIDE
                g = 2 * (j % 2) + r // 2
                if not first:
                    sp.wait_ge(scores_ready, 8 * j + 2 * r - 6)
                for tile, c in ((q_parts, g), (k_parts, g + DC)):
                    h = 2 * (r % 2)
                    src = qk_dram[bass.ds(c, 1), h:h + 2, :, :, bass.ds(row0, WIN)]
                    sp.dma_start(tile[:, 2 * r:2 * r + 2, :].bitcast(F32),
                                 src.rearrange("a h x p t -> (x p) (a h) t")).then_inc(parts_loaded[r], 16)

            for parity in range(2):
                sp.wait_ge(qk_stored[parity], 48 * B * DC)
            for r in range(4):
                load_parts(0, r, True)
            for q in range(2):
                sp.wait_ge(wq_lo_ready, DC)
                load_quarter(0, q)
            with sp.Fori(1, 8) as j:
                for r in range(4):
                    load_parts(j, r)
            for i in range(NT):
                sp.wait_ge(x3_ready, i + 1)
                sp.dma_start(x3_dram[i * P:(i + 1) * P, :], x3[:, i % 2, :]).then_inc(x3_stored[i % 2], 16)
                if i in (1, 2, 6, 7):
                    n = (1, 2, 6, 7).index(i)
                    sp.wait_ge(hi_split, n + 1)
                    sp.wait_ge(lo_split, n + 1)
                    load_quarter((n + 2) // WQ, (n + 2) % WQ)

            def load_b1(t, r, first=False):
                e = sp.value_load(tile_expert[0:1, bass.ds(t, 1)], min_val=0, max_val=E - 1)
                if not first:
                    sp.wait_ge(h_ready, t - 1)
                sp.dma_start(b1_row[:, r, :], b1[bass.ds(e, 1), :].rearrange("a n -> (a n)").partition_broadcast(P)
                             ).then_inc(b1_loaded[r], 16)

            def load_b2(t, r, first=False):
                e = sp.value_load(tile_expert[0:1, bass.ds(t, 1)], min_val=0, max_val=E - 1)
                if not first:
                    sp.wait_ge(y_added, t - 1)
                sp.dma_start(b2_row[:, r, :], b2[bass.ds(e, 1), :].rearrange("a n -> (a n)").partition_broadcast(P)
                             ).then_inc(b2_loaded[r], 16)

            def load_next_expert(t):
                load = sp.value_load(tile_loads[0:1, bass.ds(t, 1)], min_val=0, max_val=1)
                e = sp.value_load(tile_next[0:1, bass.ds(t, 1)], min_val=0, max_val=E - 1)
                e_after = sp.value_load(tile_after[0:1, bass.ds(t, 1)], min_val=0, max_val=E - 1)
                sp.wait_ge(hi_split, WQ * t + WQ)
                sp.wait_ge(lo_split, WQ * t + WQ)
                sp.nop(nofuse=True)
                with sp.If(load == 1):
                    for q in range(WQ):
                        sp.wait_ge(hi_split, WQ * t + WQ + q + 1)
                        sp.wait_ge(lo_split, WQ * t + WQ + q + 1)
                        load_quarter(e if q < 2 else e_after, q % 2 + 2 if q < 2 else q - 2)
                with sp.Else():
                    for q in range(2):
                        sp.sem_inc(raw_loaded[q], 32)
                sp.nop(nofuse=True)

            sp.wait_ge(tables_ready, 1)
            for r in range(2):
                sp.wait_ge(x3_stored[r], 16 * NT // 2)
            load_b1(0, 0, True)
            load_b2(0, 0, True)

            def tile(t, r, first=False):
                load_b1(t + 1, 1 - r, first)
                load_next_expert(t)
                load_b2(t + 1, 1 - r, first)

            tile(0, 0, first=True)
            with sp.Fori(0, (SLOT_TILES - 3) // 2) as j:
                for r in (1, 0):
                    tile(2 * j + 2 - r, r)
            tile(SLOT_TILES - 2, 1)
            load_next_expert(SLOT_TILES - 1)
            for q in range(2):
                sp.wait_ge(raw_loaded[q], 32 * SLOT_TILES + 48)
            for i in range(NT):
                sp.wait_ge(x_out, i + 1)
                sp.dma_start(out_rows[:, i, :], x_res[:, i, :]).then_inc(out_stored[i % 2], 16)
            for r in range(2):
                sp.wait_ge(out_stored[r], 16 * NT // 2)

        @block.gpsimd
        def _(pool):
            pool.memset(ident[:], 0.0).then_inc(consts, 1)
            pool.memset(before[:], 1.0).then_inc(consts, 1)
            pool.memset(ones_bf[:], 1.0).then_inc(consts, 1)
            pool.memset(lnb[:], LOGP).then_inc(consts, 1)
            pool.memset(ones_f[:], 1.0).then_inc(consts, 1)
            pool.memset(diag16[:], 0.0).then_inc(consts, 1)
            pool.wait_ge(consts, 6)
            pool.affine_select(out=ident[:], in_=ident[:], compare_op=ALU.not_equal, fill=1.0, base=0,
                               pattern=[[-1, P]], channel_multiplier=1).then_inc(consts2, 1)
            pool.affine_select(out=before[:], in_=before[:], compare_op=ALU.is_gt, fill=0.0, base=0,
                               pattern=[[1, P]], channel_multiplier=-1).then_inc(consts2, 1)
            pool.affine_select(out=diag16[:], in_=diag16[:], compare_op=ALU.not_equal, fill=1.0, base=0,
                               pattern=[[-1, 16]], channel_multiplier=1).then_inc(consts2, 1)
            exact = dict(allow_small_or_imprecise_dtypes=True)
            pool.iota(s_col[:], [[P, LT]], base=0, channel_multiplier=1, **exact).then_inc(consts2, 1)
            pool.iota(iota16[:], [[1, 16]], base=0, channel_multiplier=0, **exact).then_inc(consts2, 1)
            pool.iota(iota32[:], [[1, 32]], base=0, channel_multiplier=0, **exact).then_inc(consts2, 1)
            pool.wait_ge(rows_loaded, 48)
            for n, i in enumerate(ORDER):
                pool.wait_ge(normed, n + 1)
                pool.tensor_tensor(out=x_res[:, i, :], in0=x_res[:, i, :], in1=b_in_row[:], op=ALU.add).then_inc(xb_ready, 1)
            pool.wait_ge(cols_loaded, 48)
            for n, i in enumerate(ORDER):
                pool.wait_ge(x1_ready, n + 1)
                if n < B * AT:
                    pool.wait_ge(xn_ready, n + 1)
                pool.tensor_tensor(out=x_res[:, i, :], in0=x_res[:, i, :], in1=b_out_row[:],
                                   op=ALU.add).then_inc(xo_ready, 1)

            def stage_v(j, r, first=False):
                if not first:
                    pool.wait_ge(pv_done, 8 * j + 4 * r - 4)
                tile = (j // 4) * AT + (j // 2) % 2
                pool.tensor_copy(v_heads[:, r], v_sb[:, bass.ds(tile, 2), bass.ds((2 * (j % 2) + r) * P, P)]
                                 ).then_inc(v_staged, 1)

            def normalise(n, s, first=False):
                pool.wait_ge(inv_ready, n + 1)
                if not first:
                    pool.wait_ge(turned, n - 1)
                pool.tensor_tensor(out=probs_n[:, s % 2], in0=probs[:, s % 4],
                                   in1=prob_inv[:, s % 4].unsqueeze(2).to_broadcast([P, 2, WIN]),
                                   op=ALU.mult).then_inc(normalised, 1)

            def heads(j, first=False, last=False):
                for r in range(8):
                    if r == 1:
                        stage_v(j, 1, first)
                    if r == 5 and not last:
                        stage_v(j + 1, 0)
                    if not (last and r + 2 >= 8):
                        normalise(8 * j + r + 2, r + 2)

            pool.wait_ge(v_ready, B * AT)
            stage_v(0, 0, True)
            normalise(0, 0, True)
            normalise(1, 1, True)
            heads(0, first=True)
            with pool.Fori(1, 7) as j:
                heads(j)
            heads(7, last=True)
            pool.wait_ge(projected, NT)
            pool.memset(down8[:], 0.0).then_inc(route_consts, 1)
            pool.iota(token_tile[:], [[0, 2], [1, NT]], base=0, channel_multiplier=0, **exact).then_inc(route_consts, 1)
            pool.iota(token_row[:], [[1, 1]], base=0, channel_multiplier=1, **exact).then_inc(route_consts, 1)
            pool.iota(iota128[:], [[1, P]], base=0, channel_multiplier=0, **exact).then_inc(route_consts, 1)
            pool.iota(iota_tc[:], [[1, TC]], base=0, channel_multiplier=0, **exact).then_inc(route_consts, 1)
            pool.wait_ge(route_consts, 1)
            pool.iota(down8[:], [[-1, E]], base=E, channel_multiplier=0, **exact).then_inc(route_consts, 1)

            def gather(t, r, first=False):
                if not first:
                    pool.wait_ge(xg_turned, t - 1)
                pool.tensor_copy(gather_at[r][:], slot_token[:, bass.ds(t, 1)]).then_inc(picked, 1)
                pool.wait_ge(picked, t + 1)
                pool.nop(nofuse=True)
                pool.indirect_dma_start(out=x_gath[:, r, :], out_offset=None, in_=x3_dram,
                                        in_offset=bass.IndirectOffsetOnAxis(ap=gather_at[r][:].bitcast(U32), axis=0)
                                        ).then_inc(gathered[r], 16)

            def pick_score(t, r, first=False):
                if not first:
                    pool.wait_ge(y_scaled, t - 1)
                pool.tensor_copy(score_col[:, r:r + 1], slot_score[:, bass.ds(t, 1)]).then_inc(score_picked, 1)

            pool.wait_ge(routed, 1)
            for r in range(2):
                pool.wait_ge(x3_stored[r], 16 * NT // 2)
            gather(0, 0, True)
            gather(1, 1, True)
            pool.wait_ge(scored, 1)
            pick_score(0, 0, True)
            pick_score(1, 1, True)
            gather(2, 0)
            gather(3, 1)
            pick_score(2, 0)
            with pool.Fori(2, (SLOT_TILES - 1) // 2) as j:
                for r in range(2):
                    gather(2 * j + r, r)
                    pick_score(2 * j + r - 1, 1 - r)
            gather(SLOT_TILES - 1, 0)
            for t in range(SLOT_TILES - 2, SLOT_TILES):
                pick_score(t, t % 2)
            pool.wait_ge(y_stored[0], 16 * (SLOT_TILES + 1) // 2)
            pool.wait_ge(y_stored[1], 16 * (SLOT_TILES // 2))
            pool.nop(nofuse=True)
            for i in range(NT):
                for c in range(2):
                    n = c * NT + i
                    pool.indirect_dma_start(out=y_back[:, n, :], out_offset=None, in_=y_dram,
                                            in_offset=bass.IndirectOffsetOnAxis(ap=slot_u[:, n:n + 1].bitcast(U32), axis=0)
                                            ).then_inc(y_fetched[i], 16)

        @block.scalar
        def _(act):
            act.dma_start(b_in_row[:], b_in.partition_broadcast(P)).then_inc(rows_loaded, 16)
            act.dma_start(g_init_row[:], g_init[0:D].partition_broadcast(P)).then_inc(rows_loaded, 16)
            act.dma_start(g_res_col[:], g_res.rearrange("(k p) -> p k", p=P), allow_slow_non_contiguous=True).then_inc(rows_loaded, 16)
            act.dma_start(b_qk_col[:], b_qkv[0:2 * D].rearrange("(k p) -> p k", p=P),
                          allow_slow_non_contiguous=True).then_inc(cols_loaded, 16)
            act.dma_start(w_gate_sb[:], w_gate.rearrange("(k p) e -> p k e", p=P)).then_inc(gate_loaded, 16)
            act.dma_start(b_v_row[:], b_qkv[2 * D:3 * D].partition_broadcast(P)).then_inc(cols_loaded, 16)
            act.dma_start(b_out_row[:], b_out.partition_broadcast(P)).then_inc(cols_loaded, 16)
            act.wait_ge(var_ready, 1)
            act.activation(sd[:], var_eps[:], ACT.Sqrt).then_inc(rooted, 1)
            act.wait_ge(var_ready, 2)
            act.activation(sd[:], var_eps[:], ACT.Sqrt).then_inc(rooted, 1)
            act.wait_ge(scales_ready, 1)

            def norm_row(n):
                if n >= 2:
                    act.wait_ge(h_turned, n - 1)
                i = ORDER[n]
                act.activation(hn[:, n % 2, :], x_res[:, i, :], ACT.Identity, bias=row_shift[:, i:i + 1],
                               scale=row_scale[:, i:i + 1]).then_inc(normed, 1)

            def sum_ctx(n):
                act.wait_ge(ctx_loaded[n // LT], 16)
                if n > 0:
                    act.wait_ge(ctx_summed, n)
                act.activation(squares[:], ctx_sb[:, n, :], ACT.Square, accum_out=ctx_ss[:, n:n + 1]).then_inc(ctx_summed, 1)

            def split_wq(k):
                act.wait_ge(patches_ready, (2, 3, NT, NT)[k])
                act.wait_ge(wq_loaded[k], 16)
                act.activation(wq_hi[:, k, :], wq_raw[k][:], ACT.Copy).then_inc(wq_hi_ready, 1)

            norm_row(0)
            norm_row(1)
            for n in range(B * LT):
                sum_ctx(n)
                if n % 2 == 1:
                    norm_row(2 + n // 2)
            act.wait_ge(ctx_eps, 1)
            act.activation(ctx_sd[:], ctx_rs[:], ACT.Sqrt).then_inc(ctx_rooted, 1)
            for n, i in enumerate(ORDER):
                act.wait_ge(gap_ready, n + 1)
                lo = (i % LT) * P
                act.activation(gap[:, n % 2, lo:], gap[:, n % 2, lo:], ACT.Exp, bias=lnb[:], scale=-DT).then_inc(decayed, 1)
                if n == LT - 1:
                    norm_row(6)
                    norm_row(7)
                if n in (3, 4):
                    split_wq(n - 3)

            def keep_xnT(m):
                act.wait_ge(xn_turned, m + 1)
                act.activation(xnT_hi[:, :, m * P:(m + 1) * P], banks[3 + m % 2][:].rearrange("p (k t) -> p k t", k=DC),
                               ACT.Copy).then_inc(xnT_hi_ready, 1)

            for m in range(B * AT):
                i = ORDER[m]
                act.wait_ge(att_var, m + 1)
                act.activation(sd[:, i:i + 1], var_eps[:, i:i + 1], ACT.Sqrt).then_inc(att_root, 1)
                act.wait_ge(att_scale, m + 1)
                if m >= 2:
                    act.wait_ge(xn_turned, m - 1)
                if m == 0:
                    act.wait_ge(patches_ready, B * LT)
                act.activation(xn[:, m % 2, :], x_res[:, i, :], ACT.Identity, bias=row_shift[:, i:i + 1],
                               scale=rstd[:, i:i + 1]).then_inc(xn_ready, 1)
                if m >= 1:
                    keep_xnT(m - 1)
                if m in (1, 2):
                    split_wq(m + 1)
            keep_xnT(B * AT - 1)
            act.wait_ge(cols_loaded, 48)
            for u in range(B * 2 * DC):
                c = u % (2 * DC)
                act.wait_ge(qk_summed, u + 1)
                if u >= 2:
                    act.wait_ge(qk_stored[u % 2], 48 * (u // 2))
                act.activation(qk_hi[:, u % 2, :].bitcast(F32R), banks[u % 3][:, 0:AROWS], ACT.Identity,
                               bias=b_qk_col[:, c:c + 1]).then_inc(qk_hi_ready, 1)

            def split_hi(base, q, n):
                act.wait_ge(raw_loaded[q % 2], 16 * (2 * n + q // 2) + 16)
                act.activation(w_hi[:, bass.ds(base + q * QCOLS, QCOLS)], w_raw[:, q % 2, :], ACT.Copy).then_inc(hi_split, 1)

            def exponents(n, s, first=False):
                act.wait_ge(max_ready, n + 1)
                if not first:
                    act.wait_ge(normalised, n - 3)
                for q in range(2):
                    last = act.activation(probs[:, s % 4, q], banks[s % 4][:, q * WIN:(q + 1) * WIN], ACT.Exp,
                                          bias=max_bias[:, s % 4, q:q + 1], scale=HD ** -0.5,
                                          accum_out=prob_sum[:, s % 4, q:q + 1])
                last.then_inc(exp_done, 1)

            def keep_heads(it, r):
                act.wait_ge(pv_done, 4 * it + 4)
                act.activation(oT_hi[:, bass.ds(it, 1), :].rearrange("p a t -> p (a t)"), banks[6 + r % 2][:, 0:WIN],
                               ACT.Copy).then_inc(oT_ready, 1)

            def heads(j, first=False, last=False):
                for r in range(8):
                    if not (last and r + 3 >= 8):
                        exponents(8 * j + r + 3, r + 3, first and r + 3 < 4)
                    if r == 4:
                        keep_heads(2 * j, 0)
                    if r == 0 and not first:
                        keep_heads(2 * j - 1, 1)

            act.wait_ge(v_ready, B * AT)
            act.wait_ge(w_out_loaded, 16)
            act.activation(w_out_hi[:], w_out_sb[:], ACT.Copy).then_inc(w_out_hi_ready, 1)
            for n in range(3):
                exponents(n, n, True)
            heads(0, first=True)
            with act.Fori(1, 7) as j:
                heads(j)
            heads(7, last=True)
            keep_heads(15, 1)
            for i in range(NT):
                act.wait_ge(x3_var, i + 1)
                act.activation(sd[:, i:i + 1], var_eps[:, i:i + 1], ACT.Sqrt).then_inc(x3_root, 1)
                act.wait_ge(x3_scale, i + 1)
                if i >= 2:
                    act.wait_ge(x3_turned, i - 1)
                    act.wait_ge(x3_stored[i % 2], 16 * (i // 2))
                act.activation(x3[:, i % 2, :], x_res[:, i, :], ACT.Identity, bias=row_shift[:, i:i + 1],
                               scale=rstd[:, i:i + 1]).then_inc(x3_ready, 1)
                if i in (0, 1, 4, 6):
                    split_hi(0, (0, 1, 4, 6).index(i), 0)

            act.wait_ge(gap2_ready, 1)
            act.activation(exp_gap[:], exp_gap[:], ACT.Exp).then_inc(gap2_exp, 1)

            def take_x(t, r):
                act.wait_ge(xg_turned, t + 1)
                act.activation(xT_hi[:].rearrange("p k t -> p (k t)"), banks[5][:], ACT.Copy).then_inc(xT_hi_ready, 1)

            def take_h(t):
                act.wait_ge(h_turned2, t + 1)
                for a in range(2):
                    last = act.activation(hT_hi[:, 4 * a:4 * a + 4, :].rearrange("p k t -> p (k t)"), banks[2 + a][:],
                                          ACT.Relu)
                last.then_inc(hT_hi_ready, 1)

            def give_y(t, r):
                act.wait_ge(y_added, t + 1)
                act.wait_ge(score_picked, t + 1)
                act.activation(y_sb[:, r, :], y_sb[:, r, :], ACT.Copy, scale=score_col[:, r:r + 1]).then_inc(y_scaled, 1)
                act.wait_ge(y_scaled, t + 1)
                act.dma_start(y_dram[bass.ds(t * P, P), :], y_sb[:, r, :]).then_inc(y_stored[r], 16)

            def tile(t, r, first=False, last=False):
                load = act.value_load(tile_loads[0:1, bass.ds(t, 1)], min_val=0, max_val=1)
                e = act.value_load(tile_next[0:1, bass.ds(t, 1)], min_val=0, max_val=E - 1)

                def work(split_next):
                    split_next(0)
                    split_next(1)
                    if not last:
                        take_x(t + 1, 1 - r)
                    if not first:
                        give_y(t - 1, 1 - r)
                    take_h(t)
                    split_next(2)
                    split_next(3)

                def split(q):
                    if not first:
                        act.wait_ge((up_done, up_done, down_half, down_done)[q], t)
                    split_hi(base, q, t + 1)

                act.wait_ge(hi_split, WQ * t + WQ)
                act.nop(nofuse=True)
                with act.If(load == 1):
                    base = act.snap((e % 2) * WCOLS)
                    work(split)
                with act.Else():
                    act.sem_inc(hi_split, WQ)
                    work(lambda q: None)
                act.nop(nofuse=True)

            take_x(0, 0)
            tile(0, 0, first=True)

            with act.Fori(0, (SLOT_TILES - 3) // 2) as j:
                for r in (1, 0):
                    tile(2 * j + 2 - r, r)
            tile(SLOT_TILES - 2, 1)
            tile(SLOT_TILES - 1, 0, last=True)
            give_y(SLOT_TILES - 1, 0)
            for r in range(2):
                act.wait_ge(y_stored[r], 16 * ((SLOT_TILES + 1 - r) // 2))

        @block.vector
        def _(dve):
            own = Steps(dve, vector_step)
            dve.wait_ge(consts, 6)
            dve.wait_ge(lens_loaded, 16)
            own.then(dve.tensor_copy(lens_f[:], lens_i[:].rearrange("p b j -> p (b j)")))
            for b in range(B):
                dve.tensor_tensor_scan(within[:, b, :], ones_f[:, 0:NJ], lens_f[:, b * NJ:(b + 1) * NJ], 0.0,
                                       ALU.mult, ALU.add).then_inc(lens_scanned, 1)
            for i in range(NT):
                if i % LT == 0:
                    dve.wait_ge(x_loaded[i // LT], 16)
                own.step(dve.bn_stats(bn[:, i, :], x_res[:, i, :]))
            own.join()
            for i in range(NT):
                own.step(dve.bn_aggr(mv[:, i, :], bn[:, i, :]))
            own.join()
            dve.tensor_scalar(var_eps[:], mv[:, :, 1], LN_EPS, None, ALU.add).then_inc(var_ready, 1)
            dve.wait_ge(prefix_done, 1)
            own.then(dve.tensor_copy(prefix[:], banks[0][:, 0:B]))
            for b in range(B):
                own.step(dve.tensor_scalar(bidx[:, b * NJ:(b + 1) * NJ], within[:, b, :], prefix[:, b:b + 1], -1.0,
                                           ALU.add, ALU.add))
            own.join()
            own.then(dve.tensor_scalar(wrap[:], bidx[:], 0.0, float(L), ALU.is_lt, ALU.mult))
            own.then(dve.tensor_tensor(cell[:], bidx[:], wrap[:], ALU.add))
            own.step(dve.tensor_scalar(cell_hi[:], cell[:], 5, None, ALU.arith_shift_right))
            own.step(dve.tensor_scalar(cell_lo[:], cell[:], 31, None, ALU.bitwise_and))
            dve.wait_ge(rooted, 1)
            own.then(dve.reciprocal(rstd[:], sd[:]))
            own.then(dve.tensor_tensor(tmp8[:], rstd[:], rstd[:], ALU.mult))
            own.then(dve.tensor_tensor(tmp8[:], tmp8[:], mv[:, :, 1], ALU.mult))
            dve.tensor_scalar(var_eps[:], tmp8[:], RMS_EPS, None, ALU.add).then_inc(var_ready, 1)
            dve.wait_ge(consts2, 6)
            dve.tensor_tensor(oh_hi[:], cell_hi[:].unsqueeze(2).to_broadcast([P, B * NJ, 16]),
                              iota16[:].unsqueeze(1).to_broadcast([P, B * NJ, 16]), ALU.is_equal).then_inc(onehots, 1)
            dve.wait_ge(rooted, 2)
            own.then(dve.reciprocal(tmp8[:], sd[:]))
            own.then(dve.tensor_tensor(row_scale[:], tmp8[:], rstd[:], ALU.mult))
            dve.scalar_tensor_tensor(row_shift[:], mv[:, :, 0], -1.0, row_scale[:], ALU.mult,
                                     ALU.mult).then_inc(scales_ready, 1)
            dve.wait_ge(rows_loaded, 48)
            for k in range(DC):
                dve.wait_ge(w_in_turned, k + 1)
                dve.tensor_scalar(w_inT[:, k, :], banks[1 + k % 2][:], g_res_col[:, k:k + 1], None,
                                  ALU.mult).then_inc(w_in_ready, 1)

            def copy_hT(n):
                dve.wait_ge(h_turned, n + 1)
                if n >= 2:
                    dve.wait_ge(h_used, n - 1)
                dve.tensor_copy(hT[:, n % 2].rearrange("p k t -> p (k t)"), banks[3 + n % 2][:]).then_inc(h_copied, 1)

            copy_hT(0)
            dve.tensor_tensor(oh_lo[:], cell_lo[:].unsqueeze(2).to_broadcast([P, B * NJ, 32]),
                              iota32[:].unsqueeze(1).to_broadcast([P, B * NJ, 32]), ALU.is_equal).then_inc(onehots, 1)
            copy_hT(1)
            copy_hT(2)
            dve.wait_ge(hits_done, 1)
            own.then(dve.tensor_scalar(hits[:], banks[0][0:16, 64:64 + B * 32].rearrange("p (b c) -> p b c", b=B),
                                       1.0, None, ALU.min))
            for b in range(B):
                dve.tensor_tensor(blocks[:, b], hits[:, b, :].unsqueeze(1).to_broadcast([16, 16, 32]),
                                  diag16[:].unsqueeze(2).to_broadcast([16, 16, 32]), ALU.mult).then_inc(blocks_ready, 1)
            copy_hT(3)
            dve.wait_ge(ctx_summed, B * LT)
            dve.tensor_scalar(ctx_rs[:], ctx_ss[:], 1.0 / DG, RMS_EPS, ALU.mult, ALU.add).then_inc(ctx_eps, 1)
            for b in range(B):
                dve.wait_ge(rows_counted, b + 1)
                own.then(dve.tensor_tensor_scan(plug[:, b, :], ones_f[:], banks[1 + b][:], 0.0, ALU.mult, ALU.add))
                own.then(dve.tensor_scalar(plug[:, b, :], plug[:, b, :], -1.0, 0.0, ALU.add, ALU.max))
            dve.wait_ge(ctx_rooted, 1)
            own.then(dve.reciprocal(ctx_rs[:], ctx_sd[:]))

            copy_hT(4)

            def decay_gap(n):
                b, k = divmod(ORDER[n], LT)
                if n >= 2:
                    dve.wait_ge(decay_ready, n - 1)
                dve.tensor_scalar(gap[:, n % 2, k * P:], plug[:, b, k * P:], s_col[:, k:k + 1], 0.0,
                                  ALU.subtract, ALU.max).then_inc(gap_ready, 1)

            def decay_mask(n):
                b, k = divmod(ORDER[n], LT)
                dve.wait_ge(decayed, n + 1)
                dve.scalar_tensor_tensor(decay[:, ORDER[n], k * P:], plug[:, b, k * P:], s_col[:, k:k + 1],
                                         gap[:, n % 2, k * P:], ALU.is_ge, ALU.mult).then_inc(decay_ready, 1)

            def depool_rows(n):
                if n + 1 < NT:
                    decay_gap(n + 1)
                i = ORDER[n]
                dve.scalar_tensor_tensor(patches[:, i, :], ctx_sb[:, i, 0:D], ctx_rs[:, i:i + 1], g_init_row[:],
                                         ALU.mult, ALU.mult).then_inc(patches_ready, 1)
                decay_mask(n)

            decay_gap(0)
            for n in range(4):
                depool_rows(n)

            def keep_xnT_lo(m):
                dve.wait_ge(xnT_hi_ready, m + 1)
                dve.tensor_tensor(xnT_lo[:, :, m * P:(m + 1) * P], banks[3 + m % 2][:].rearrange("p (k t) -> p k t", k=DC),
                                  xnT_hi[:, :, m * P:(m + 1) * P].bitcast(F32), ALU.subtract).then_inc(xnT_lo_ready, 1)

            def scale_att(m):
                i = ORDER[m]
                dve.wait_ge(att_root, m + 1)
                own.then(dve.reciprocal(rstd[:, i:i + 1], sd[:, i:i + 1]))
                dve.scalar_tensor_tensor(row_shift[:, i:i + 1], mv[:, i, 0:1], -1.0, rstd[:, i:i + 1], ALU.mult,
                                         ALU.mult).then_inc(att_scale, 1)

            SCALED_AFTER = ((), (), (), (0, 1), (2, 3), (4,), (5,), ())
            for n, i in enumerate(ORDER):
                dve.wait_ge(embedded, n + 1)
                dve.wait_ge(xb_ready, n + 1)
                dve.tensor_tensor(x_res[:, i, :], x_res[:, i, :], banks[(5, 6, 7, 0)[n % 4]][:], ALU.add
                                  ).then_inc(x1_ready, 1)
                if n + 5 < NT:
                    copy_hT(n + 5)
                if n + 4 < NT:
                    depool_rows(n + 4)
                if n < B * AT:
                    dve.wait_ge(x1_ready, n + 1)
                    own.then(dve.bn_stats(bn[:, i, :], x_res[:, i, :]))
                    own.then(dve.bn_aggr(mv[:, i, :], bn[:, i, :]))
                    dve.tensor_scalar(var_eps[:, i:i + 1], mv[:, i, 1:2], LN_EPS, None, ALU.add).then_inc(att_var, 1)
                for m in SCALED_AFTER[n]:
                    scale_att(m)
                if n >= 4:
                    keep_xnT_lo(n - 4)
                if n in (1, 2, 4, 5):
                    k = (1, 2, 4, 5).index(n)
                    dve.wait_ge(wq_hi_ready, k + 1)
                    dve.tensor_tensor(wq_lo[:, k, :], wq_raw[k][:], wq_hi[:, k, :].bitcast(F32),
                                      ALU.subtract).then_inc(wq_lo_ready, 1)
            for m in range(NT - 4, B * AT):
                keep_xnT_lo(m)
            dve.wait_ge(cols_loaded, 48)
            for u in range(B * 2 * DC):
                c = u % (2 * DC)
                dve.wait_ge(qk_hi_ready, u + 1)
                if u >= 2:
                    dve.wait_ge(qk_stored[u % 2], 48 * (u // 2))
                dve.scalar_tensor_tensor(qk_lo[:, u % 2, :].bitcast(F32R), banks[u % 3][:, 0:AROWS], b_qk_col[:, c:c + 1],
                                         qk_hi[:, u % 2, :], ALU.add, ALU.subtract).then_inc(qk_lo_ready, 1)
            for m in range(B * AT):
                dve.wait_ge(v_summed, m + 1)
                dve.tensor_tensor(v_sb[:, m, :], banks[5 + m % 2][:], b_v_row[:], ALU.add).then_inc(v_ready, 1)

            def split_lo(base, q, n):
                dve.wait_ge(raw_loaded[q % 2], 16 * (2 * n + q // 2) + 16)
                dve.wait_ge(hi_split, WQ * n + q + 1)
                dve.tensor_tensor(w_lo[:, bass.ds(base + q * QCOLS, QCOLS)], w_raw[:, q % 2, :],
                                  w_hi[:, bass.ds(base + q * QCOLS, QCOLS)].bitcast(F32), ALU.subtract).then_inc(lo_split, 1)

            def maxima(n, s):
                dve.wait_ge(scores_ready, n + 1)
                dve.tensor_reduce(neg_max[:, s % 4, :], banks[s % 4][:].rearrange("p (q k) -> p q k", q=2),
                                  AX.X, ALU.max, negate=True).then_inc(max_taken, 1)
                dve.wait_ge(max_taken, n + 1)
                dve.tensor_scalar(max_bias[:, s % 4, :], neg_max[:, s % 4, :], HD ** -0.5, None,
                                  ALU.mult).then_inc(max_ready, 1)

            def inverse(n, s, first=False):
                dve.wait_ge(exp_done, n + 1)
                if not first:
                    dve.wait_ge(normalised, n - 3)
                dve.reciprocal(prob_inv[:, s % 4, :], prob_sum[:, s % 4, :]).then_inc(inv_ready, 1)

            def copy_probsT(n, s, first=False):
                dve.wait_ge(turned, n + 1)
                if not first:
                    dve.wait_ge(pv_done, n - 1)
                dve.tensor_copy(probsT[:, s % 2].rearrange("p a q -> p (a q)"), banks[4 + s % 2][:]).then_inc(probsT_ready, 1)

            def heads(j, first=False, last=False):
                for r in range(8):
                    if not (last and r + 3 >= 8):
                        maxima(8 * j + r + 3, r + 3)
                    if not (last and r + 2 >= 8):
                        inverse(8 * j + r + 2, r + 2, first and r + 2 < 4)
                    copy_probsT(8 * j + r, r, first and r < 2)
                    if r == 5:
                        keep_heads_lo(2 * j, 0)
                    if r == 1 and not first:
                        keep_heads_lo(2 * j - 1, 1)

            def keep_heads_lo(it, r):
                dve.wait_ge(oT_ready, it + 1)
                dve.tensor_tensor(oT_lo[:, bass.ds(it, 1), :].rearrange("p a t -> p (a t)"), banks[6 + r][:, 0:WIN],
                                  oT_hi[:, bass.ds(it, 1), :].rearrange("p a t -> p (a t)").bitcast(F32),
                                  ALU.subtract).then_inc(oT_lo_ready, 1)

            dve.wait_ge(w_out_hi_ready, 1)
            dve.tensor_tensor(w_out_lo[:], w_out_sb[:], w_out_hi[:].bitcast(F32),
                              ALU.subtract).then_inc(w_out_lo_ready, 1)
            for n in range(3):
                maxima(n, n)
            inverse(0, 0, True)
            inverse(1, 1, True)
            heads(0, first=True)
            with dve.Fori(1, 7) as j:
                heads(j)
            heads(7, last=True)
            keep_heads_lo(15, 1)
            def copy_x3T(i):
                dve.wait_ge(x3_turned, i + 1)
                if i >= 2:
                    dve.wait_ge(gated, i - 1)
                dve.tensor_copy(x3T[:, i % 2].rearrange("p k t -> p (k t)"), banks[3 + i % 2][:]).then_inc(x3T_ready, 1)

            own.step(dve.memset(ones8[:], 1.0))
            for i in range(NT):
                dve.wait_ge(projected, i + 1)
                dve.wait_ge(xo_ready, NT)
                dve.tensor_tensor(x_res[:, i, :], x_res[:, i, :], banks[i % 3][:], ALU.add).then_inc(x2_ready, 1)
                dve.wait_ge(x2_ready, i + 1)
                own.then(dve.bn_stats(bn[:, i, :], x_res[:, i, :]))
                own.then(dve.bn_aggr(mv[:, i, :], bn[:, i, :]))
                dve.tensor_scalar(var_eps[:, i:i + 1], mv[:, i, 1:2], LN_EPS, None, ALU.add).then_inc(x3_var, 1)
                dve.wait_ge(x3_root, i + 1)
                own.then(dve.reciprocal(rstd[:, i:i + 1], sd[:, i:i + 1]))
                dve.scalar_tensor_tensor(row_shift[:, i:i + 1], mv[:, i, 0:1], -1.0, rstd[:, i:i + 1], ALU.mult,
                                         ALU.mult).then_inc(x3_scale, 1)
                if i >= 1:
                    copy_x3T(i - 1)
                if i in (1, 2, 5, 7):
                    split_lo(0, (1, 2, 5, 7).index(i), 0)
            copy_x3T(NT - 1)
            dve.wait_ge(gated, NT)
            dve.wait_ge(route_consts, 6)
            own.then(dve.tensor_copy(logit[:].rearrange("p i e -> p (i e)"), banks[5][:, 0:NT * E]))

            def over_e(row):
                return row.unsqueeze(2).to_broadcast([P, NT, E])

            down = down8[:].unsqueeze(1).to_broadcast([P, NT, E])
            for c in range(2):
                own.then(dve.tensor_reduce(top[c][:], logit[:], AX.X, ALU.max))
                own.then(dve.tensor_tensor(eq[:], logit[:], over_e(top[c][:]), ALU.is_equal))
                own.then(dve.tensor_tensor(eq[:], eq[:], down, ALU.mult))
                own.then(dve.tensor_reduce(rank_key[:], eq[:], AX.X, ALU.max))
                own.then(dve.tensor_tensor(pick[:, c], down, over_e(rank_key[:]), ALU.is_equal))
                if c == 0:
                    own.then(dve.scalar_tensor_tensor(logit[:], pick[:, 0], -1e30, logit[:], ALU.mult, ALU.add))
            dve.tensor_tensor(exp_gap[:], top[1][:], top[0][:], ALU.subtract).then_inc(gap2_ready, 1)
            own.step(dve.tensor_copy(before_bf[:], before[:]))
            own.step(dve.memset(earlier[:, 0, :], 0.0))
            own.then(dve.tensor_tensor(chosen[:], pick[:, 0], pick[:, 1], ALU.add))
            for i in range(NT):
                own.then(dve.tensor_tensor(earlier[:, i + 1, :], earlier[:, i, :], chosen[:, i, :], ALU.add))
            dve.sem_inc(ranks_asked, 1)

            dve.wait_ge(gap2_exp, 1)
            own.then(dve.tensor_scalar(denom[:], exp_gap[:], 1.0, None, ALU.add))
            own.then(dve.reciprocal(score[:, 0, :], denom[:]))
            own.then(dve.tensor_tensor(score[:, 1, :], score[:, 0, :], exp_gap[:], ALU.mult))
            dve.wait_ge(ranked, 1)
            own.then(dve.tensor_copy(rank_sb[:].rearrange("p i e -> p (i e)"), banks[7][:, 0:(NT + 1) * E]))
            own.then(dve.tensor_scalar(count_i[:], rank_sb[:, NT, :], float(P - 1), None, ALU.add))
            own.then(dve.tensor_scalar(count_i[:], count_i[:], 7, None, ALU.arith_shift_right))
            own.then(dve.tensor_scalar(tiles_of[:], count_i[:], 1.0, None, ALU.max))
            own.then(dve.tensor_tensor_scan(tiles_end[:], ones8[:], tiles_of[:], 0.0, ALU.mult, ALU.add))
            own.then(dve.tensor_tensor(slot_base[:], tiles_end[:], tiles_of[:], ALU.subtract))
            own.then(dve.scalar_tensor_tensor(slot_all[:], slot_base[:].unsqueeze(1).to_broadcast([P, NT, E]), float(P),
                                              rank_sb[:, 0:NT, :], ALU.mult, ALU.add))
            for c in range(2):
                own.step(dve.tensor_tensor(slot_pick[:, c], slot_all[:], pick[:, c], ALU.mult))
            own.join()
            own.then(dve.tensor_reduce(slot_f[:], slot_pick[:], AX.X, ALU.add))
            own.then(dve.tensor_copy(slot_u[:], slot_f[:].rearrange("p c i -> p (c i)")))
            own.step(dve.tensor_scalar(slot_hi[:], slot_u[:], 7, None, ALU.arith_shift_right))
            own.step(dve.tensor_scalar(slot_lo[:], slot_u[:], P - 1, None, ALU.bitwise_and))
            own.join()
            own.step(dve.tensor_tensor(hi_hot[:], slot_hi[:].unsqueeze(2).to_broadcast([P, 2 * NT, TC]),
                                       iota_tc[:].unsqueeze(1).to_broadcast([P, 2 * NT, TC]), ALU.is_equal))
            own.then(dve.tensor_tensor(lo_hot[:], slot_lo[:].unsqueeze(2).to_broadcast([P, 2 * NT, P]),
                                       iota128[:].unsqueeze(1).to_broadcast([P, 2 * NT, P]), ALU.is_equal))
            own.step(dve.tensor_tensor(cast_token[:, :, 0, :], hi_hot[:],
                                       token_tile[:].rearrange("p c i -> p (c i)").unsqueeze(2).to_broadcast([P, 2 * NT, TC]),
                                       ALU.mult))
            own.step(dve.tensor_scalar(cast_token[:, :, 1, :], hi_hot[:], token_row[:, 0:1], None, ALU.mult))
            own.join()
            dve.sem_inc(casts_ready, 1)
            own.then(dve.tensor_tensor(tile_cmp[:], iota_tc[:].unsqueeze(2).to_broadcast([P, TC, E]),
                                       tiles_end[:].unsqueeze(1).to_broadcast([P, TC, E]), ALU.is_ge))
            own.then(dve.tensor_reduce(tile_e[:], tile_cmp[:], AX.X, ALU.add))
            dve.wait_ge(cast_done, 1)
            own.then(dve.tensor_copy(slot_row[:], banks[6][:, TC:2 * TC]))
            dve.scalar_tensor_tensor(slot_token[:], banks[6][:, 0:TC], float(P), slot_row[:], ALU.mult,
                                     ALU.add).then_inc(routed, 1)
            own.then(dve.tensor_scalar(tile_used[:], tile_e[0:1, :], float(E), None, ALU.is_lt))
            own.step(dve.memset(tile_new[:], 1.0))
            own.then(dve.tensor_scalar(tile_e[:], tile_e[:], float(E - 1), None, ALU.min))
            own.step(dve.tensor_copy(tile_expert[:], tile_e[0:1, :]))
            own.then(dve.tensor_tensor(tile_new[:, 1:], tile_e[:, 1:], tile_e[:, :-1], ALU.is_gt))
            own.then(dve.scalar_tensor_tensor(tile_loads[:], tile_e[0:1, :], float(E - 1), tile_new[0:1, :], ALU.is_lt,
                                              ALU.mult))
            own.step(dve.tensor_scalar(tile_next[:], tile_e[0:1, :], 1.0, float(E - 1), ALU.add, ALU.min))
            own.then(dve.tensor_scalar(tile_after[:], tile_e[0:1, :], 2.0, float(E - 1), ALU.add, ALU.min))
            dve.sem_inc(tables_ready, 1)
            left = score[:].rearrange("p c i -> p (c i)")
            for n in range(3):
                own.then(dve.tensor_copy(score_part[n][:], left))
                if n < 2:
                    own.then(dve.tensor_tensor(score_left[n][:], left, score_part[n][:], ALU.subtract))
                    left = score_left[n][:]
            for n in range(3):
                own.step(dve.tensor_tensor(cast_score[:, :, n, :], hi_hot[:],
                                           score_part[n][:].unsqueeze(2).to_broadcast([P, 2 * NT, TC]), ALU.mult))
            own.join()
            dve.sem_inc(scores_asked, 1)
            dve.wait_ge(scores_cast, 1)
            own.then(dve.tensor_copy(slot_parts[:], banks[7][:, 0:3 * TC]))
            own.then(dve.tensor_tensor(slot_parts[:, TC:2 * TC], slot_parts[:, TC:2 * TC], slot_parts[:, 2 * TC:], ALU.add))
            dve.tensor_tensor(slot_score[:], slot_parts[:, 0:TC], slot_parts[:, TC:2 * TC], ALU.add).then_inc(scored, 1)

            def take_x(t):
                dve.wait_ge(xT_hi_ready, t + 1)
                dve.tensor_tensor(xT_lo[:].rearrange("p k t -> p (k t)"), banks[5][:],
                                  xT_hi[:].rearrange("p k t -> p (k t)").bitcast(F32), ALU.subtract).then_inc(xT_lo_ready, 1)

            def take_h(t, r):
                dve.wait_ge(up_done, t + 1)
                dve.wait_ge(b1_loaded[r], 16 * (t // 2) + 16)
                for a in range(2):
                    last = dve.tensor_tensor(h_sb[:, a * 512:(a + 1) * 512], banks[a][:],
                                             b1_row[:, r, a * 512:(a + 1) * 512], ALU.add)
                last.then_inc(h_ready, 1)

            def take_hT(t):
                dve.wait_ge(hT_hi_ready, t + 1)
                for a in range(2):
                    last = dve.scalar_tensor_tensor(hT_lo[:, 4 * a:4 * a + 4, :].rearrange("p k t -> p (k t)"),
                                                    banks[2 + a][:], 0.0,
                                                    hT_hi[:, 4 * a:4 * a + 4, :].rearrange("p k t -> p (k t)").bitcast(F32),
                                                    ALU.max, ALU.subtract)
                last.then_inc(hT_lo_ready, 1)

            def take_y(t, r, first=False):
                dve.wait_ge(down_done, t + 1)
                dve.wait_ge(b2_loaded[r], 16 * (t // 2) + 16)
                if not first:
                    dve.wait_ge(y_stored[r], 16 * (t // 2))
                dve.tensor_tensor(y_sb[:, r, :], banks[4][:], b2_row[:, r, :], ALU.add).then_inc(y_added, 1)

            def tile(t, r, first=False, last=False, begin=False):
                load = dve.value_load(tile_loads[0:1, bass.ds(t, 1)], min_val=0, max_val=1)
                e = dve.value_load(tile_next[0:1, bass.ds(t, 1)], min_val=0, max_val=E - 1)

                def work(split_next):
                    split_next(0)
                    take_h(t, r)
                    if not last:
                        take_x(t + 1)
                    split_next(1)
                    if not begin:
                        take_y(t - 1, 1 - r, first)
                    take_hT(t)
                    split_next(2)
                    split_next(3)

                def split(q):
                    if not begin:
                        dve.wait_ge((up_done, up_done, down_half, down_done)[q], t)
                    split_lo(base, q, t + 1)

                dve.wait_ge(lo_split, WQ * t + WQ)
                dve.nop(nofuse=True)
                with dve.If(load == 1):
                    base = dve.snap((e % 2) * WCOLS)
                    work(split)
                with dve.Else():
                    dve.sem_inc(lo_split, WQ)
                    work(lambda q: None)
                dve.nop(nofuse=True)

            take_x(0)
            tile(0, 0, begin=True)

            tile(1, 1, first=True)
            tile(2, 0, first=True)
            with dve.Fori(1, (SLOT_TILES - 3) // 2) as j:
                for r in (1, 0):
                    tile(2 * j + 2 - r, r)
            tile(SLOT_TILES - 2, 1)
            tile(SLOT_TILES - 1, 0, last=True)
            take_y(SLOT_TILES - 1, 0)
            for i in range(NT):
                dve.wait_ge(y_fetched[i], 32)
                dve.tensor_tensor(x_res[:, i, :], x_res[:, i, :], y_back[:, i, :], ALU.add).then_inc(y_first, 1)
                dve.wait_ge(y_first, i + 1)
                dve.tensor_tensor(x_res[:, i, :], x_res[:, i, :], y_back[:, NT + i, :], ALU.add).then_inc(x_out, 1)

        @block.tensor
        def _(pe):
            pe.wait_ge(consts2, 6)
            pe.wait_ge(lens_scanned, 2)
            pe.matmul(banks[0][:, 0:B], before[:], within[:, :, NJ - 1], start=True, stop=True).then_inc(prefix_done, 1)
            pe.wait_ge(w_in_loaded, 16)
            for k in range(DC):
                if k >= 2:
                    pe.wait_ge(w_in_ready, k - 1)
                for j in range(DC):
                    last = pe.transpose(banks[1 + k % 2][:, j * P:(j + 1) * P], w_in_sb[:, j, k * P:(k + 1) * P], ident[:])
                last.then_inc(w_in_turned, 1)

            def turn_h(n):
                pe.wait_ge(normed, n + 1)
                if n >= 2:
                    pe.wait_ge(h_copied, n - 1)
                for k in range(DC):
                    last = pe.transpose(banks[3 + n % 2][:, k * P:(k + 1) * P], hn[:, n % 2, k * P:(k + 1) * P], ident[:])
                last.then_inc(h_turned, 1)

            def embed(n):
                pe.wait_ge(h_copied, n + 1)
                if n >= 4:
                    pe.wait_ge(x1_ready, n - 3)
                for k in range(DC):
                    last = pe.matmul(banks[(5, 6, 7, 0)[n % 4]][:], hT[:, n % 2, k, :], w_inT[:, k, :], start=(k == 0),
                                     stop=False)
                last.then_inc(h_used, 1)

            def depool(n):
                b, li = divmod(ORDER[n], LT)
                for k in range(li + 1):
                    if li == k:
                        pe.wait_ge(patches_ready, n + 1)
                        pe.wait_ge(decay_ready, n + 1)
                    last = pe.matmul(banks[(5, 6, 7, 0)[n % 4]][:], decay[:, b * LT + k, li * P:(li + 1) * P],
                                     patches[:, b * LT + k, :], start=False, stop=(k == li))
                last.then_inc(embedded, 1)

            def turn_xn(m):
                pe.wait_ge(xn_ready, m + 1)
                if m >= 2:
                    pe.wait_ge(xnT_lo_ready, m - 1)
                else:
                    pe.wait_ge(h_copied, NT - 1 + m)
                for k in range(DC):
                    last = pe.transpose(banks[3 + m % 2][:, k * P:(k + 1) * P], xn[:, m % 2, k * P:(k + 1) * P], ident[:])
                last.then_inc(xn_turned, 1)

            turn_h(0)
            turn_h(1)
            pe.wait_ge(w_in_ready, DC)
            embed(0)
            turn_h(2)
            embed(1)
            turn_h(3)
            pe.wait_ge(onehots, 2)
            for b in range(B):
                for j in range(NJ):
                    n = b * NJ + j
                    last = pe.matmul(banks[0][0:16, 64 + b * 32:96 + b * 32], oh_hi[:, n, :], oh_lo[:, n, :],
                                     start=(j == 0), stop=(j == NJ - 1))
            last.then_inc(hits_done, 1)
            embed(2)
            for b in range(B):
                pe.wait_ge(blocks_ready, b + 1)
                pe.matmul(banks[1 + b][:], ones_bf[0:16, :], blocks[:, b].rearrange("p a c -> p (a c)"),
                          start=True, stop=True).then_inc(rows_counted, 1)
            turn_h(4)
            embed(3)
            turn_h(5)
            for n in range(NT):
                depool(n)
                if n >= 1 and n + 3 < NT:
                    embed(n + 3)
                    if n + 5 < NT:
                        turn_h(n + 5)
                if n >= 3:
                    turn_xn(n - 3)
            for m in range(NT - 3, B * AT):
                turn_xn(m)
            pe.wait_ge(wq_lo_ready, DC)
            pe.wait_ge(xnT_lo_ready, B * AT)
            pe.wait_ge(x1_ready, NT)
            part_pairs = ((wq_hi, xnT_hi), (wq_hi, xnT_lo), (wq_lo, xnT_hi))
            for u in range(B * 2 * DC):
                b, c = divmod(u, 2 * DC)
                if u >= 3:
                    pe.wait_ge(qk_lo_ready, u - 2)
                for k in range(DC):
                    for n, (w, xt) in enumerate(part_pairs):
                        last = pe.matmul(banks[u % 3][:, 0:AROWS], w[:, k, c * P:(c + 1) * P],
                                         xt[:, k, b * AROWS:(b + 1) * AROWS], start=(k == 0 and n == 0),
                                         stop=(k == DC - 1 and n == 2))
                last.then_inc(qk_summed, 1)
            for m in range(B * AT):
                if m >= 2:
                    pe.wait_ge(v_ready, m - 1)
                for k in range(DC):
                    for n, (w, xt) in enumerate(part_pairs):
                        last = pe.matmul(banks[5 + m % 2][:], xt[:, k, m * P:(m + 1) * P], w[:, k, 2 * D:3 * D],
                                         start=(k == 0 and n == 0), stop=(k == DC - 1 and n == 2))
                last.then_inc(v_summed, 1)

            def scores(n, s, j, first=False):
                if s % 2 == 0:
                    pe.wait_ge(parts_loaded[s // 2 % 4], 32 * j + 32)
                if not first:
                    pe.wait_ge(exp_done, n - 3)
                for q in range(2):
                    last = pe.matmul(banks[s % 4][:, q * WIN:(q + 1) * WIN], q_parts[:, s % 8, q * P:(q + 1) * P],
                                     k_parts[:, s % 8, :], start=True, stop=True)
                last.then_inc(scores_ready, 1)

            def turn_probs(n, s, first=False):
                pe.wait_ge(normalised, n + 1)
                if not first:
                    pe.wait_ge(probsT_ready, n - 1)
                for a in range(2):
                    for q in range(2):
                        last = pe.transpose(banks[4 + s % 2][:, (2 * a + q) * P:(2 * a + q + 1) * P],
                                            probs_n[:, s % 2, q, a * P:(a + 1) * P], ident[:])
                last.then_inc(turned, 1)

            def weigh(n, s, it, first=False):
                r, h = s // 4 % 2, s % 4
                pe.wait_ge(probsT_ready, n + 1)
                if h == 0:
                    pe.wait_ge(v_staged, it + 1)
                    if not first:
                        pe.wait_ge(oT_lo_ready, it - 1)
                for a in range(2):
                    last = pe.matmul(banks[6 + r][h * HD:(h + 1) * HD, 0:WIN], v_heads[:, r, a, h * HD:(h + 1) * HD],
                                     probsT[:, s % 2, a, :], start=(a == 0), stop=(a == 1))
                last.then_inc(pv_done, 1)

            def heads(j, first=False, last=False):
                for r in range(8):
                    if not (last and r + 3 >= 8):
                        scores(8 * j + r + 3, r + 3, j + (r + 3) // 8, first and r + 3 < 4)
                    turn_probs(8 * j + r, r, first and r < 2)
                    if not (first and r == 0):
                        weigh(8 * j + r - 1, (r - 1) % 8, 2 * j + (r - 1) // 4, first)

            pe.wait_ge(qk_lo_ready, B * 2 * DC)
            pe.wait_ge(v_ready, B * AT)
            for n in range(3):
                scores(n, n, 0, True)
            heads(0, first=True)
            with pe.Fori(1, 7) as j:
                heads(j)
            heads(7, last=True)
            weigh(63, 7, 15)
            def turn_x3(i):
                pe.wait_ge(x3_ready, i + 1)
                if i >= 2:
                    pe.wait_ge(x3T_ready, i - 1)
                for k in range(DC):
                    last = pe.transpose(banks[3 + i % 2][:, k * P:(k + 1) * P], x3[:, i % 2, k * P:(k + 1) * P], ident[:])
                last.then_inc(x3_turned, 1)

            pe.wait_ge(gate_loaded, 16)

            def gate(i):
                pe.wait_ge(x3T_ready, i + 1)
                for k in range(DC):
                    last = pe.matmul(banks[5][:, i * E:(i + 1) * E], x3T[:, i % 2, k, :], w_gate_sb[:, k, :],
                                     start=(k == 0), stop=(k == DC - 1))
                last.then_inc(gated, 1)

            pe.wait_ge(w_out_lo_ready, 1)
            for i in range(NT):
                w, q = divmod(i, 2)
                pe.wait_ge(oT_lo_ready, 4 * w + 4)
                if i >= 3:
                    pe.wait_ge(x2_ready, i - 2)
                for g in range(4):
                    for n, (o, wo) in enumerate(((oT_hi, w_out_hi[:, g, :]), (oT_hi, w_out_lo[:, g, :]),
                                                 (oT_lo, w_out_hi[:, g, :]))):
                        last = pe.matmul(banks[i % 3][:], o[:, 4 * w + g, q * P:(q + 1) * P], wo,
                                         start=(g == 0 and n == 0), stop=(g == 3 and n == 2))
                last.then_inc(projected, 1)
                if i >= 2:
                    turn_x3(i - 2)
                if i >= 3:
                    gate(i - 3)
            for i in range(NT, NT + 3):
                if i < NT + 2:
                    turn_x3(i - 2)
                gate(i - 3)
            pe.wait_ge(ranks_asked, 1)
            pe.matmul(banks[7][:, 0:(NT + 1) * E], ones_bf[:], earlier[:].rearrange("p i e -> p (i e)"), start=True,
                      stop=False)
            pe.matmul(banks[7][:, 0:NT * E], before_bf[:], chosen[:].rearrange("p i e -> p (i e)"), start=False,
                      stop=True).then_inc(ranked, 1)
            pe.wait_ge(casts_ready, 1)
            for n in range(2 * NT):
                last = pe.matmul(banks[6][:, 0:2 * TC], lo_hot[:, n, :], cast_token[:, n].rearrange("p a t -> p (a t)"),
                                 start=(n == 0), stop=(n == 2 * NT - 1))
            last.then_inc(cast_done, 1)

            def cast_scores():
                pe.wait_ge(scores_asked, 1)
                for n in range(2 * NT):
                    last = pe.matmul(banks[7][:, 0:3 * TC], lo_hot[:, n, :], cast_score[:, n].rearrange("p a t -> p (a t)"),
                                     start=(n == 0), stop=(n == 2 * NT - 1))
                last.then_inc(scores_cast, 1)

            def turn_x(t, r, first=False):
                pe.wait_ge(gathered[r], 16 * (t // 2) + 16)
                if not first:
                    pe.wait_ge(xT_lo_ready, t)
                for k in range(DC):
                    last = pe.transpose(banks[5][:, k * P:(k + 1) * P], x_gath[:, r, k * P:(k + 1) * P], ident[:])
                last.then_inc(xg_turned, 1)

            def is_used(t):
                return pe.value_load(tile_used[0:1, bass.ds(t, 1)], min_val=0, max_val=1)

            def when_used(t, used, done, products, skipped):
                pe.wait_ge(done, t)
                pe.nop(nofuse=True)
                with pe.If(used == 1):
                    products()
                with pe.Else():
                    for count in skipped:
                        pe.sem_inc(count, 1)
                pe.nop(nofuse=True)

            def up(t, first=False, spare=False):
                used = is_used(t) if spare else None
                s = 0 if first else half_of(t)
                pe.wait_ge(xT_lo_ready, t + 1)
                if not first:
                    pe.wait_ge(h_ready, t)

                def products():
                    for k in range(DC):
                        if k % 2 == 0:
                            pe.wait_ge(hi_split, WQ * t + 1 + k // 2)
                            pe.wait_ge(lo_split, WQ * t + 1 + k // 2)
                        for x_part, w_parts in ((xT_hi, (w_hi, w_lo)), (xT_lo, (w_hi,))):
                            for a in range(2):
                                for w in w_parts:
                                    last = pe.matmul(banks[a][:], x_part[:, k, :],
                                                     w[:, bass.ds(s + k * H + a * 512, 512)],
                                                     start=(k == 0 and x_part is xT_hi and w is w_hi),
                                                     stop=(k == DC - 1 and x_part is xT_lo))
                    last.then_inc(up_done, 1)

                if spare:
                    when_used(t, used, up_done, products, (up_done,))
                else:
                    products()

            def down(t, first=False, spare=False):
                used = is_used(t) if spare else None
                s = half_of(t)
                pe.wait_ge(hT_lo_ready, t + 1)
                if not first:
                    pe.wait_ge(y_added, t)

                def products():
                    for k in range(HC):
                        if k % 4 == 0:
                            pe.wait_ge(hi_split, WQ * t + 3 + k // 4)
                            pe.wait_ge(lo_split, WQ * t + 3 + k // 4)
                        for h_part, w_parts in ((hT_hi, (w_hi, w_lo)), (hT_lo, (w_hi,))):
                            for w in w_parts:
                                last = pe.matmul(banks[4][:], h_part[:, k, :], w[:, bass.ds(s + DC * H + k * D, D)],
                                                 start=(k == 0 and h_part is hT_hi and w is w_hi),
                                                 stop=(k == HC - 1 and h_part is hT_lo))
                        if k == HC // 2 - 1:
                            last.then_inc(down_half, 1)
                    last.then_inc(down_done, 1)

                if spare:
                    when_used(t, used, down_done, products, (down_half, down_done))
                else:
                    products()

            def turn_hidden(t, first=False):
                pe.wait_ge(h_ready, t + 1)
                if not first:
                    pe.wait_ge(hT_lo_ready, t)
                for k in range(HC):
                    last = pe.transpose(banks[2 + k // 4][:, k % 4 * P:(k % 4 + 1) * P], h_sb[:, k * P:(k + 1) * P], ident[:])
                last.then_inc(h_turned2, 1)

            def half_of(t):
                e = pe.value_load(tile_expert[0:1, bass.ds(t, 1)], min_val=0, max_val=E - 1)
                return pe.snap((e % 2) * WCOLS)

            def tile(t, r, first=False, last=False, spare=False):
                up(t, spare=spare)
                if not last:
                    turn_x(t + 1, 1 - r)
                down(t - 1, first, spare)
                turn_hidden(t)

            pe.wait_ge(tables_ready, 1)
            cast_scores()
            turn_x(0, 0, True)
            up(0, True)
            turn_x(1, 1)
            turn_hidden(0, True)
            tile(1, 1, first=True)
            tile(2, 0)
            with pe.Fori(1, FULL_TILES // 2 - 1) as j:
                for r in (1, 0):
                    tile(2 * j + 2 - r, r)
            with pe.Fori(FULL_TILES // 2 - 1, (SLOT_TILES - 3) // 2) as j:
                for r in (1, 0):
                    tile(2 * j + 2 - r, r, spare=True)
            tile(SLOT_TILES - 2, 1, spare=True)
            tile(SLOT_TILES - 1, 0, last=True, spare=True)
            down(SLOT_TILES - 1, spare=True)

    return nc


_INS = ['x', 'ctx_2048', 'mask_BxS2_if0', 'L0_xattn_W_in', 'L0_xattn_b_in', 'L0_xattn_g_res', 'L0_xattn_g_init',
        'L0_attn_w_qkv', 'L0_attn_b_qkv', 'L0_attn_w_out', 'L0_attn_b_out', 'L0_ffn_Wg', 'L0_ffn_W1', 'L0_ffn_b1',
        'L0_ffn_W2', 'L0_ffn_b2']


def kernel(**inputs):
    import numpy as _np
    import concourse.bacc as _bacc
    from concourse import mybir as _mybir
    from concourse.bass_utils import run_bass_kernel_spmd as _run

    nc = _bacc.Bacc("TRN2", target_bir_lowering=False, num_devices=1)
    arrays, args = {}, []
    for name in _INS:
        a = _np.ascontiguousarray(inputs[name])
        arrays[f"in_{name}_dram"] = a
        args.append(nc.dram_tensor(f"in_{name}_dram", a.shape, _mybir.dt.from_np(a.dtype), kind="ExternalInput").ap())
    args.append(nc.dram_tensor("out_0_dram", (B, L, D), _mybir.dt.float32, kind="ExternalOutput").ap())
    perceiver_layer(nc, *args)
    r = _run(nc, [arrays], core_ids=[0])
    return r.results[0]["out_0_dram"]
```

```python
import math
from contextlib import ExitStack

import concourse.bass as bass
from concourse import mybir

F32 = mybir.dt.float32
F32R = mybir.dt.float32r
BF16 = mybir.dt.bfloat16
I32 = mybir.dt.int32
U32 = mybir.dt.uint32
ALU = mybir.AluOpType
ACT = mybir.ActivationFunctionType
AX = mybir.AxisListType

P = 128
B, L, D = 2, 512, 512
T = B * L
NT = T // P
LT = L // P
DC = D // P
DG = 1024
NLEN = 8192
NJ = NLEN // P
HEADS, HD = D // 32, 32
WIN, STRIDE = 256, 128
NWIN = 2
AROWS = STRIDE * (NWIN - 1) + WIN
AT = AROWS // P
ORDER = [b * (L // P) + i for b in range(B) for i in range(AROWS // P)] + \
        [b * (L // P) + i for b in range(B) for i in range(AROWS // P, L // P)]
E, H = 8, 1024
HC = H // P
LN_EPS = 1e-5
RMS_EPS = 1e-5
LOGP = -0.001
DT = -math.log(-math.expm1(LOGP))
SLOT_TILES = 2 * T // P + E - 1
FULL_TILES = 2 * T // P
TC = SLOT_TILES + 1
WQ = 4
WCOLS = DC * H + HC * D
QCOLS = WCOLS // WQ


def perceiver_layer(nc, x_in, ctx_in, lens_in, w_in, b_in, g_res, g_init, w_qkv, b_qkv, w_out, b_out,
                    w_gate, w1, b1, w2, b2, out):
    x_rows = x_in.rearrange("b (i p) d -> p (b i) d", p=P)

    with ExitStack() as ctx:
        def sem(name):
            return ctx.enter_context(nc.semaphore(name))

        banks = [ctx.enter_context(nc.psum_tensor(f"bank{i}", [P, 512], F32)) for i in range(8)]

        BASE = 16512
        K = 1024

        def place(name, shape, dtype, at):
            return nc.alloc_sbuf_tensor_at(name, shape, dtype, offset=BASE + at)

        x_res = place("x_res", [P, NT, D], F32, 0)
        SMALL, RAW, MID, BIG = 16 * K, 27 * K, 43 * K, 79 * K
        small_at = [SMALL]

        def small(name, shape, dtype):
            words = 1
            for n in shape[1:]:
                words *= n
            size = words * (2 if dtype == BF16 else 4)
            t = place(name, shape, dtype, small_at[0])
            small_at[0] += -(-size // 32) * 32
            assert small_at[0] <= RAW
            return t

        ident = small("ident", [P, P], F32)
        before = small("before", [P, P], F32)
        ones_bf = small("ones_bf", [P, P], BF16)
        s_col = small("s_col", [P, LT], F32)
        lnb = small("lnb", [P, 1], F32)
        iota16 = small("iota16", [P, 16], F32)
        iota32 = small("iota32", [P, 32], F32)
        diag16 = small("diag16", [16, 16], F32)
        g_res_col = small("g_res_col", [P, DC], F32)
        bn = small("bn", [P, NT, 6], F32)
        mv = small("mv", [P, NT, 2], F32)
        var_eps = small("var_eps", [P, NT], F32)
        sd = small("sd", [P, NT], F32)
        rstd = small("rstd", [P, NT], F32)
        row_scale = small("row_scale", [P, NT], F32)
        row_shift = small("row_shift", [P, NT], F32)
        tmp8 = small("tmp8", [P, NT], F32)
        ctx_ss = small("ctx_ss", [P, NT], F32)
        ctx_rs = small("ctx_rs", [P, NT], F32)
        ctx_sd = small("ctx_sd", [P, NT], F32)
        prefix = small("prefix", [P, B], F32)

        ctx_sb = place("ctx_sb", [P, B * LT, DG], F32, BIG)
        patches = place("patches", [P, B * LT, D], F32, BIG + 32 * K)
        decay = place("decay", [P, B * LT, L], F32, BIG + 48 * K)
        w_in_sb = place("w_in_sb", [P, DC, D], F32, BIG + 64 * K)
        w_inT_hi = place("w_inT_hi", [P, DC, D], F32R, BIG + 72 * K)
        w_inT_lo = [place(f"w_inT_lo{k}", [P, D], F32R, at) for k, at in
                    enumerate((RAW + 12 * K, RAW + 14 * K, MID + 12 * K, MID + 14 * K))]
        hnT_hi = place("hnT_hi", [P, 2, DC, P], F32R, BIG + 80 * K)
        hnT_lo = place("hnT_lo", [P, 2, DC, P], F32R, BIG + 64 * K)
        hn = place("hn", [P, 2, D], F32, BIG + 84 * K)
        oh_hi = place("oh_hi", [P, B * NJ, 16], BF16, BIG + 88 * K)
        oh_lo = place("oh_lo", [P, B * NJ, 32], BF16, BIG + 92 * K)
        lens_f = place("lens_f", [P, B * NJ], F32, BIG + 100 * K)
        within = place("within", [P, B, NJ], F32, BIG + 100 * K + 512)
        bidx = place("bidx", [P, B * NJ], F32, BIG + 101 * K)
        wrap = place("wrap", [P, B * NJ], F32, BIG + 101 * K + 512)
        cell = place("cell", [P, B * NJ], I32, BIG + 102 * K)
        cell_hi = place("cell_hi", [P, B * NJ], I32, BIG + 102 * K + 512)
        cell_lo = place("cell_lo", [P, B * NJ], I32, BIG + 123 * K)
        plug = place("plug", [P, B, L], F32, BIG + 103 * K)
        ones_f = place("ones_f", [P, L], F32, BIG + 107 * K)
        gap = place("gap", [P, 2, L], F32, BIG + 109 * K)
        blocks = place("blocks", [16, B, 16, 32], BF16, BIG + 113 * K)
        b_in_row = place("b_in_row", [P, D], F32, BIG + 126 * K)
        g_init_row = place("g_init_row", [P, D], F32, BIG + 117 * K)
        squares = place("squares", [P, DG], F32, BIG + 119 * K)
        lens_i = place("lens_i", [P, B, NJ], I32, BIG + 123 * K + 512)
        hits = place("hits", [16, B, 32], F32, BIG + 124 * K)

        w_raw = place("w_raw", [P, 2, QCOLS], F32, RAW)

        wq_raw = [place(f"wq_raw{k}", [P, 3 * D], F32, at) for k, at in
                  enumerate((RAW, RAW + 6 * K, MID + 24 * K, MID + 30 * K))]

        b_v_row = small("b_v_row", [P, D], F32)
        b_out_row = small("b_out_row", [P, D], F32)
        b_qk_col = small("b_qk_col", [P, 2 * DC], F32)
        neg_max = small("neg_max", [P, 4, 2], F32)
        max_bias = small("max_bias", [P, 4, 2], F32)
        prob_sum = small("prob_sum", [P, 4, 2], F32)
        prob_inv = small("prob_inv", [P, 4, 2], F32)
        wq_hi = place("wq_hi", [P, DC, 3 * D], F32R, BIG)
        wq_lo = place("wq_lo", [P, DC, 3 * D], F32R, BIG + 88 * K)
        xn = place("xn", [P, 2, D], F32, BIG + 24 * K)
        xnT_hi = place("xnT_hi", [P, DC, B * AROWS], F32R, MID)
        xnT_lo = place("xnT_lo", [P, DC, B * AROWS], F32R, BIG + 112 * K)
        qk_hi = place("qk_hi", [P, 2, AROWS], F32, BIG + 28 * K)
        qk_lo = place("qk_lo", [P, 2, AROWS], F32, BIG + 31 * K)
        q_parts = place("q_parts", [3 * HD, 8, WIN], F32R, BIG + 46 * K)
        k_parts = place("k_parts", [3 * HD, 8, WIN], F32R, BIG + 54 * K)
        v_heads = place("v_heads", [P, 2, 2, P], F32, BIG + 62 * K)
        probs = place("probs", [P, 4, 2, WIN], F32, BIG + 34 * K)
        probs_n = place("probs_n", [P, 2, 2, WIN], F32, BIG + 64 * K)
        probsT = place("probsT", [P, 2, 2, WIN], F32, BIG + 68 * K)
        oT_hi = place("oT_hi", [P, B * NWIN * 4, WIN], F32R, MID)
        oT_lo = place("oT_lo", [P, B * NWIN * 4, WIN], F32R, BIG + 104 * K)
        w_out_sb = place("w_out_sb", [P, DC, D], F32, MID + 16 * K)
        w_out_hi = [place(f"w_out_hi{k}", [P, D], F32R, BIG + at * K) for k, at in enumerate((42, 44, 124, 126))]
        w_out_lo = place("w_out_lo", [P, DC, D], F32R, MID + 16 * K)
        v_sb = place("v_sb", [P, B * AT, D], F32, MID + 24 * K)
        qk_dram = nc.dram_tensor("qk_parts", (2 * DC, 4, 3, HD, B * AROWS), F32, kind="Internal").ap()
        Q_PARTS, K_PARTS = (0, 1, 0), (0, 0, 1)

        w_gate_sb = small("w_gate_sb", [P, DC, E], F32)
        x3 = place("x3", [P, 2, D], F32, MID + 24 * K)
        x3T = place("x3T", [P, 2, DC, P], F32, MID + 28 * K)
        ROUTE = BIG + 110 * K
        route_at = [ROUTE]

        def route(name, shape, dtype=F32):
            words = 1
            for n in shape[1:]:
                words *= n
            t = place(name, shape, dtype, route_at[0])
            route_at[0] += -(-words * (2 if dtype == BF16 else 4) // 32) * 32
            assert route_at[0] <= BIG + 128 * K
            return t

        logit = route("logit", [P, NT, E])
        top = [route(f"top{c}", [P, NT]) for c in range(2)]
        eq = route("eq", [P, NT, E])
        rank_key = route("rank_key", [P, NT])
        pick = route("pick", [P, 2, NT, E])
        score = route("score", [P, 2, NT])
        exp_gap = route("exp_gap", [P, NT])
        denom = route("denom", [P, NT])
        PAD = NT // 2
        chosen_sums = [route(f"chosen_sums{i}", [P, PAD + NT, E], BF16) for i in range(4)]
        chosen = chosen_sums[0][:, PAD:, :]
        earlier = chosen_sums[3][:, PAD - 1:, :]
        before_bf = small("before_bf", [P, P], BF16)
        rank_sb = route("rank_sb", [P, NT + 1, E])
        count_i = route("count_i", [P, E], I32)
        tiles_of = route("tiles_of", [P, E])
        tiles_end = route("tiles_end", [P, E])
        slot_base = route("slot_base", [P, E])
        slot_all = route("slot_all", [P, NT, E])
        slot_pick = route("slot_pick", [P, 2, NT, E])
        slot_f = route("slot_f", [P, 2, NT])
        slot_hi = route("slot_hi", [P, 2 * NT], I32)
        slot_lo = route("slot_lo", [P, 2 * NT], I32)
        lo_hot = route("lo_hot", [P, 2 * NT, P], BF16)
        cast_token = route("cast_token", [P, 2 * NT, 3, TC], BF16)
        pad_row = route("pad_row", [P, 2])
        cast_score = route("cast_score", [P, 2 * NT, 3, TC], BF16)
        score_part = [route(f"score_part{i}", [P, 2 * NT], BF16) for i in range(3)]
        score_left = [route(f"score_left{i}", [P, 2 * NT]) for i in range(2)]
        token_tile = route("token_tile", [P, 2, NT])
        token_row = route("token_row", [P, 1])
        slot_parts = route("slot_parts", [P, 3 * TC])
        slot_row = route("slot_row", [P, TC])
        iota128 = route("iota128", [P, P])
        iota_tc = route("iota_tc", [P, TC])
        down8 = route("down8", [P, E])
        tile_cmp = route("tile_cmp", [P, TC, E])
        tile_e = route("tile_e", [P, TC])
        tile_new = route("tile_new", [P, TC])
        slot_u = small("slot_u", [P, 2 * NT], I32)
        tile_expert = small("tile_expert", [1, TC], I32)
        tile_loads = small("tile_loads", [1, TC], I32)
        tile_next = small("tile_next", [1, TC], I32)
        tile_after = small("tile_after", [1, TC], I32)
        tile_used = small("tile_used", [1, TC], I32)
        slot_token = small("slot_token", [P, TC], I32)
        slot_score = small("slot_score", [P, TC], F32)
        add_at = [small(f"add_at{i}", [P, 1], I32) for i in range(2)]
        gather_at = [small(f"gather_at{i}", [P, 1], I32) for i in range(2)]
        score_col = small("score_col", [P, 2], F32)
        ones8 = small("ones8", [P, E], F32)

        x_gath = place("x_gath", [P, 2, D], F32, MID + 32 * K)
        xT_hi = place("xT_hi", [P, DC, P], F32R, MID)
        xT_lo = place("xT_lo", [P, DC, P], F32R, MID + 2 * K)
        h_sb = place("h_sb", [P, H], F32, MID + 4 * K)
        hT_hi = place("hT_hi", [P, HC, P], F32R, MID + 8 * K)
        hT_lo = place("hT_lo", [P, HC, P], F32R, MID + 12 * K)
        b1_row = place("b1_row", [P, 2, H], F32, MID + 16 * K)
        b2_row = place("b2_row", [P, 2, D], F32, MID + 24 * K)
        y_sb = place("y_sb", [P, 2, D], F32, MID + 28 * K)
        w_hi = place("w_hi", [P, 2 * WCOLS], F32R, BIG)
        w_lo = place("w_lo", [P, 2 * WCOLS], F32R, BIG + 64 * K)
        x3_dram = nc.dram_tensor("x3_rows", (T + P, D), F32, kind="Internal").ap()
        sum_dram = nc.dram_tensor("sum_rows", (T + P, D), F32, kind="Internal").ap()

        x_loaded, h_used = [sem("x_loaded0"), sem("x_loaded1")], sem("h_used")
        lens_loaded, ctx_loaded = sem("lens_loaded"), [sem("ctx_loaded0"), sem("ctx_loaded1")]
        w_in_loaded, rows_loaded = sem("w_in_loaded"), sem("rows_loaded")
        consts, consts2 = sem("consts"), sem("consts2")
        vector_step = sem("vector_step")
        lens_scanned, prefix_done, onehots, hits_done, blocks_ready, rows_counted = (
            sem(n) for n in ("lens_scanned", "prefix_done", "onehots", "hits_done", "blocks_ready", "rows_counted"))
        ctx_summed, ctx_eps, ctx_rooted, patches_ready = (
            sem(n) for n in ("ctx_summed", "ctx_eps", "ctx_rooted", "patches_ready"))
        var_ready, rooted, scales_ready, normed, xb_ready = (
            sem(n) for n in ("var_ready", "rooted", "scales_ready", "normed", "xb_ready"))
        gap_ready, decayed, decay_ready = sem("gap_ready"), sem("decayed"), sem("decay_ready")
        w_in_turned, w_in_ready = sem("w_in_turned"), sem("w_in_ready")
        h_turned, hnT_hi_ready, hnT_lo_ready, embedded, x1_ready = (
            sem(n) for n in ("h_turned", "hnT_hi_ready", "hnT_lo_ready", "embedded", "x1_ready"))
        w_inT_hi_ready, ctx_scale, ctx_scaled = sem("w_inT_hi_ready"), sem("ctx_scale"), sem("ctx_scaled")
        wq_hi_ready, wq_lo_ready = sem("wq_hi_ready"), sem("wq_lo_ready")
        wq_loaded = [sem(f"wq_loaded{k}") for k in range(DC)]
        w_out_loaded, x2_ready = sem("w_out_loaded"), sem("x2_ready")
        att_var, att_root, att_scale, xn_ready, xn_turned, xnT_hi_ready = (
            sem(n) for n in ("att_var", "att_root", "att_scale", "xn_ready", "xn_turned", "xnT_hi_ready"))
        xnT_lo_ready = sem("xnT_lo_ready")
        qk_summed, qk_hi_ready, qk_lo_ready, qk_stored, v_summed, v_ready, xo_ready = (
            sem(n) for n in ("qk_summed", "qk_hi_ready", "qk_lo_ready", "qk_stored", "v_summed", "v_ready", "xo_ready"))
        qk_stored = [qk_stored, sem("qk_stored1")]
        parts_loaded = [sem(f"parts_loaded{i}") for i in range(4)]
        v_staged, scores_ready, max_ready, exp_done, inv_ready, normalised, turned, probsT_ready, pv_done, oT_ready = (
            sem(n) for n in ("v_staged", "scores_ready", "max_ready", "exp_done", "inv_ready", "normalised",
                             "turned", "probsT_ready", "pv_done", "oT_ready"))
        oT_lo_ready, w_out_hi_ready, w_out_lo_ready = sem("oT_lo_ready"), sem("w_out_hi_ready"), sem("w_out_lo_ready")
        projected, cols_loaded = sem("projected"), sem("cols_loaded")
        max_taken = sem("max_taken")
        out_stored = [sem("out_stored0"), sem("out_stored1")]
        x3_var, x3_root, x3_scale, x3_ready, x3_turned, x3T_ready, gated = (
            sem(n) for n in ("x3_var", "x3_root", "x3_scale", "x3_ready", "x3_turned", "x3T_ready", "gated"))
        x3_stored = [sem("x3_stored0"), sem("x3_stored1")]
        route_consts, gap2_ready, gap2_exp, ranks_asked, ranked, casts_ready, cast_done, tables_ready, routed = (
            sem(n) for n in ("route_consts", "gap2_ready", "gap2_exp", "ranks_asked", "ranked", "casts_ready",
                             "cast_done", "tables_ready", "routed"))
        scores_asked, scores_cast, scored = sem("scores_asked"), sem("scores_cast"), sem("scored")
        raw_loaded, hi_split, lo_split = sem("raw_loaded"), sem("hi_split"), sem("lo_split")
        raw_loaded = [raw_loaded, sem("raw_loaded1")]
        b1_loaded = [sem("b1_loaded0"), sem("b1_loaded1")]
        b2_loaded = [sem("b2_loaded0"), sem("b2_loaded1")]
        picked, gathered = sem("picked"), [sem("gathered0"), sem("gathered1")]
        xg_turned, xT_hi_ready, xT_lo_ready, up_done, h_ready, h_turned2, hT_hi_ready, hT_lo_ready, down_done = (
            sem(n) for n in ("xg_turned", "xT_hi_ready", "xT_lo_ready", "up_done", "h_ready", "h_turned2",
                             "hT_hi_ready", "hT_lo_ready", "down_done"))
        y_added, y_scaled = sem("y_added"), sem("y_scaled")
        y_stored = [sem("y_stored0"), sem("y_stored1")]
        x2_stored = sem("x2_stored")
        gate_loaded, score_picked = sem("gate_loaded"), sem("score_picked")
        down_half = sem("down_half")
        placed = sem("placed")

        block = ctx.enter_context(nc.Block())

        class Steps:

            def __init__(self, eng, done):
                self.eng, self.done, self.count = eng, done, 0

            def step(self, ins):
                ins.then_inc(self.done, 1)
                self.count += 1

            def join(self):
                self.eng.wait_ge(self.done, self.count)

            def then(self, ins):
                self.step(ins)
                self.join()

        def pass_on(eng, count, n):
            eng.wait_ge(count, n)
            eng.nop(nofuse=True)
            eng.sem_inc(count, 1)

        @block.sync
        def _(sp):
            def w_quarter(e, q):
                if q < 2:
                    return w1[bass.ds(e, 1), q * 2 * P:(q + 1) * 2 * P, :].rearrange("a (k p) n -> p (a k) n", p=P)
                return w2[bass.ds(e, 1), (q - 2) * 4 * P:(q - 1) * 4 * P, :].rearrange("a (k p) n -> p (a k) n", p=P)

            def load_quarter(e, q):
                n = H if q < 2 else D
                sp.dma_start(w_raw[:, q % 2, :].rearrange("p (k n) -> p k n", n=n),
                             w_quarter(e, q)).then_inc(raw_loaded[q % 2], 16)

            lens_v = lens_in.rearrange("b (p j) -> p b j", p=P)
            sp.dma_start(lens_i[:], lens_v).then_inc(lens_loaded, 16)
            for b in range(B):
                sp.dma_start(x_res[:, b * LT:(b + 1) * LT, :], x_rows[:, b * LT:(b + 1) * LT, :]).then_inc(x_loaded[b], 16)
            sp.dma_start(w_in_sb[:], w_in.rearrange("(j p) d -> p j d", p=P)).then_inc(w_in_loaded, 16)
            for b in range(B):
                sp.dma_start(ctx_sb[:, b * LT:(b + 1) * LT, :],
                             ctx_in[b, 0:L, :].rearrange("(k p) d -> p k d", p=P)).then_inc(ctx_loaded[b], 16)
            sp.dma_start(w_out_sb[:], w_out.rearrange("(k p) n -> p k n", p=P)).then_inc(w_out_loaded, 16)
            for k in range(DC):
                sp.dma_start(wq_raw[k][:], w_qkv[k * P:(k + 1) * P, :]).then_inc(wq_loaded[k], 16)
            for u in range(B * 2 * DC):
                b, c = divmod(u, 2 * DC)
                cols = slice(b * AROWS, (b + 1) * AROWS)
                held = Q_PARTS if c < DC else K_PARTS
                for part, src, ready in ((0, qk_hi, qk_hi_ready), (1, qk_lo, qk_lo_ready)):
                    sp.wait_ge(ready, u + 1)
                    for n in range(3):
                        if held[n] == part:
                            sp.dma_start(qk_dram[c, :, n, :, cols], src[:, u % 2, :]).then_inc(qk_stored[u % 2], 16)

            def load_parts(j, r, first=False):
                row0 = (j // 4) * AROWS + ((j // 2) % 2) * STRIDE
                g = 2 * (j % 2) + r // 2
                if not first:
                    sp.wait_ge(scores_ready, 8 * j + 2 * r - 6)
                for tile, c in ((q_parts, g), (k_parts, g + DC)):
                    h = 2 * (r % 2)
                    src = qk_dram[bass.ds(c, 1), h:h + 2, :, :, bass.ds(row0, WIN)]
                    sp.dma_start(tile[:, 2 * r:2 * r + 2, :].bitcast(F32),
                                 src.rearrange("a h x p t -> (x p) (a h) t")).then_inc(parts_loaded[r], 16)

            for parity in range(2):
                sp.wait_ge(qk_stored[parity], 48 * B * DC)
            for r in range(4):
                load_parts(0, r, True)
            for q in range(2):
                sp.wait_ge(wq_lo_ready, DC)
                load_quarter(0, q)
            with sp.Fori(1, 8) as j:
                for r in range(4):
                    load_parts(j, r)
            for i in range(NT):
                sp.wait_ge(x2_ready, i + 1)
                sp.dma_start(sum_dram[i * P:(i + 1) * P, :], x_res[:, i, :]).then_inc(x2_stored, 16)
                sp.wait_ge(x3_ready, i + 1)
                sp.dma_start(x3_dram[i * P:(i + 1) * P, :], x3[:, i % 2, :]).then_inc(x3_stored[i % 2], 16)
                if i == 0:
                    sp.dma_start(sum_dram[T:T + P, :], x_res[:, 0, :]).then_inc(x2_stored, 16)
                    sp.dma_start(x3_dram[T:T + P, :], x_res[:, 0, :]).then_inc(x2_stored, 16)
                if i in (1, 2, 6, 7):
                    n = (1, 2, 6, 7).index(i)
                    sp.wait_ge(hi_split, n + 1)
                    sp.wait_ge(lo_split, n + 1)
                    load_quarter((n + 2) // WQ, (n + 2) % WQ)

            def load_b1(t, r, first=False):
                e = sp.value_load(tile_expert[0:1, bass.ds(t, 1)], min_val=0, max_val=E - 1)
                if not first:
                    sp.wait_ge(h_ready, t - 1)
                sp.dma_start(b1_row[:, r, :], b1[bass.ds(e, 1), :].rearrange("a n -> (a n)").partition_broadcast(P)
                             ).then_inc(b1_loaded[r], 16)

            def load_b2(t, r, first=False):
                e = sp.value_load(tile_expert[0:1, bass.ds(t, 1)], min_val=0, max_val=E - 1)
                if not first:
                    sp.wait_ge(y_added, t - 1)
                sp.dma_start(b2_row[:, r, :], b2[bass.ds(e, 1), :].rearrange("a n -> (a n)").partition_broadcast(P)
                             ).then_inc(b2_loaded[r], 16)

            def load_next_expert(t):
                load = sp.value_load(tile_loads[0:1, bass.ds(t, 1)], min_val=0, max_val=1)
                e = sp.value_load(tile_next[0:1, bass.ds(t, 1)], min_val=0, max_val=E - 1)
                e_after = sp.value_load(tile_after[0:1, bass.ds(t, 1)], min_val=0, max_val=E - 1)
                sp.wait_ge(hi_split, WQ * t + WQ)
                sp.wait_ge(lo_split, WQ * t + WQ)
                sp.nop(nofuse=True)
                with sp.If(load == 1):
                    for q in range(WQ):
                        sp.wait_ge(hi_split, WQ * t + WQ + q + 1)
                        sp.wait_ge(lo_split, WQ * t + WQ + q + 1)
                        load_quarter(e if q < 2 else e_after, q % 2 + 2 if q < 2 else q - 2)
                with sp.Else():
                    for q in range(2):
                        sp.sem_inc(raw_loaded[q], 32)
                sp.nop(nofuse=True)

            sp.wait_ge(tables_ready, 1)
            for r in range(2):
                sp.wait_ge(x3_stored[r], 16 * NT // 2)
            load_b1(0, 0, True)
            load_b2(0, 0, True)

            def tile(t, r, first=False):
                load_b1(t + 1, 1 - r, first)
                load_next_expert(t)
                load_b2(t + 1, 1 - r, first)

            tile(0, 0, first=True)
            with sp.Fori(0, (SLOT_TILES - 3) // 2) as j:
                for r in (1, 0):
                    tile(2 * j + 2 - r, r)
            tile(SLOT_TILES - 2, 1)
            load_next_expert(SLOT_TILES - 1)
            for q in range(2):
                sp.wait_ge(raw_loaded[q], 32 * SLOT_TILES + 48)
            sp.wait_ge(y_stored[0], 16 * ((SLOT_TILES + 1) // 2))
            sp.wait_ge(y_stored[1], 16 * (SLOT_TILES // 2))
            sp.dma_start(out[0], sum_dram[0:L, :]).then_inc(out_stored[0], 16)
            sp.wait_ge(out_stored[0], 16)
            sp.wait_ge(out_stored[1], 16)

        @block.gpsimd
        def _(pool):
            pool.memset(ident[:], 0.0).then_inc(consts, 1)
            pool.memset(before[:], 1.0).then_inc(consts, 1)
            pool.memset(ones_bf[:], 1.0).then_inc(consts, 1)
            pool.memset(lnb[:], LOGP).then_inc(consts, 1)
            pool.memset(ones_f[:], 1.0).then_inc(consts, 1)
            pool.memset(diag16[:], 0.0).then_inc(consts, 1)
            pool.wait_ge(consts, 6)
            pool.affine_select(out=ident[:], in_=ident[:], compare_op=ALU.not_equal, fill=1.0, base=0,
                               pattern=[[-1, P]], channel_multiplier=1).then_inc(consts2, 1)
            pool.affine_select(out=before[:], in_=before[:], compare_op=ALU.is_gt, fill=0.0, base=0,
                               pattern=[[1, P]], channel_multiplier=-1).then_inc(consts2, 1)
            pool.affine_select(out=diag16[:], in_=diag16[:], compare_op=ALU.not_equal, fill=1.0, base=0,
                               pattern=[[-1, 16]], channel_multiplier=1).then_inc(consts2, 1)
            exact = dict(allow_small_or_imprecise_dtypes=True)
            pool.iota(s_col[:], [[P, LT]], base=0, channel_multiplier=1, **exact).then_inc(consts2, 1)
            pool.iota(iota16[:], [[1, 16]], base=0, channel_multiplier=0, **exact).then_inc(consts2, 1)
            pool.iota(iota32[:], [[1, 32]], base=0, channel_multiplier=0, **exact).then_inc(consts2, 1)
            pool.wait_ge(rows_loaded, 48)
            for n, i in enumerate(ORDER):
                pool.wait_ge(normed, n + 1)
                pool.tensor_tensor(out=x_res[:, i, :], in0=x_res[:, i, :], in1=b_in_row[:], op=ALU.add).then_inc(xb_ready, 1)
                if n == 3:
                    for m in range(NT):
                        pool.wait_ge(ctx_scaled, m + 1)
                        pool.tensor_tensor(out=patches[:, ORDER[m], :], in0=patches[:, ORDER[m], :], in1=g_init_row[:],
                                           op=ALU.mult).then_inc(patches_ready, 1)
            pool.wait_ge(cols_loaded, 48)
            for n, i in enumerate(ORDER):
                pool.wait_ge(x1_ready, n + 1)
                if n < B * AT:
                    pool.wait_ge(xn_ready, n + 1)
                pool.tensor_tensor(out=x_res[:, i, :], in0=x_res[:, i, :], in1=b_out_row[:],
                                   op=ALU.add).then_inc(xo_ready, 1)

            def stage_v(j, r, first=False):
                if not first:
                    pool.wait_ge(pv_done, 8 * j + 4 * r - 4)
                tile = (j // 4) * AT + (j // 2) % 2
                pool.tensor_copy(v_heads[:, r], v_sb[:, bass.ds(tile, 2), bass.ds((2 * (j % 2) + r) * P, P)]
                                 ).then_inc(v_staged, 1)

            def normalise(n, s, first=False):
                pool.wait_ge(inv_ready, n + 1)
                if not first:
                    pool.wait_ge(turned, n - 1)
                pool.tensor_tensor(out=probs_n[:, s % 2], in0=probs[:, s % 4],
                                   in1=prob_inv[:, s % 4].unsqueeze(2).to_broadcast([P, 2, WIN]),
                                   op=ALU.mult).then_inc(normalised, 1)

            def heads(j, first=False, last=False):
                for r in range(8):
                    if r == 1:
                        stage_v(j, 1, first)
                    if r == 5 and not last:
                        stage_v(j + 1, 0)
                    if not (last and r + 2 >= 8):
                        normalise(8 * j + r + 2, r + 2)

            normalise(0, 0, True)
            normalise(1, 1, True)
            pool.wait_ge(v_ready, B * AT)
            stage_v(0, 0, True)
            heads(0, first=True)
            with pool.Fori(1, 7) as j:
                heads(j)
            heads(7, last=True)
            pool.wait_ge(projected, NT)
            pool.memset(down8[:], 0.0).then_inc(route_consts, 1)
            pool.iota(token_tile[:], [[0, 2], [1, NT]], base=0, channel_multiplier=0, **exact).then_inc(route_consts, 1)
            pool.iota(token_row[:], [[1, 1]], base=0, channel_multiplier=1, **exact).then_inc(route_consts, 1)
            pool.iota(iota128[:], [[1, P]], base=0, channel_multiplier=0, **exact).then_inc(route_consts, 1)
            pool.iota(iota_tc[:], [[1, TC]], base=0, channel_multiplier=0, **exact).then_inc(route_consts, 1)
            pool.wait_ge(route_consts, 1)
            pool.iota(down8[:], [[-1, E]], base=E, channel_multiplier=0, **exact).then_inc(route_consts, 1)

            def gather(t, r, first=False):
                if not first:
                    pool.wait_ge(xg_turned, t - 1)
                pool.tensor_copy(gather_at[r][:], slot_token[:, bass.ds(t, 1)]).then_inc(picked, 1)
                pool.wait_ge(picked, t + 1)
                pool.nop(nofuse=True)
                pool.indirect_dma_start(out=x_gath[:, r, :], out_offset=None, in_=x3_dram,
                                        in_offset=bass.IndirectOffsetOnAxis(ap=gather_at[r][:].bitcast(U32), axis=0)
                                        ).then_inc(gathered[r], 16)

            def pick_score(t, r, first=False):
                if not first:
                    pool.wait_ge(y_scaled, t - 1)
                pool.tensor_copy(score_col[:, r:r + 1], slot_score[:, bass.ds(t, 1)]).then_inc(score_picked, 1)

            def add_rows(t, r, first=False):
                pool.wait_ge(y_scaled, t + 1)
                pool.tensor_copy(add_at[r][:], slot_token[:, bass.ds(t, 1)]).then_inc(placed, 1)
                pool.wait_ge(placed, t + 1)
                if not first:
                    pool.wait_ge(y_stored[1 - r], 16 * (t // 2 + r))
                pool.nop(nofuse=True)
                pool.indirect_dma_start(out=sum_dram, out_offset=bass.IndirectOffsetOnAxis(ap=add_at[r][:].bitcast(U32), axis=0),
                                        in_=y_sb[:, r, :], in_offset=None, compute_op=ALU.add).then_inc(y_stored[r], 16)

            pool.wait_ge(routed, 1)
            pool.wait_ge(x2_stored, 16 * (NT + 2))
            for r in range(2):
                pool.wait_ge(x3_stored[r], 16 * NT // 2)
            gather(0, 0, True)
            gather(1, 1, True)
            pool.wait_ge(scored, 1)
            pick_score(0, 0, True)
            pick_score(1, 1, True)
            gather(2, 0)
            gather(3, 1)
            pick_score(2, 0)
            add_rows(0, 0, True)
            with pool.Fori(2, (SLOT_TILES - 1) // 2) as j:
                for r in range(2):
                    gather(2 * j + r, r)
                    pick_score(2 * j + r - 1, 1 - r)
                    add_rows(2 * j + r - 3, 1 - r)
            gather(SLOT_TILES - 1, 0)
            for t in range(SLOT_TILES - 2, SLOT_TILES):
                pick_score(t, t % 2)
                add_rows(t - 2, t % 2)
            for t in range(SLOT_TILES - 2, SLOT_TILES):
                add_rows(t, t % 2)

        @block.scalar
        def _(act):
            act.dma_start(b_in_row[:], b_in.partition_broadcast(P)).then_inc(rows_loaded, 16)
            act.dma_start(g_init_row[:], g_init[0:D].partition_broadcast(P)).then_inc(rows_loaded, 16)
            act.dma_start(g_res_col[:], g_res.rearrange("(k p) -> p k", p=P), allow_slow_non_contiguous=True).then_inc(rows_loaded, 16)
            act.dma_start(b_qk_col[:], b_qkv[0:2 * D].rearrange("(k p) -> p k", p=P),
                          allow_slow_non_contiguous=True).then_inc(cols_loaded, 16)
            act.dma_start(w_gate_sb[:], w_gate.rearrange("(k p) e -> p k e", p=P)).then_inc(gate_loaded, 16)
            act.dma_start(b_v_row[:], b_qkv[2 * D:3 * D].partition_broadcast(P)).then_inc(cols_loaded, 16)
            act.dma_start(b_out_row[:], b_out.partition_broadcast(P)).then_inc(cols_loaded, 16)
            act.wait_ge(var_ready, 1)
            act.activation(sd[:], var_eps[:], ACT.Sqrt).then_inc(rooted, 1)
            act.wait_ge(rows_loaded, 48)

            def keep_w_inT_hi(k):
                act.wait_ge(w_in_turned, k + 1)
                act.activation(w_inT_hi[:, k, :], banks[(1, 2, 5, 6)[k]][:], ACT.Copy,
                               scale=g_res_col[:, k:k + 1]).then_inc(w_inT_hi_ready, 1)

            keep_w_inT_hi(0)
            keep_w_inT_hi(1)
            act.wait_ge(var_ready, 2)
            act.activation(sd[:], var_eps[:], ACT.Sqrt).then_inc(rooted, 1)
            keep_w_inT_hi(2)
            keep_w_inT_hi(3)
            act.wait_ge(scales_ready, 1)

            def norm_row(n):
                if n >= 2:
                    act.wait_ge(h_turned, n - 1)
                i = ORDER[n]
                act.activation(hn[:, n % 2, :], x_res[:, i, :], ACT.Identity, bias=row_shift[:, i:i + 1],
                               scale=row_scale[:, i:i + 1]).then_inc(normed, 1)

            def sum_ctx(n):
                act.wait_ge(ctx_loaded[n // LT], 16)
                if n > 0:
                    act.wait_ge(ctx_summed, n)
                act.activation(squares[:], ctx_sb[:, n, :], ACT.Square, accum_out=ctx_ss[:, n:n + 1]).then_inc(ctx_summed, 1)

            def split_wq(k):
                act.wait_ge(ctx_scaled, (2, 3, NT, NT)[k])
                act.wait_ge(wq_loaded[k], 16)
                act.activation(wq_hi[:, k, :], wq_raw[k][:], ACT.Copy).then_inc(wq_hi_ready, 1)

            def keep_hnT_hi(n):
                act.wait_ge(h_turned, n + 1)
                if n >= 2:
                    act.wait_ge(h_used, n - 1)
                act.activation(hnT_hi[:, n % 2].rearrange("p k t -> p (k t)"), banks[3 + n % 2][:],
                               ACT.Copy).then_inc(hnT_hi_ready, 1)

            norm_row(0)
            norm_row(1)
            def scale_ctx(first, end):
                act.wait_ge(ctx_scale, 1)
                for i in ORDER[first:end]:
                    act.activation(patches[:, i, :], ctx_sb[:, i, 0:D], ACT.Copy,
                                   scale=ctx_rs[:, i:i + 1]).then_inc(ctx_scaled, 1)

            for n in range(B * LT):
                if n < 2:
                    keep_hnT_hi(n)
                    norm_row(n + 2)
                sum_ctx(n)
            for n in range(2, 5):
                keep_hnT_hi(n)
                if n == 2:
                    act.wait_ge(ctx_eps, 1)
                    act.activation(ctx_sd[:], ctx_rs[:], ACT.Sqrt).then_inc(ctx_rooted, 1)
                    scale_ctx(0, 4)
                if n + 2 < 6:
                    norm_row(n + 2)
            scale_ctx(4, NT)
            for n, i in enumerate(ORDER):
                act.wait_ge(gap_ready, n + 1)
                lo = (i % LT) * P
                act.activation(gap[:, n % 2, lo:], gap[:, n % 2, lo:], ACT.Exp, bias=lnb[:], scale=-DT).then_inc(decayed, 1)
                if n == LT - 1:
                    norm_row(6)
                    norm_row(7)
                    keep_hnT_hi(5)
                if n in (5, 6):
                    keep_hnT_hi(n + 1)
                if n in (3, 4):
                    split_wq(n - 3)

            def keep_xnT(m):
                act.wait_ge(xn_turned, m + 1)
                act.activation(xnT_hi[:, :, m * P:(m + 1) * P], banks[3 + m % 2][:].rearrange("p (k t) -> p k t", k=DC),
                               ACT.Copy).then_inc(xnT_hi_ready, 1)

            for m in range(B * AT):
                i = ORDER[m]
                act.wait_ge(att_var, m + 1)
                act.activation(sd[:, i:i + 1], var_eps[:, i:i + 1], ACT.Sqrt).then_inc(att_root, 1)
                act.wait_ge(att_scale, m + 1)
                if m >= 2:
                    act.wait_ge(xn_turned, m - 1)
                if m == 0:
                    act.wait_ge(ctx_scaled, NT)
                act.activation(xn[:, m % 2, :], x_res[:, i, :], ACT.Identity, bias=row_shift[:, i:i + 1],
                               scale=rstd[:, i:i + 1]).then_inc(xn_ready, 1)
                if m >= 1:
                    keep_xnT(m - 1)
                if m in (1, 2):
                    split_wq(m + 1)
            keep_xnT(B * AT - 1)
            act.wait_ge(cols_loaded, 48)
            for u in range(B * 2 * DC):
                c = u % (2 * DC)
                act.wait_ge(qk_summed, u + 1)
                if u >= 2:
                    act.wait_ge(qk_stored[u % 2], 48 * (u // 2))
                act.activation(qk_hi[:, u % 2, :].bitcast(F32R), banks[u % 3][:, 0:AROWS], ACT.Identity,
                               bias=b_qk_col[:, c:c + 1]).then_inc(qk_hi_ready, 1)
                if u < DC:
                    act.wait_ge(w_out_loaded, 16)
                    act.activation(w_out_hi[u][:], w_out_sb[:, u, :], ACT.Copy).then_inc(w_out_hi_ready, 1)

            def split_hi(base, q, n):
                act.wait_ge(raw_loaded[q % 2], 16 * (2 * n + q // 2) + 16)
                act.activation(w_hi[:, bass.ds(base + q * QCOLS, QCOLS)], w_raw[:, q % 2, :], ACT.Copy).then_inc(hi_split, 1)

            def exponents(n, s, first=False):
                act.wait_ge(max_ready, n + 1)
                if not first:
                    act.wait_ge(normalised, n - 3)
                for q in range(2):
                    last = act.activation(probs[:, s % 4, q], banks[s % 4][:, q * WIN:(q + 1) * WIN], ACT.Exp,
                                          bias=max_bias[:, s % 4, q:q + 1], scale=HD ** -0.5,
                                          accum_out=prob_sum[:, s % 4, q:q + 1])
                last.then_inc(exp_done, 1)

            def keep_heads(it, r):
                act.wait_ge(pv_done, 4 * it + 4)
                act.activation(oT_hi[:, bass.ds(it, 1), :].rearrange("p a t -> p (a t)"), banks[6 + r % 2][:, 0:WIN],
                               ACT.Copy).then_inc(oT_ready, 1)

            def heads(j, first=False, last=False):
                for r in range(8):
                    if not (last and r + 3 >= 8):
                        exponents(8 * j + r + 3, r + 3, first and r + 3 < 4)
                    if r == 4:
                        keep_heads(2 * j, 0)
                    if r == 0 and not first:
                        keep_heads(2 * j - 1, 1)

            for n in range(3):
                exponents(n, n, True)
            heads(0, first=True)
            with act.Fori(1, 7) as j:
                heads(j)
            heads(7, last=True)
            keep_heads(15, 1)
            for i in range(NT):
                act.wait_ge(x3_var, i + 1)
                act.activation(sd[:, i:i + 1], var_eps[:, i:i + 1], ACT.Sqrt).then_inc(x3_root, 1)
                act.wait_ge(x3_scale, i + 1)
                if i >= 2:
                    act.wait_ge(x3_turned, i - 1)
                    act.wait_ge(x3_stored[i % 2], 16 * (i // 2))
                act.activation(x3[:, i % 2, :], x_res[:, i, :], ACT.Identity, bias=row_shift[:, i:i + 1],
                               scale=rstd[:, i:i + 1]).then_inc(x3_ready, 1)
                if i in (0, 1, 4, 6):
                    split_hi(0, (0, 1, 4, 6).index(i), 0)

            act.wait_ge(gap2_ready, 1)
            act.activation(exp_gap[:], exp_gap[:], ACT.Exp).then_inc(gap2_exp, 1)

            def take_x(t, r):
                act.wait_ge(xg_turned, t + 1)
                act.activation(xT_hi[:].rearrange("p k t -> p (k t)"), banks[5][:], ACT.Copy).then_inc(xT_hi_ready, 1)

            def take_h(t):
                act.wait_ge(h_turned2, t + 1)
                for a in range(2):
                    last = act.activation(hT_hi[:, 4 * a:4 * a + 4, :].rearrange("p k t -> p (k t)"), banks[2 + a][:],
                                          ACT.Relu)
                last.then_inc(hT_hi_ready, 1)

            def give_y(t, r):
                act.wait_ge(y_added, t + 1)
                act.wait_ge(score_picked, t + 1)
                act.activation(y_sb[:, r, :], y_sb[:, r, :], ACT.Copy, scale=score_col[:, r:r + 1]).then_inc(y_scaled, 1)

            def tile(t, r, first=False, last=False, spare=False):
                load = act.value_load(tile_loads[0:1, bass.ds(t, 1)], min_val=0, max_val=1)
                if spare:
                    used = act.value_load(tile_used[0:1, bass.ds(t, 1)], min_val=0, max_val=1)
                e = act.value_load(tile_next[0:1, bass.ds(t, 1)], min_val=0, max_val=E - 1)

                def work(split_next):
                    split_next(0)
                    split_next(1)
                    if not last:
                        take_x(t + 1, 1 - r)
                    if not first:
                        give_y(t - 1, 1 - r)
                    take_h(t)
                    split_next(2)
                    split_next(3)

                def pass_tile():
                    if not last:
                        act.wait_ge(xg_turned, t + 2)
                        pass_on(act, xT_hi_ready, t + 1)
                    give_y(t - 1, 1 - r)
                    act.wait_ge(h_turned2, t + 1)
                    pass_on(act, hT_hi_ready, t)

                def split(q):
                    if not first:
                        act.wait_ge((up_done, up_done, down_half, down_done)[q], t)
                    split_hi(base, q, t + 1)

                act.wait_ge(hi_split, WQ * t + WQ)
                act.nop(nofuse=True)
                with act.If(load == 1):
                    base = act.snap((e % 2) * WCOLS)
                    work(split)
                with act.Else():
                    act.sem_inc(hi_split, WQ)
                    if spare:
                        with act.If(used == 1):
                            work(lambda q: None)
                        with act.Else():
                            pass_tile()
                    else:
                        work(lambda q: None)
                act.nop(nofuse=True)

            take_x(0, 0)
            tile(0, 0, first=True)

            with act.Fori(0, FULL_TILES // 2 - 1) as j:
                for r in (1, 0):
                    tile(2 * j + 2 - r, r)
            with act.Fori(FULL_TILES // 2 - 1, (SLOT_TILES - 3) // 2) as j:
                for r in (1, 0):
                    tile(2 * j + 2 - r, r, spare=True)
            tile(SLOT_TILES - 2, 1, spare=True)
            tile(SLOT_TILES - 1, 0, last=True, spare=True)
            give_y(SLOT_TILES - 1, 0)
            act.wait_ge(y_stored[0], 16 * ((SLOT_TILES + 1) // 2))
            act.wait_ge(y_stored[1], 16 * (SLOT_TILES // 2))
            act.dma_start(out[1], sum_dram[L:T, :]).then_inc(out_stored[1], 16)

        @block.vector
        def _(dve):
            own = Steps(dve, vector_step)
            dve.wait_ge(consts, 6)
            dve.wait_ge(lens_loaded, 16)
            own.then(dve.tensor_copy(lens_f[:], lens_i[:].rearrange("p b j -> p (b j)")))
            for b in range(B):
                dve.tensor_tensor_scan(within[:, b, :], ones_f[:, 0:NJ], lens_f[:, b * NJ:(b + 1) * NJ], 0.0,
                                       ALU.mult, ALU.add).then_inc(lens_scanned, 1)
            for i in range(NT):
                if i % LT == 0:
                    dve.wait_ge(x_loaded[i // LT], 16)
                own.step(dve.bn_stats(bn[:, i, :], x_res[:, i, :]))
            own.join()
            for i in range(NT):
                own.step(dve.bn_aggr(mv[:, i, :], bn[:, i, :]))
            own.join()
            dve.tensor_scalar(var_eps[:], mv[:, :, 1], LN_EPS, None, ALU.add).then_inc(var_ready, 1)
            dve.wait_ge(prefix_done, 1)
            own.then(dve.tensor_copy(prefix[:], banks[0][:, 0:B]))
            for b in range(B):
                own.step(dve.tensor_scalar(bidx[:, b * NJ:(b + 1) * NJ], within[:, b, :], prefix[:, b:b + 1], -1.0,
                                           ALU.add, ALU.add))
            own.join()
            own.then(dve.tensor_scalar(wrap[:], bidx[:], 0.0, float(L), ALU.is_lt, ALU.mult))
            own.then(dve.tensor_tensor(cell[:], bidx[:], wrap[:], ALU.add))
            own.step(dve.tensor_scalar(cell_hi[:], cell[:], 5, None, ALU.arith_shift_right))
            own.step(dve.tensor_scalar(cell_lo[:], cell[:], 31, None, ALU.bitwise_and))
            dve.wait_ge(rooted, 1)
            own.then(dve.reciprocal(rstd[:], sd[:]))
            own.then(dve.tensor_tensor(tmp8[:], rstd[:], rstd[:], ALU.mult))
            own.then(dve.tensor_tensor(tmp8[:], tmp8[:], mv[:, :, 1], ALU.mult))
            dve.tensor_scalar(var_eps[:], tmp8[:], RMS_EPS, None, ALU.add).then_inc(var_ready, 1)
            dve.wait_ge(consts2, 6)
            dve.tensor_tensor(oh_hi[:], cell_hi[:].unsqueeze(2).to_broadcast([P, B * NJ, 16]),
                              iota16[:].unsqueeze(1).to_broadcast([P, B * NJ, 16]), ALU.is_equal).then_inc(onehots, 1)
            dve.wait_ge(rooted, 2)
            own.then(dve.reciprocal(tmp8[:], sd[:]))
            own.then(dve.tensor_tensor(row_scale[:], tmp8[:], rstd[:], ALU.mult))
            dve.scalar_tensor_tensor(row_shift[:], mv[:, :, 0], -1.0, row_scale[:], ALU.mult,
                                     ALU.mult).then_inc(scales_ready, 1)
            dve.wait_ge(rows_loaded, 48)
            for k in range(DC):
                dve.wait_ge(w_in_turned, k + 1)
                dve.wait_ge(w_inT_hi_ready, k + 1)
                dve.scalar_tensor_tensor(w_inT_lo[k][:], banks[(1, 2, 5, 6)[k]][:], g_res_col[:, k:k + 1],
                                         w_inT_hi[:, k, :].bitcast(F32), ALU.mult, ALU.subtract).then_inc(w_in_ready, 1)

            def keep_hnT_lo(n):
                dve.wait_ge(hnT_hi_ready, n + 1)
                if n >= 2:
                    dve.wait_ge(h_used, n - 1)
                dve.tensor_tensor(hnT_lo[:, n % 2].rearrange("p k t -> p (k t)"), banks[3 + n % 2][:],
                                  hnT_hi[:, n % 2].rearrange("p k t -> p (k t)").bitcast(F32),
                                  ALU.subtract).then_inc(hnT_lo_ready, 1)

            for b in range(B):
                keep_hnT_lo(b)
                dve.tensor_tensor(oh_lo[:, b * NJ:(b + 1) * NJ, :],
                                  cell_lo[:, b * NJ:(b + 1) * NJ].unsqueeze(2).to_broadcast([P, NJ, 32]),
                                  iota32[:].unsqueeze(1).to_broadcast([P, NJ, 32]), ALU.is_equal).then_inc(onehots, 1)
            keep_hnT_lo(2)
            dve.wait_ge(hits_done, 1)
            own.then(dve.tensor_scalar(hits[:], banks[0][0:16, 64:64 + B * 32].rearrange("p (b c) -> p b c", b=B),
                                       1.0, None, ALU.min))
            for b in range(B):
                dve.tensor_tensor(blocks[:, b], hits[:, b, :].unsqueeze(1).to_broadcast([16, 16, 32]),
                                  diag16[:].unsqueeze(2).to_broadcast([16, 16, 32]), ALU.mult).then_inc(blocks_ready, 1)
            dve.wait_ge(ctx_summed, B * LT)
            dve.tensor_scalar(ctx_rs[:], ctx_ss[:], 1.0 / DG, RMS_EPS, ALU.mult, ALU.add).then_inc(ctx_eps, 1)
            dve.wait_ge(ctx_rooted, 1)
            dve.reciprocal(ctx_rs[:], ctx_sd[:]).then_inc(ctx_scale, 1)
            for b in range(B):
                dve.wait_ge(rows_counted, b + 1)
                own.then(dve.tensor_tensor_scan(plug[:, b, :], ones_f[:], banks[1 + b][:], 0.0, ALU.mult, ALU.add))
                own.then(dve.tensor_scalar(plug[:, b, :], plug[:, b, :], -1.0, 0.0, ALU.add, ALU.max))
            keep_hnT_lo(3)
            keep_hnT_lo(4)


            def decay_gap(n):
                b, k = divmod(ORDER[n], LT)
                if n >= 2:
                    dve.wait_ge(decay_ready, n - 1)
                dve.tensor_scalar(gap[:, n % 2, k * P:], plug[:, b, k * P:], s_col[:, k:k + 1], 0.0,
                                  ALU.subtract, ALU.max).then_inc(gap_ready, 1)

            def decay_mask(n):
                b, k = divmod(ORDER[n], LT)
                dve.wait_ge(decayed, n + 1)
                dve.scalar_tensor_tensor(decay[:, ORDER[n], k * P:], plug[:, b, k * P:], s_col[:, k:k + 1],
                                         gap[:, n % 2, k * P:], ALU.is_ge, ALU.mult).then_inc(decay_ready, 1)

            def depool_rows(n):
                if n + 1 < NT:
                    decay_gap(n + 1)
                decay_mask(n)

            decay_gap(0)
            for n in range(4):
                depool_rows(n)

            def keep_xnT_lo(m):
                dve.wait_ge(xnT_hi_ready, m + 1)
                dve.tensor_tensor(xnT_lo[:, :, m * P:(m + 1) * P], banks[3 + m % 2][:].rearrange("p (k t) -> p k t", k=DC),
                                  xnT_hi[:, :, m * P:(m + 1) * P].bitcast(F32), ALU.subtract).then_inc(xnT_lo_ready, 1)

            def scale_att(m):
                i = ORDER[m]
                dve.wait_ge(att_root, m + 1)
                own.then(dve.reciprocal(rstd[:, i:i + 1], sd[:, i:i + 1]))
                dve.scalar_tensor_tensor(row_shift[:, i:i + 1], mv[:, i, 0:1], -1.0, rstd[:, i:i + 1], ALU.mult,
                                         ALU.mult).then_inc(att_scale, 1)

            SCALED_AFTER = ((), (), (), (0, 1), (2, 3), (4,), (5,), ())
            for n, i in enumerate(ORDER):
                dve.wait_ge(embedded, n + 1)
                dve.wait_ge(xb_ready, n + 1)
                dve.tensor_tensor(x_res[:, i, :], x_res[:, i, :], banks[(5, 6, 7, 0)[n % 4]][:], ALU.add
                                  ).then_inc(x1_ready, 1)
                if n + 5 < NT:
                    keep_hnT_lo(n + 5)
                if n + 4 < NT:
                    depool_rows(n + 4)
                if n < B * AT:
                    dve.wait_ge(x1_ready, n + 1)
                    own.then(dve.bn_stats(bn[:, i, :], x_res[:, i, :]))
                    own.then(dve.bn_aggr(mv[:, i, :], bn[:, i, :]))
                    dve.tensor_scalar(var_eps[:, i:i + 1], mv[:, i, 1:2], LN_EPS, None, ALU.add).then_inc(att_var, 1)
                for m in SCALED_AFTER[n]:
                    scale_att(m)
                if n >= 4:
                    keep_xnT_lo(n - 4)
                if n in (3, 4, 6, 7):
                    k = n - 3 if n < 5 else n - 4
                    dve.wait_ge(wq_hi_ready, k + 1)
                    dve.tensor_tensor(wq_lo[:, k, :], wq_raw[k][:], wq_hi[:, k, :].bitcast(F32),
                                      ALU.subtract).then_inc(wq_lo_ready, 1)
            for m in range(NT - 4, B * AT):
                keep_xnT_lo(m)
            dve.wait_ge(cols_loaded, 48)
            for u in range(B * 2 * DC):
                c = u % (2 * DC)
                dve.wait_ge(qk_hi_ready, u + 1)
                if u >= 2:
                    dve.wait_ge(qk_stored[u % 2], 48 * (u // 2))
                dve.scalar_tensor_tensor(qk_lo[:, u % 2, :].bitcast(F32R), banks[u % 3][:, 0:AROWS], b_qk_col[:, c:c + 1],
                                         qk_hi[:, u % 2, :], ALU.add, ALU.subtract).then_inc(qk_lo_ready, 1)
                if u < DC:
                    dve.wait_ge(w_out_hi_ready, u + 1)
                    dve.tensor_tensor(w_out_lo[:, u, :], w_out_sb[:, u, :], w_out_hi[u][:].bitcast(F32),
                                      ALU.subtract).then_inc(w_out_lo_ready, 1)

            def keep_v(m):
                dve.wait_ge(v_summed, m + 1)
                dve.tensor_tensor(v_sb[:, m, :], banks[5 + m % 2][:], b_v_row[:], ALU.add).then_inc(v_ready, 1)

            def split_lo(base, q, n):
                dve.wait_ge(raw_loaded[q % 2], 16 * (2 * n + q // 2) + 16)
                dve.wait_ge(hi_split, WQ * n + q + 1)
                dve.tensor_tensor(w_lo[:, bass.ds(base + q * QCOLS, QCOLS)], w_raw[:, q % 2, :],
                                  w_hi[:, bass.ds(base + q * QCOLS, QCOLS)].bitcast(F32), ALU.subtract).then_inc(lo_split, 1)

            def maxima(n, s):
                dve.wait_ge(scores_ready, n + 1)
                dve.tensor_reduce(neg_max[:, s % 4, :], banks[s % 4][:].rearrange("p (q k) -> p q k", q=2),
                                  AX.X, ALU.max, negate=True).then_inc(max_taken, 1)
                dve.wait_ge(max_taken, n + 1)
                dve.tensor_scalar(max_bias[:, s % 4, :], neg_max[:, s % 4, :], HD ** -0.5, None,
                                  ALU.mult).then_inc(max_ready, 1)

            def inverse(n, s, first=False):
                dve.wait_ge(exp_done, n + 1)
                if not first:
                    dve.wait_ge(normalised, n - 3)
                dve.reciprocal(prob_inv[:, s % 4, :], prob_sum[:, s % 4, :]).then_inc(inv_ready, 1)

            def copy_probsT(n, s, first=False):
                dve.wait_ge(turned, n + 1)
                if not first:
                    dve.wait_ge(pv_done, n - 1)
                dve.tensor_copy(probsT[:, s % 2].rearrange("p a q -> p (a q)"), banks[4 + s % 2][:]).then_inc(probsT_ready, 1)

            def heads(j, first=False, last=False):
                for r in range(8):
                    if not (last and r + 3 >= 8):
                        maxima(8 * j + r + 3, r + 3)
                    if not (last and r + 2 >= 8):
                        inverse(8 * j + r + 2, r + 2, first and r + 2 < 4)
                    copy_probsT(8 * j + r, r, first and r < 2)
                    if r == 5:
                        keep_heads_lo(2 * j, 0)
                    if r == 1 and not first:
                        keep_heads_lo(2 * j - 1, 1)

            def keep_heads_lo(it, r):
                dve.wait_ge(oT_ready, it + 1)
                dve.tensor_tensor(oT_lo[:, bass.ds(it, 1), :].rearrange("p a t -> p (a t)"), banks[6 + r][:, 0:WIN],
                                  oT_hi[:, bass.ds(it, 1), :].rearrange("p a t -> p (a t)").bitcast(F32),
                                  ALU.subtract).then_inc(oT_lo_ready, 1)

            for m in range(4):
                keep_v(m)
            maxima(0, 0)
            maxima(1, 1)
            keep_v(4)
            inverse(0, 0, True)
            maxima(2, 2)
            inverse(1, 1, True)
            keep_v(5)
            heads(0, first=True)
            with dve.Fori(1, 7) as j:
                heads(j)
            heads(7, last=True)
            keep_heads_lo(15, 1)
            def copy_x3T(i):
                dve.wait_ge(x3_turned, i + 1)
                if i >= 2:
                    dve.wait_ge(gated, i - 1)
                dve.tensor_copy(x3T[:, i % 2].rearrange("p k t -> p (k t)"), banks[3 + i % 2][:]).then_inc(x3T_ready, 1)

            own.step(dve.memset(ones8[:], 1.0))
            own.step(dve.tensor_copy(before_bf[:], before[:]))
            for i in range(NT):
                dve.wait_ge(projected, i + 1)
                dve.wait_ge(xo_ready, NT)
                dve.tensor_tensor(x_res[:, i, :], x_res[:, i, :], banks[i % 3][:], ALU.add).then_inc(x2_ready, 1)
                dve.wait_ge(x2_ready, i + 1)
                own.then(dve.bn_stats(bn[:, i, :], x_res[:, i, :]))
                own.then(dve.bn_aggr(mv[:, i, :], bn[:, i, :]))
                dve.tensor_scalar(var_eps[:, i:i + 1], mv[:, i, 1:2], LN_EPS, None, ALU.add).then_inc(x3_var, 1)
                dve.wait_ge(x3_root, i + 1)
                own.then(dve.reciprocal(rstd[:, i:i + 1], sd[:, i:i + 1]))
                dve.scalar_tensor_tensor(row_shift[:, i:i + 1], mv[:, i, 0:1], -1.0, rstd[:, i:i + 1], ALU.mult,
                                         ALU.mult).then_inc(x3_scale, 1)
                if i >= 1:
                    copy_x3T(i - 1)
                if i in (1, 2, 5):
                    split_lo(0, (1, 2, 5).index(i), 0)
            copy_x3T(NT - 1)
            split_lo(0, 3, 0)
            for sums in chosen_sums:
                own.step(dve.memset(sums[:, 0:PAD, :], 0.0))
            dve.wait_ge(gated, NT)
            dve.wait_ge(route_consts, 6)
            own.then(dve.tensor_copy(logit[:].rearrange("p i e -> p (i e)"), banks[5][:, 0:NT * E]))

            def over_e(row):
                return row.unsqueeze(2).to_broadcast([P, NT, E])

            down = down8[:].unsqueeze(1).to_broadcast([P, NT, E])
            for c in range(2):
                own.then(dve.tensor_reduce(top[c][:], logit[:], AX.X, ALU.max))
                own.then(dve.tensor_tensor(eq[:], logit[:], over_e(top[c][:]), ALU.is_equal))
                own.then(dve.tensor_tensor(eq[:], eq[:], down, ALU.mult))
                own.then(dve.tensor_reduce(rank_key[:], eq[:], AX.X, ALU.max))
                own.then(dve.tensor_tensor(pick[:, c], down, over_e(rank_key[:]), ALU.is_equal))
                if c == 0:
                    own.then(dve.scalar_tensor_tensor(logit[:], pick[:, 0], -1e30, logit[:], ALU.mult, ALU.add))
            dve.tensor_tensor(exp_gap[:], top[1][:], top[0][:], ALU.subtract).then_inc(gap2_ready, 1)
            own.then(dve.tensor_tensor(chosen, pick[:, 0], pick[:, 1], ALU.add))
            for n in range(3):
                back = 1 << n
                own.then(dve.tensor_tensor(chosen_sums[n + 1][:, PAD:, :], chosen_sums[n][:, PAD:, :],
                                           chosen_sums[n][:, PAD - back:PAD + NT - back, :], ALU.add))
            dve.sem_inc(ranks_asked, 1)

            dve.wait_ge(gap2_exp, 1)
            own.then(dve.tensor_scalar(denom[:], exp_gap[:], 1.0, None, ALU.add))
            own.then(dve.reciprocal(score[:, 0, :], denom[:]))
            own.then(dve.tensor_tensor(score[:, 1, :], score[:, 0, :], exp_gap[:], ALU.mult))
            dve.wait_ge(ranked, 1)
            own.then(dve.tensor_copy(rank_sb[:].rearrange("p i e -> p (i e)"), banks[7][:, 0:(NT + 1) * E]))
            own.then(dve.tensor_scalar(count_i[:], rank_sb[:, NT, :], float(P - 1), None, ALU.add))
            own.then(dve.tensor_scalar(count_i[:], count_i[:], 7, None, ALU.arith_shift_right))
            own.then(dve.tensor_scalar(tiles_of[:], count_i[:], 1.0, None, ALU.max))
            own.then(dve.tensor_tensor_scan(tiles_end[:], ones8[:], tiles_of[:], 0.0, ALU.mult, ALU.add))
            own.then(dve.tensor_tensor(slot_base[:], tiles_end[:], tiles_of[:], ALU.subtract))
            own.then(dve.scalar_tensor_tensor(slot_all[:], slot_base[:].unsqueeze(1).to_broadcast([P, NT, E]), float(P),
                                              rank_sb[:, 0:NT, :], ALU.mult, ALU.add))
            own.step(dve.tensor_scalar(pad_row[:, 0:1], token_row[:], float(T), None, ALU.add))
            own.step(dve.tensor_scalar(pad_row[:, 1:2], token_row[:], -1.0, float(-T), ALU.mult, ALU.add))
            for c in range(2):
                own.step(dve.tensor_tensor(slot_pick[:, c], slot_all[:], pick[:, c], ALU.mult))
            own.join()
            own.then(dve.tensor_reduce(slot_f[:], slot_pick[:], AX.X, ALU.add))
            own.then(dve.tensor_copy(slot_u[:], slot_f[:].rearrange("p c i -> p (c i)")))
            own.step(dve.tensor_scalar(slot_hi[:], slot_u[:], 7, None, ALU.arith_shift_right))
            own.step(dve.tensor_scalar(slot_lo[:], slot_u[:], P - 1, None, ALU.bitwise_and))
            own.join()
            own.step(dve.tensor_tensor(cast_token[:, :, 0, :], slot_hi[:].unsqueeze(2).to_broadcast([P, 2 * NT, TC]),
                                       iota_tc[:].unsqueeze(1).to_broadcast([P, 2 * NT, TC]), ALU.is_equal))
            own.then(dve.tensor_tensor(lo_hot[:], slot_lo[:].unsqueeze(2).to_broadcast([P, 2 * NT, P]),
                                       iota128[:].unsqueeze(1).to_broadcast([P, 2 * NT, P]), ALU.is_equal))
            own.step(dve.tensor_tensor(cast_token[:, :, 1, :], cast_token[:, :, 0, :],
                                       token_tile[:].rearrange("p c i -> p (c i)").unsqueeze(2).to_broadcast([P, 2 * NT, TC]),
                                       ALU.mult))
            own.step(dve.tensor_scalar(cast_token[:, :, 2, :], cast_token[:, :, 0, :], token_row[:, 0:1], None, ALU.mult))
            own.join()
            dve.sem_inc(casts_ready, 1)
            own.then(dve.tensor_tensor(tile_cmp[:], iota_tc[:].unsqueeze(2).to_broadcast([P, TC, E]),
                                       tiles_end[:].unsqueeze(1).to_broadcast([P, TC, E]), ALU.is_ge))
            own.then(dve.tensor_reduce(tile_e[:], tile_cmp[:], AX.X, ALU.add))
            dve.wait_ge(cast_done, 1)
            own.then(dve.tensor_scalar(slot_row[:], banks[6][:, 0:TC], pad_row[:, 1:2], pad_row[:, 0:1], ALU.mult, ALU.add))
            own.then(dve.tensor_tensor(slot_row[:], slot_row[:], banks[6][:, 2 * TC:3 * TC], ALU.add))
            dve.scalar_tensor_tensor(slot_token[:], banks[6][:, TC:2 * TC], float(P), slot_row[:], ALU.mult,
                                     ALU.add).then_inc(routed, 1)
            own.then(dve.tensor_scalar(tile_used[:], tile_e[0:1, :], float(E), None, ALU.is_lt))
            own.step(dve.memset(tile_new[:], 1.0))
            own.then(dve.tensor_scalar(tile_e[:], tile_e[:], float(E - 1), None, ALU.min))
            own.step(dve.tensor_copy(tile_expert[:], tile_e[0:1, :]))
            own.then(dve.tensor_tensor(tile_new[:, 1:], tile_e[:, 1:], tile_e[:, :-1], ALU.is_gt))
            own.then(dve.scalar_tensor_tensor(tile_loads[:], tile_e[0:1, :], float(E - 1), tile_new[0:1, :], ALU.is_lt,
                                              ALU.mult))
            own.step(dve.tensor_scalar(tile_next[:], tile_e[0:1, :], 1.0, float(E - 1), ALU.add, ALU.min))
            own.then(dve.tensor_scalar(tile_after[:], tile_e[0:1, :], 2.0, float(E - 1), ALU.add, ALU.min))
            dve.sem_inc(tables_ready, 1)
            left = score[:].rearrange("p c i -> p (c i)")
            for n in range(3):
                own.then(dve.tensor_copy(score_part[n][:], left))
                if n < 2:
                    own.then(dve.tensor_tensor(score_left[n][:], left, score_part[n][:], ALU.subtract))
                    left = score_left[n][:]
            for n in range(3):
                own.step(dve.tensor_tensor(cast_score[:, :, n, :], cast_token[:, :, 0, :],
                                           score_part[n][:].unsqueeze(2).to_broadcast([P, 2 * NT, TC]), ALU.mult))
            own.join()
            dve.sem_inc(scores_asked, 1)
            dve.wait_ge(scores_cast, 1)
            own.then(dve.tensor_copy(slot_parts[:], banks[7][:, 0:3 * TC]))
            own.then(dve.tensor_tensor(slot_parts[:, TC:2 * TC], slot_parts[:, TC:2 * TC], slot_parts[:, 2 * TC:], ALU.add))
            dve.tensor_tensor(slot_score[:], slot_parts[:, 0:TC], slot_parts[:, TC:2 * TC], ALU.add).then_inc(scored, 1)

            def take_x(t):
                dve.wait_ge(xT_hi_ready, t + 1)
                dve.tensor_tensor(xT_lo[:].rearrange("p k t -> p (k t)"), banks[5][:],
                                  xT_hi[:].rearrange("p k t -> p (k t)").bitcast(F32), ALU.subtract).then_inc(xT_lo_ready, 1)

            def take_h(t, r):
                dve.wait_ge(up_done, t + 1)
                dve.wait_ge(b1_loaded[r], 16 * (t // 2) + 16)
                for a in range(2):
                    last = dve.tensor_tensor(h_sb[:, a * 512:(a + 1) * 512], banks[a][:],
                                             b1_row[:, r, a * 512:(a + 1) * 512], ALU.add)
                last.then_inc(h_ready, 1)

            def take_hT(t):
                dve.wait_ge(hT_hi_ready, t + 1)
                for a in range(2):
                    last = dve.scalar_tensor_tensor(hT_lo[:, 4 * a:4 * a + 4, :].rearrange("p k t -> p (k t)"),
                                                    banks[2 + a][:], 0.0,
                                                    hT_hi[:, 4 * a:4 * a + 4, :].rearrange("p k t -> p (k t)").bitcast(F32),
                                                    ALU.max, ALU.subtract)
                last.then_inc(hT_lo_ready, 1)

            def take_y(t, r, first=False):
                dve.wait_ge(down_done, t + 1)
                dve.wait_ge(b2_loaded[r], 16 * (t // 2) + 16)
                if not first:
                    dve.wait_ge(y_stored[r], 16 * (t // 2))
                dve.tensor_tensor(y_sb[:, r, :], banks[4][:], b2_row[:, r, :], ALU.add).then_inc(y_added, 1)

            def tile(t, r, first=False, last=False, begin=False, spare=False):
                load = dve.value_load(tile_loads[0:1, bass.ds(t, 1)], min_val=0, max_val=1)
                if spare:
                    used = dve.value_load(tile_used[0:1, bass.ds(t, 1)], min_val=0, max_val=1)
                e = dve.value_load(tile_next[0:1, bass.ds(t, 1)], min_val=0, max_val=E - 1)

                def work(split_next):
                    split_next(0)
                    split_next(1)
                    take_h(t, r)
                    if not last:
                        take_x(t + 1)
                    if not begin:
                        take_y(t - 1, 1 - r, first)
                    take_hT(t)
                    split_next(2)
                    split_next(3)

                def pass_tile():
                    dve.wait_ge(up_done, t + 1)
                    dve.wait_ge(b1_loaded[r], 16 * (t // 2) + 16)
                    pass_on(dve, h_ready, t)
                    if not last:
                        dve.wait_ge(xT_hi_ready, t + 2)
                        pass_on(dve, xT_lo_ready, t + 1)
                    take_y(t - 1, 1 - r, first)
                    dve.wait_ge(hT_hi_ready, t + 1)
                    pass_on(dve, hT_lo_ready, t)

                def split(q):
                    if not begin:
                        dve.wait_ge((up_done, up_done, down_half, down_done)[q], t)
                    split_lo(base, q, t + 1)

                dve.wait_ge(lo_split, WQ * t + WQ)
                dve.nop(nofuse=True)
                with dve.If(load == 1):
                    base = dve.snap((e % 2) * WCOLS)
                    work(split)
                with dve.Else():
                    dve.sem_inc(lo_split, WQ)
                    if spare:
                        with dve.If(used == 1):
                            work(lambda q: None)
                        with dve.Else():
                            pass_tile()
                    else:
                        work(lambda q: None)
                dve.nop(nofuse=True)

            take_x(0)
            tile(0, 0, begin=True)

            tile(1, 1, first=True)
            tile(2, 0, first=True)
            with dve.Fori(1, FULL_TILES // 2 - 1) as j:
                for r in (1, 0):
                    tile(2 * j + 2 - r, r)
            with dve.Fori(FULL_TILES // 2 - 1, (SLOT_TILES - 3) // 2) as j:
                for r in (1, 0):
                    tile(2 * j + 2 - r, r, spare=True)
            tile(SLOT_TILES - 2, 1, spare=True)
            tile(SLOT_TILES - 1, 0, last=True, spare=True)
            take_y(SLOT_TILES - 1, 0)

        @block.tensor
        def _(pe):
            pe.wait_ge(consts2, 6)
            pe.wait_ge(lens_scanned, 2)
            pe.matmul(banks[0][:, 0:B], before[:], within[:, :, NJ - 1], start=True, stop=True).then_inc(prefix_done, 1)
            pe.wait_ge(w_in_loaded, 16)
            for k in range(DC):
                for j in range(DC):
                    last = pe.transpose(banks[(1, 2, 5, 6)[k]][:, j * P:(j + 1) * P], w_in_sb[:, j, k * P:(k + 1) * P], ident[:])
                last.then_inc(w_in_turned, 1)

            def turn_h(n):
                pe.wait_ge(normed, n + 1)
                if n >= 2:
                    pe.wait_ge(hnT_lo_ready, n - 1)
                for k in range(DC):
                    last = pe.transpose(banks[3 + n % 2][:, k * P:(k + 1) * P], hn[:, n % 2, k * P:(k + 1) * P], ident[:])
                last.then_inc(h_turned, 1)

            def embed(n):
                pe.wait_ge(hnT_lo_ready, n + 1)
                if n >= 4:
                    pe.wait_ge(x1_ready, n - 3)
                for k in range(DC):
                    for part, (h, w) in enumerate(((hnT_hi, w_inT_hi[:, k, :]), (hnT_hi, w_inT_lo[k][:]),
                                                   (hnT_lo, w_inT_hi[:, k, :]))):
                        last = pe.matmul(banks[(5, 6, 7, 0)[n % 4]][:], h[:, n % 2, k, :], w,
                                         start=(k == 0 and part == 0), stop=False)
                last.then_inc(h_used, 1)

            def depool(n):
                b, li = divmod(ORDER[n], LT)
                for k in range(li + 1):
                    if li == k:
                        pe.wait_ge(patches_ready, n + 1)
                        pe.wait_ge(decay_ready, n + 1)
                    last = pe.matmul(banks[(5, 6, 7, 0)[n % 4]][:], decay[:, b * LT + k, li * P:(li + 1) * P],
                                     patches[:, b * LT + k, :], start=False, stop=(k == li))
                last.then_inc(embedded, 1)

            def turn_xn(m):
                pe.wait_ge(xn_ready, m + 1)
                if m >= 2:
                    pe.wait_ge(xnT_lo_ready, m - 1)
                else:
                    pe.wait_ge(hnT_lo_ready, NT - 1 + m)
                for k in range(DC):
                    last = pe.transpose(banks[3 + m % 2][:, k * P:(k + 1) * P], xn[:, m % 2, k * P:(k + 1) * P], ident[:])
                last.then_inc(xn_turned, 1)

            turn_h(0)
            turn_h(1)
            pe.wait_ge(w_in_ready, DC)
            for b in range(B):
                embed(b)
                pe.wait_ge(onehots, b + 2)
                for j in range(NJ):
                    n = b * NJ + j
                    last = pe.matmul(banks[0][0:16, 64 + b * 32:96 + b * 32], oh_hi[:, n, :], oh_lo[:, n, :],
                                     start=(j == 0), stop=(j == NJ - 1))
            last.then_inc(hits_done, 1)
            turn_h(2)
            turn_h(3)
            embed(2)
            for b in range(B):
                pe.wait_ge(blocks_ready, b + 1)
                pe.matmul(banks[1 + b][:], ones_bf[0:16, :], blocks[:, b].rearrange("p a c -> p (a c)"),
                          start=True, stop=True).then_inc(rows_counted, 1)
            turn_h(4)
            embed(3)
            turn_h(5)
            for n in range(NT):
                depool(n)
                if n >= 1 and n + 3 < NT:
                    embed(n + 3)
                    if n + 5 < NT:
                        turn_h(n + 5)
                if n >= 3:
                    turn_xn(n - 3)
            for m in range(NT - 3, B * AT):
                turn_xn(m)
            pe.wait_ge(wq_lo_ready, DC)
            pe.wait_ge(xnT_lo_ready, B * AT)
            pe.wait_ge(x1_ready, NT)
            part_pairs = ((wq_hi, xnT_hi), (wq_hi, xnT_lo), (wq_lo, xnT_hi))
            for u in range(B * 2 * DC):
                b, c = divmod(u, 2 * DC)
                if u >= 3:
                    pe.wait_ge(qk_lo_ready, u - 2)
                for k in range(DC):
                    for n, (w, xt) in enumerate(part_pairs):
                        last = pe.matmul(banks[u % 3][:, 0:AROWS], w[:, k, c * P:(c + 1) * P],
                                         xt[:, k, b * AROWS:(b + 1) * AROWS], start=(k == 0 and n == 0),
                                         stop=(k == DC - 1 and n == 2))
                last.then_inc(qk_summed, 1)

            def project_v(m):
                if m >= 2:
                    pe.wait_ge(v_ready, m - 1)
                for k in range(DC):
                    for n, (w, xt) in enumerate(part_pairs):
                        last = pe.matmul(banks[5 + m % 2][:], xt[:, k, m * P:(m + 1) * P], w[:, k, 2 * D:3 * D],
                                         start=(k == 0 and n == 0), stop=(k == DC - 1 and n == 2))
                last.then_inc(v_summed, 1)

            def scores(n, s, j, first=False):
                if s % 2 == 0:
                    pe.wait_ge(parts_loaded[s // 2 % 4], 32 * j + 32)
                if not first:
                    pe.wait_ge(exp_done, n - 3)
                for q in range(2):
                    last = pe.matmul(banks[s % 4][:, q * WIN:(q + 1) * WIN], q_parts[:, s % 8, q * P:(q + 1) * P],
                                     k_parts[:, s % 8, :], start=True, stop=True)
                last.then_inc(scores_ready, 1)

            def turn_probs(n, s, first=False):
                pe.wait_ge(normalised, n + 1)
                if not first:
                    pe.wait_ge(probsT_ready, n - 1)
                for a in range(2):
                    for q in range(2):
                        last = pe.transpose(banks[4 + s % 2][:, (2 * a + q) * P:(2 * a + q + 1) * P],
                                            probs_n[:, s % 2, q, a * P:(a + 1) * P], ident[:])
                last.then_inc(turned, 1)

            def weigh(n, s, it, first=False):
                r, h = s // 4 % 2, s % 4
                pe.wait_ge(probsT_ready, n + 1)
                if h == 0:
                    pe.wait_ge(v_staged, it + 1)
                    if not first:
                        pe.wait_ge(oT_lo_ready, it - 1)
                for a in range(2):
                    last = pe.matmul(banks[6 + r][h * HD:(h + 1) * HD, 0:WIN], v_heads[:, r, a, h * HD:(h + 1) * HD],
                                     probsT[:, s % 2, a, :], start=(a == 0), stop=(a == 1))
                last.then_inc(pv_done, 1)

            def heads(j, first=False, last=False):
                for r in range(8):
                    if not (last and r + 3 >= 8):
                        scores(8 * j + r + 3, r + 3, j + (r + 3) // 8, first and r + 3 < 4)
                    turn_probs(8 * j + r, r, first and r < 2)
                    if not (first and r == 0):
                        weigh(8 * j + r - 1, (r - 1) % 8, 2 * j + (r - 1) // 4, first)

            for m in range(4):
                project_v(m)
            pe.wait_ge(qk_lo_ready, B * 2 * DC)
            scores(0, 0, 0, True)
            scores(1, 1, 0, True)
            project_v(4)
            scores(2, 2, 0, True)
            project_v(5)
            pe.wait_ge(v_ready, B * AT)
            heads(0, first=True)
            with pe.Fori(1, 7) as j:
                heads(j)
            heads(7, last=True)
            weigh(63, 7, 15)
            def turn_x3(i):
                pe.wait_ge(x3_ready, i + 1)
                if i >= 2:
                    pe.wait_ge(x3T_ready, i - 1)
                for k in range(DC):
                    last = pe.transpose(banks[3 + i % 2][:, k * P:(k + 1) * P], x3[:, i % 2, k * P:(k + 1) * P], ident[:])
                last.then_inc(x3_turned, 1)

            pe.wait_ge(gate_loaded, 16)

            def gate(i):
                pe.wait_ge(x3T_ready, i + 1)
                for k in range(DC):
                    last = pe.matmul(banks[5][:, i * E:(i + 1) * E], x3T[:, i % 2, k, :], w_gate_sb[:, k, :],
                                     start=(k == 0), stop=(k == DC - 1))
                last.then_inc(gated, 1)

            pe.wait_ge(w_out_lo_ready, DC)
            for i in range(NT):
                w, q = divmod(i, 2)
                pe.wait_ge(oT_lo_ready, 4 * w + 4)
                if i >= 3:
                    pe.wait_ge(x2_ready, i - 2)
                for g in range(4):
                    for n, (o, wo) in enumerate(((oT_hi, w_out_hi[g][:]), (oT_hi, w_out_lo[:, g, :]),
                                                 (oT_lo, w_out_hi[g][:]))):
                        last = pe.matmul(banks[i % 3][:], o[:, 4 * w + g, q * P:(q + 1) * P], wo,
                                         start=(g == 0 and n == 0), stop=(g == 3 and n == 2))
                last.then_inc(projected, 1)
                if i >= 2:
                    turn_x3(i - 2)
                if i >= 3:
                    gate(i - 3)
            for i in range(NT, NT + 3):
                if i < NT + 2:
                    turn_x3(i - 2)
                gate(i - 3)
            pe.wait_ge(ranks_asked, 1)
            pe.matmul(banks[7][:, 0:(NT + 1) * E], ones_bf[:], earlier.rearrange("p i e -> p (i e)"), start=True,
                      stop=False)
            pe.matmul(banks[7][:, 0:NT * E], before_bf[:], chosen.rearrange("p i e -> p (i e)"), start=False,
                      stop=True).then_inc(ranked, 1)
            pe.wait_ge(casts_ready, 1)
            for n in range(2 * NT):
                last = pe.matmul(banks[6][:, 0:3 * TC], lo_hot[:, n, :], cast_token[:, n].rearrange("p a t -> p (a t)"),
                                 start=(n == 0), stop=(n == 2 * NT - 1))
            last.then_inc(cast_done, 1)

            def cast_scores():
                pe.wait_ge(scores_asked, 1)
                for n in range(2 * NT):
                    last = pe.matmul(banks[7][:, 0:3 * TC], lo_hot[:, n, :], cast_score[:, n].rearrange("p a t -> p (a t)"),
                                     start=(n == 0), stop=(n == 2 * NT - 1))
                last.then_inc(scores_cast, 1)

            def when_used(used, done, n, products, skipped):
                pe.wait_ge(done, n)
                pe.nop(nofuse=True)
                with pe.If(used == 1):
                    products()
                with pe.Else():
                    for count in skipped:
                        pe.sem_inc(count, 1)
                pe.nop(nofuse=True)

            def turn_x(t, r, first=False, used=None):
                pe.wait_ge(gathered[r], 16 * (t // 2) + 16)
                if not first:
                    pe.wait_ge(xT_lo_ready, t)

                def turns():
                    for k in range(DC):
                        last = pe.transpose(banks[5][:, k * P:(k + 1) * P], x_gath[:, r, k * P:(k + 1) * P], ident[:])
                    last.then_inc(xg_turned, 1)

                if used is None:
                    turns()
                else:
                    when_used(used, xg_turned, t, turns, (xg_turned,))

            def is_used(t):
                return pe.value_load(tile_used[0:1, bass.ds(t, 1)], min_val=0, max_val=1)

            def up(t, first=False, used=None):
                s = 0 if first else half_of(t)
                pe.wait_ge(xT_lo_ready, t + 1)
                if not first:
                    pe.wait_ge(h_ready, t)

                def products():
                    for k in range(DC):
                        if k % 2 == 0:
                            pe.wait_ge(hi_split, WQ * t + 1 + k // 2)
                            pe.wait_ge(lo_split, WQ * t + 1 + k // 2)
                        for x_part, w_parts in ((xT_hi, (w_hi, w_lo)), (xT_lo, (w_hi,))):
                            for a in range(2):
                                for w in w_parts:
                                    last = pe.matmul(banks[a][:], x_part[:, k, :],
                                                     w[:, bass.ds(s + k * H + a * 512, 512)],
                                                     start=(k == 0 and x_part is xT_hi and w is w_hi),
                                                     stop=(k == DC - 1 and x_part is xT_lo))
                    last.then_inc(up_done, 1)

                if used is None:
                    products()
                else:
                    when_used(used, up_done, t, products, (up_done,))

            def down(t, first=False, spare=False):
                used = is_used(t) if spare else None
                s = half_of(t)
                pe.wait_ge(hT_lo_ready, t + 1)
                if not first:
                    pe.wait_ge(y_added, t)

                def products():
                    for k in range(HC):
                        if k % 4 == 0:
                            pe.wait_ge(hi_split, WQ * t + 3 + k // 4)
                            pe.wait_ge(lo_split, WQ * t + 3 + k // 4)
                        for h_part, w_parts in ((hT_hi, (w_hi, w_lo)), (hT_lo, (w_hi,))):
                            for w in w_parts:
                                last = pe.matmul(banks[4][:], h_part[:, k, :], w[:, bass.ds(s + DC * H + k * D, D)],
                                                 start=(k == 0 and h_part is hT_hi and w is w_hi),
                                                 stop=(k == HC - 1 and h_part is hT_lo))
                        if k == HC // 2 - 1:
                            last.then_inc(down_half, 1)
                    last.then_inc(down_done, 1)

                if spare:
                    when_used(used, down_done, t, products, (down_half, down_done))
                else:
                    products()

            def turn_hidden(t, first=False, used=None):
                pe.wait_ge(h_ready, t + 1)
                if not first:
                    pe.wait_ge(hT_lo_ready, t)

                def turns():
                    for k in range(HC):
                        last = pe.transpose(banks[2 + k // 4][:, k % 4 * P:(k % 4 + 1) * P], h_sb[:, k * P:(k + 1) * P],
                                            ident[:])
                    last.then_inc(h_turned2, 1)

                if used is None:
                    turns()
                else:
                    when_used(used, h_turned2, t, turns, (h_turned2,))

            def half_of(t):
                e = pe.value_load(tile_expert[0:1, bass.ds(t, 1)], min_val=0, max_val=E - 1)
                return pe.snap((e % 2) * WCOLS)

            def tile(t, r, first=False, last=False, spare=False):
                used = is_used(t) if spare else None
                up(t, used=used)
                if not last:
                    turn_x(t + 1, 1 - r, used=used)
                down(t - 1, first, spare)
                turn_hidden(t, used=used)

            pe.wait_ge(tables_ready, 1)
            cast_scores()
            turn_x(0, 0, True)
            up(0, True)
            turn_x(1, 1)
            turn_hidden(0, True)
            tile(1, 1, first=True)
            tile(2, 0)
            with pe.Fori(1, FULL_TILES // 2 - 1) as j:
                for r in (1, 0):
                    tile(2 * j + 2 - r, r)
            with pe.Fori(FULL_TILES // 2 - 1, (SLOT_TILES - 3) // 2) as j:
                for r in (1, 0):
                    tile(2 * j + 2 - r, r, spare=True)
            tile(SLOT_TILES - 2, 1, spare=True)
            tile(SLOT_TILES - 1, 0, last=True, spare=True)
            down(SLOT_TILES - 1, spare=True)

    return nc


_INS = ['x', 'ctx_2048', 'mask_BxS2_if0', 'L0_xattn_W_in', 'L0_xattn_b_in', 'L0_xattn_g_res', 'L0_xattn_g_init',
        'L0_attn_w_qkv', 'L0_attn_b_qkv', 'L0_attn_w_out', 'L0_attn_b_out', 'L0_ffn_Wg', 'L0_ffn_W1', 'L0_ffn_b1',
        'L0_ffn_W2', 'L0_ffn_b2']


def kernel(**inputs):
    import numpy as _np
    import concourse.bacc as _bacc
    from concourse import mybir as _mybir
    from concourse.bass_utils import run_bass_kernel_spmd as _run

    nc = _bacc.Bacc("TRN2", target_bir_lowering=False, num_devices=1)
    arrays, args = {}, []
    for name in _INS:
        a = _np.ascontiguousarray(inputs[name])
        arrays[f"in_{name}_dram"] = a
        args.append(nc.dram_tensor(f"in_{name}_dram", a.shape, _mybir.dt.from_np(a.dtype), kind="ExternalInput").ap())
    args.append(nc.dram_tensor("out_0_dram", (B, L, D), _mybir.dt.float32, kind="ExternalOutput").ap())
    perceiver_layer(nc, *args)
    r = _run(nc, [arrays], core_ids=[0])
    return r.results[0]["out_0_dram"]
```
